# Optimizing a Trainium2 kernel written in Bass

```python
import numpy as np
import jax
import jax.numpy as jnp

def _softmax(x, axis=-1):
    return jax.nn.softmax(x, axis=axis)

def _gelu(x):
    return jax.nn.gelu(x, approximate=True)

def _silu(x):
    return jax.nn.silu(x)

def _sigmoid(x):
    return jax.nn.sigmoid(x)

def _layernorm(x, axis=-1, eps=1e-05):
    m = jnp.mean(x, axis=axis, keepdims=True)
    v = jnp.var(x, axis=axis, keepdims=True)
    return (x - m) / jnp.sqrt(v + eps)

def _scatter_add(tgt, idx, src, axis=0):
    return tgt.at[idx].add(src)

def _segment_sum(src, seg, n):
    return jax.ops.segment_sum(src, seg, n)
kernel_name = 'mk_sandwich_d1_jaxref_r8_26acef'

def setup_inputs(seed: int=0):
    np.random.seed(seed)
    _w = jnp.asarray

    def _L0_attn_setup():
        import jax, jax.numpy as jnp
        import numpy as np
        B, S, E, H, P = (2, 256, 128, 16, 256)
        HD = E // H
        key = jax.random.key(seed)
        ks = jax.random.split(key, 10)
        std = E ** (-0.5)
        x = jax.random.normal(ks[0], (B, S, E), jnp.float32)
        Wq = jax.random.normal(ks[1], (E, E), jnp.float32) * std
        Wk = jax.random.normal(ks[2], (E, E), jnp.float32) * std
        Wv = jax.random.normal(ks[3], (E, E), jnp.float32) * std
        Wo = jax.random.normal(ks[4], (E, E), jnp.float32) * std
        rel_key = jax.random.normal(ks[5], (P, HD), jnp.float32) * 0.02
        z = jnp.zeros((E,), jnp.float32)
        return {'x': x, 'Wq': Wq, 'bq': z, 'Wk': Wk, 'bk': z, 'Wv': Wv, 'bv': z, 'Wo': Wo, 'bo': z, 'rel_key': rel_key}
    _L0_attn_in = _L0_attn_setup()

    def _L0_ffn_setup():
        import jax, jax.numpy as jnp
        import numpy as np
        D_IN, D_HID = (128, 512)

        def _ternary(key, shape):
            return jax.random.randint(key, shape, -1, 2).astype(jnp.float32)

        def _tlin(x, w, s):
            return jnp.einsum('bsi,oi->bso', x, w) * s
        key = jax.random.key(seed)
        ks = jax.random.split(key, 12)
        inv = lambda fan: 1.0 / np.sqrt(fan).astype(np.float32)
        return {'x': jax.random.normal(ks[0], (4, 256, D_IN), dtype=jnp.float32), 'w1_w': _ternary(ks[1], (D_HID, D_IN)), 'w1_s': jax.random.uniform(ks[2], (D_HID,), dtype=jnp.float32) * inv(D_IN), 'w2_w': _ternary(ks[3], (D_HID, D_IN)), 'w2_s': jax.random.uniform(ks[4], (D_HID,), dtype=jnp.float32) * inv(D_IN), 'h1_w': _ternary(ks[5], (D_HID, D_HID)), 'h1_s': jax.random.uniform(ks[6], (D_HID,), dtype=jnp.float32) * inv(D_HID), 'h2_w': _ternary(ks[7], (D_HID, D_HID)), 'h2_s': jax.random.uniform(ks[8], (D_HID,), dtype=jnp.float32) * inv(D_HID), 'w3_w': _ternary(ks[9], (D_IN, D_HID)), 'w3_s': jax.random.uniform(ks[10], (D_IN,), dtype=jnp.float32) * inv(D_HID)}
    _L0_ffn_in = _L0_ffn_setup()
    _d = {'L0_attn_x': _L0_attn_in['x'], 'L0_attn_Wq': _L0_attn_in['Wq'], 'L0_attn_bq': _L0_attn_in['bq'], 'L0_attn_Wk': _L0_attn_in['Wk'], 'L0_attn_bk': _L0_attn_in['bk'], 'L0_attn_Wv': _L0_attn_in['Wv'], 'L0_attn_bv': _L0_attn_in['bv'], 'L0_attn_Wo': _L0_attn_in['Wo'], 'L0_attn_bo': _L0_attn_in['bo'], 'L0_attn_rel_key': _L0_attn_in['rel_key'], 'L0_ffn_w1_w': _L0_ffn_in['w1_w'], 'L0_ffn_w1_s': _L0_ffn_in['w1_s'], 'L0_ffn_w2_w': _L0_ffn_in['w2_w'], 'L0_ffn_w2_s': _L0_ffn_in['w2_s'], 'L0_ffn_h1_w': _L0_ffn_in['h1_w'], 'L0_ffn_h1_s': _L0_ffn_in['h1_s'], 'L0_ffn_h2_w': _L0_ffn_in['h2_w'], 'L0_ffn_h2_s': _L0_ffn_in['h2_s'], 'L0_ffn_w3_w': _L0_ffn_in['w3_w'], 'L0_ffn_w3_s': _L0_ffn_in['w3_s']}
    _x0 = _d['L0_attn_x']
    _d['L0_attn_x'] = jax.random.normal(jax.random.fold_in(jax.random.key(seed), 1), (4, 1024, 128), dtype=_x0.dtype)
    del _x0
    return _d

def reference(L0_attn_x, L0_attn_Wq, L0_attn_bq, L0_attn_Wk, L0_attn_bk, L0_attn_Wv, L0_attn_bv, L0_attn_Wo, L0_attn_bo, L0_attn_rel_key, L0_ffn_w1_w, L0_ffn_w1_s, L0_ffn_w2_w, L0_ffn_w2_s, L0_ffn_h1_w, L0_ffn_h1_s, L0_ffn_h2_w, L0_ffn_h2_s, L0_ffn_w3_w, L0_ffn_w3_s):

    def _L0_attn_ref(x, Wq, bq, Wk, bk, Wv, bv, Wo, bo, rel_key):
        import jax, jax.numpy as jnp
        import numpy as np
        B, S, E, H, P = (2, 256, 128, 16, 256)
        HD = E // H
        b, s, e = x.shape
        p, hd = rel_key.shape
        h = e // hd
        scale = hd ** (-0.5)

        def split_heads(t):
            return t.reshape(b, s, h, hd).transpose(0, 2, 1, 3)
        q = split_heads(x @ Wq + bq)
        k = split_heads(x @ Wk + bk)
        v = split_heads(x @ Wv + bv)
        scores = jnp.einsum('bhid,bhjd->bhij', q, k)
        rel = jnp.einsum('bhid,pd->bhip', q, rel_key)
        i = jnp.arange(s)[:, None]
        j = jnp.arange(s)[None, :]
        rel_idx = jnp.clip(j - i + p - 1, 0, p - 1)
        bias = jnp.take_along_axis(rel, jnp.broadcast_to(rel_idx[None, None], (b, h, s, s)), axis=3)
        causal = j <= i
        logits = jnp.where(causal[None, None], (scores + bias) * scale, -jnp.inf)
        attn = jax.nn.softmax(logits, axis=-1)
        out = jnp.einsum('bhij,bhjd->bhid', attn, v)
        out = out.transpose(0, 2, 1, 3).reshape(b, s, e)
        return out @ Wo + bo

    def _L0_ffn_ref(x, w1_w, w1_s, w2_w, w2_s, h1_w, h1_s, h2_w, h2_s, w3_w, w3_s):
        import jax, jax.numpy as jnp
        import numpy as np
        D_IN, D_HID = (128, 512)

        def _ternary(key, shape):
            return jax.random.randint(key, shape, -1, 2).astype(jnp.float32)

        def _tlin(x, w, s):
            return jnp.einsum('bsi,oi->bso', x, w) * s
        h = jax.nn.silu(_tlin(x, w1_w, w1_s)) * _tlin(x, w2_w, w2_s)
        h = jax.nn.gelu(_tlin(h, h1_w, h1_s), approximate=False)
        h = jax.nn.gelu(_tlin(h, h2_w, h2_s), approximate=False)
        return _tlin(h, w3_w, w3_s)
    x = L0_attn_x
    x = x + _layernorm(_L0_attn_ref(_layernorm(x, axis=-1), L0_attn_Wq, L0_attn_bq, L0_attn_Wk, L0_attn_bk, L0_attn_Wv, L0_attn_bv, L0_attn_Wo, L0_attn_bo, L0_attn_rel_key), axis=-1)
    x = x + _layernorm(_L0_ffn_ref(_layernorm(x, axis=-1), L0_ffn_w1_w, L0_ffn_w1_s, L0_ffn_w2_w, L0_ffn_w2_s, L0_ffn_h1_w, L0_ffn_h1_s, L0_ffn_h2_w, L0_ffn_h2_s, L0_ffn_w3_w, L0_ffn_w3_s), axis=-1)
    return x

_drawn_inputs = setup_inputs


def setup_inputs(seed=0):
    import zlib

    import numpy as np

    out = dict(_drawn_inputs(seed))
    spreads = {'L0_attn_bq': (0.0, 0.1),
     'L0_attn_bk': (0.0, 0.8),
     'L0_attn_bv': (0.0, 0.1),
     'L0_attn_bo': (0.0, 0.1)}
    factors = {'L0_attn_rel_key': 7.261}
    for name, (base, spread) in spreads.items():
        noise = np.random.default_rng([zlib.crc32(name.encode()), seed]).standard_normal(out[name].shape)
        drawn = base * np.exp(spread * noise) if base else spread * noise
        out[name] = jnp.asarray(drawn.astype(out[name].dtype))
    for name, factor in factors.items():
        out[name] = (out[name] * factor).astype(out[name].dtype)
    return out
```

```python
import concourse.bass as bass
from concourse import mybir
from contextlib import ExitStack

F32 = mybir.dt.float32
F32R = mybir.dt.float32r
BF16 = mybir.dt.bfloat16
ALU = mybir.AluOpType
ACT = mybir.ActivationFunctionType
AX = mybir.AxisListType

B, S, E = 4, 1024, 128
HD, H = 8, 16
P = 256
HID = 512
TOK = B * S
BLK = 128
NB = S // BLK
HG = 4
UNITS = B * H // HG
PARTS = 3
ROWS = PARTS * PARTS * HD
KROWS = 96
EPS = 1e-5
SCALE = float(HD) ** -0.5
MASKED = -1.0e30
GROUPS = [(0,), (1, 7), (2, 6), (3, 5), (4,)]
NG = len(GROUPS)
STEPS = NG * HG
RCH = 16
CHUNKS = 2 * BLK // RCH
HALF = CHUNKS // 2
QB = HG * NB
BG = H // HG
UNIT_QK = PARTS * HD * HG * S
KINDS = 3
BIASCOLS = QB * KINDS * BLK
FC = 512
NFC = TOK // FC
HC = HID // 128


def is_first(u):
    return isinstance(u, int) and u == 0


def ap(handle, offset, dims):
    return bass.AP(handle, offset, dims)


def wait_alone(eng, sem, value, passed):
    eng.wait_ge(sem, value)
    eng.sem_inc(passed, 1)


def turns(eng, n, body):
    body(0, True)
    with eng.Fori(1, n) as i:
        body(i, False)


def attention_ffn(nc, x, Wq, bq, Wk, bk, Wv, bv, Wo, bo, rel, w1, s1, w2, s2, h1, sh1, h2, sh2, w3, s3, out):
    with ExitStack() as ctx:
        ctx.enter_context(nc.allow_non_contiguous_dma(reason="small parameters"))
        build(nc, ctx, x, Wq, bq, Wk, bk, Wv, bv, Wo, bo, rel, w1, s1, w2, s2, h1, sh1, h2, sh2, w3, s3, out)


def build(nc, ctx, x, Wq, bq, Wk, bk, Wv, bv, Wo, bo, rel, w1, s1, w2, s2, h1, sh1, h2, sh2, w3, s3, out):
    def sb(name, shape, dt=F32, where=ctx):
        return where.enter_context(nc.sbuf_tensor(name, shape, dt))

    def ps(name, shape, where=ctx):
        return where.enter_context(nc.psum_tensor(name, shape, F32))

    def sem(name):
        return ctx.enter_context(nc.semaphore(name))

    q_dram = nc.dram_tensor("q_dram", [UNITS, PARTS, HD, HG, S], BF16, kind="Internal")
    k_dram = nc.dram_tensor("k_dram", [UNITS, HD, PARTS, HG, S], BF16, kind="Internal")
    m_dram = nc.dram_tensor("m_dram", [UNITS, PARTS, HG, S], BF16, kind="Internal")
    v_dram = nc.dram_tensor("v_dram", [B, BG, 128, NB, HG, 32], F32, kind="Internal")
    g_dram = nc.dram_tensor("g_dram", [HD, PARTS, P], BF16, kind="Internal")
    gx_dram = nc.dram_tensor("gx_dram", [HD, 2], F32, kind="Internal")

    ident = sb("ident", [128, 128])
    rel_w = sb("rel_w", [KROWS, P + BLK], BF16)
    o_all = sb("o_all", [128, UNITS * NB * 32])

    one = ExitStack()
    wq_sb, wk_sb, wv_sb = (sb(n, [128, 128], F32, one) for n in ("wq_sb", "wk_sb", "wv_sb"))
    bq_c, bk_c, r0_c, kb_c = (sb(n, [128, 1], F32, one) for n in ("bq_c", "bk_c", "r0_c", "kb_c"))
    bv_b = sb("bv_b", [128, NB, 128], F32, one)
    rel_t = sb("rel_t", [HD, P], F32, one)
    rel_s = sb("rel_s", [HD, P], F32, one)
    rel_r = sb("rel_r", [HD, P], F32, one)
    rel_p = sb("rel_p", [HD, PARTS, P], BF16, one)
    gx = sb("gx", [HD, 2], F32, one)
    g_ext = sb("g_ext", [128, 2], F32, one)
    hmask = sb("hmask", [128, H], F32, one)
    xin = sb("xin", [128, NB, 128], F32, one)
    xh = sb("xh", [128, NB, 128], F32, one)
    stats = sb("stats", [128, NB, 6], F32, one)
    mv = sb("mv", [128, NB, 2], F32, one)
    var_e, std, rstd, nmr = (sb(n, [128, NB], F32, one) for n in ("var_e", "std", "rstd", "nmr"))
    xT = sb("xT", [128, S], F32, one)
    qf, kf, q_rest, k_rest = (sb(n, [128, S], F32, one) for n in ("qf", "kf", "q_rest", "k_rest"))
    q_parts, k_parts = (sb(n, [128, PARTS, S], BF16, one) for n in ("q_parts", "k_parts"))
    q_pos, q_neg = (sb(n, [128, S], F32, one) for n in ("q_pos", "q_neg"))
    k_ext = sb("k_ext", [128, 2], F32, one)
    k_sel = sb("k_sel", [128, 2, H], F32, one)
    m_neg, m_rest = (sb(n, [H, S], F32, one) for n in ("m_neg", "m_rest"))
    m_parts = sb("m_parts", [H, PARTS, S], BF16, one)
    v_st = sb("v_st", [128, NB, H, 32], F32, one)
    pone = ExitStack()
    p_tr, p_q, p_k, p_v = (ps(n, [128, S], pone) for n in ("p_tr", "p_q", "p_k", "p_v"))

    s_alone = sem("s_alone")
    s_par = sem("s_par")
    s_gs = sem("s_gs")
    s_gst = sem("s_gst")
    s_gld = sem("s_gld")
    s_rw = sem("s_rw")
    s_pool = sem("s_pool")
    s_xin = sem("s_xin")
    s_ln = sem("s_ln")
    s_std = sem("s_std")
    s_xh = sem("s_xh")
    s_tr = sem("s_tr")
    s_xT = sem("s_xT")
    s_q, s_k, s_v = sem("s_q"), sem("s_k"), sem("s_v")
    s_qf, s_kf = sem("s_qf"), sem("s_kf")
    s_part = sem("s_part")
    s_hi = sem("s_hi")
    s_vst = sem("s_vst")
    s_qst, s_kst, s_mst, s_vout = sem("s_qst"), sem("s_kst"), sem("s_mst"), sem("s_vout")
    s_u = sem("s_u")
    LNS = 5
    PRT = 14

    with nc.Block() as block:
        @block.sync
        def _(sp):
            for dst, src in ((wq_sb[:, :], Wq), (wk_sb[:, :], Wk), (wv_sb[:, :], Wv),
                             (bq_c[:, :], bq.rearrange("(p a) -> p a", a=1)),
                             (bk_c[:, :], bk.rearrange("(p a) -> p a", a=1)),
                             (r0_c[:, :], ap(rel.tensor, 0, [[0, H], [1, HD], [1, 1]])),
                             (bv_b[:, :, :], ap(bv.tensor, 0, [[0, 128], [0, NB], [1, 128]])),
                             (rel_t[:, :], ap(rel.tensor, 0, [[1, HD], [HD, P]]))):
                sp.dma_start(dst, src).then_inc(s_par, 16)
            sp.dma_start(xin[:, :, :], ap(x.tensor, 0, [[E, 128], [128 * E, NB], [1, E]])).then_inc(s_xin, 16)
            sp.wait_ge(s_gs, 8)
            sp.dma_start(g_dram.ap(), rel_p[:, :, :]).then_inc(s_gst, 16)
            sp.dma_start(gx_dram.ap(), gx[:, :]).then_inc(s_gst, 16)
            sp.wait_ge(s_gst, 32)
            sp.dma_start(g_ext[:, :], ap(gx_dram, 0, [[0, H], [2, HD], [1, 2]])).then_inc(s_gld, 16)
            sp.wait_ge(s_pool, 1)
            sp.dma_start(rel_w[0:ROWS, 0:P], ap(g_dram, 0, [[0, PARTS], [P, HD * PARTS], [1, P]])).then_inc(s_rw, 16)
            sp.dma_start(rel_w[0:ROWS, P:P + BLK],
                         ap(g_dram, 0, [[0, PARTS], [P, HD * PARTS], [1, BLK]])).then_inc(s_rw, 16)
            sp.wait_ge(s_rw, 32)
            def batch(b, first):
                sp.wait_ge(s_xh, b + 1)
                nxt = (b + 1) % B
                sp.dma_start(xin[:, :, :], ap(x.tensor, nxt * (S * E), [[E, 128], [128 * E, NB], [1, E]])).then_inc(s_xin, 16)
                sp.wait_ge(s_vst, b + 1)
                for g in range(BG):
                    sp.dma_start(ap(v_dram, b * (128 * NB * H * 32) + g * (128 * NB * HG * 32),
                                    [[NB * HG * 32, 128], [HG * 32, NB], [1, HG * 32]]),
                                 v_st[:, :, g * HG:(g + 1) * HG, :].rearrange("p n h d -> p n (h d)")).then_inc(s_vout, 16)
                sp.wait_ge(s_part, b * PRT + 9)
                for g in range(BG):
                    rows = slice(g * HG * HD, (g + 1) * HG * HD)
                    for part in range(PARTS):
                        sp.dma_start(ap(q_dram, b * (BG * UNIT_QK) + g * UNIT_QK + part * (HD * HG * S),
                                        [[S, HG], [HG * S, HD], [1, S]]), q_parts[rows, part, :]).then_inc(s_qst, 16)
                        sp.dma_start(ap(k_dram, b * (BG * UNIT_QK) + g * UNIT_QK + part * (HG * S),
                                        [[S, HG], [PARTS * HG * S, HD], [1, S]]), k_parts[rows, part, :]).then_inc(s_kst, 16)
                sp.wait_ge(s_part, b * PRT + PRT)
                for g in range(BG):
                    sp.dma_start(ap(m_dram, b * (H * PARTS * S) + g * (HG * PARTS * S), [[S, HG], [HG * S, PARTS], [1, S]]),
                                 m_parts[g * HG:(g + 1) * HG, :, :]).then_inc(s_mst, 16)

            turns(sp, B, batch)
            sp.wait_ge(s_xin, 16 * (B + 1))
            sp.wait_ge(s_vout, 16 * (BG) * B)
            sp.wait_ge(s_qst, 16 * PARTS * BG * B)
            sp.wait_ge(s_kst, 16 * PARTS * BG * B)
            sp.wait_ge(s_mst, 16 * BG * B)

        @block.gpsimd
        def _(pool):
            def step(ins, n):
                ins.then_inc(s_pool, 1)
                pool.wait_ge(s_pool, n)

            step(nc.gpsimd.memset(rel_w[64:KROWS, :], 0.0), 1)
            step(nc.gpsimd.memset(ident[:, :], 0.0), 2)
            step(nc.gpsimd.memset(hmask[:, :], 1.0), 3)
            step(nc.gpsimd.memset(v_st[:, :, :, HD:32], 0.0), 4)
            step(nc.gpsimd.affine_select(out=ident[:, :], in_=ident[:, :], compare_op=ALU.not_equal, fill=1.0,
                                         base=0, pattern=[[-1, 128]], channel_multiplier=1), 5)
            step(nc.gpsimd.affine_select(out=hmask[:, :], in_=hmask[:, :], compare_op=ALU.is_ge, fill=0.0,
                                         base=0, pattern=[[-HD, H]], channel_multiplier=1), 6)
            step(nc.gpsimd.affine_select(out=hmask[:, :], in_=hmask[:, :], compare_op=ALU.is_ge, fill=0.0,
                                         base=HD - 1, pattern=[[HD, H]], channel_multiplier=-1), 7)
            step(nc.gpsimd.memset(v_st[:, :, :, HD:HD + 1], 1.0), 8)

        @block.vector
        def _(dve):
            dve.wait_ge(s_par, 8 * 16)
            nc.vector.tensor_tensor(kb_c[:, :], bk_c[:, :], r0_c[:, :], ALU.add).then_inc(s_gs, 1)
            nc.vector.tensor_scalar(rel_s[:, :], rel_t[:, :], rel_t[:, 0:1], None, ALU.subtract).then_inc(s_gs, 1)
            dve.wait_ge(s_gs, 2)
            nc.vector.tensor_reduce(out=gx[:, 0:1], in_=rel_s[:, :], op=ALU.max, axis=AX.X).then_inc(s_gs, 1)
            nc.vector.tensor_reduce(out=gx[:, 1:2], in_=rel_s[:, :], op=ALU.min, axis=AX.X).then_inc(s_gs, 1)
            nc.vector.tensor_copy(rel_p[:, 0, :], rel_s[:, :]).then_inc(s_gs, 1)
            dve.wait_ge(s_gs, 5)
            nc.vector.tensor_tensor(rel_r[:, :], rel_s[:, :], rel_p[:, 0, :], ALU.subtract).then_inc(s_gs, 1)
            dve.wait_ge(s_gs, 6)
            nc.vector.tensor_copy(rel_p[:, 1, :], rel_r[:, :]).then_inc(s_gs, 1)
            dve.wait_ge(s_gs, 7)
            nc.vector.tensor_tensor(rel_p[:, 2, :], rel_r[:, :], rel_p[:, 1, :], ALU.subtract).then_inc(s_gs, 1)
            dve.wait_ge(s_gld, 16)
            dve.wait_ge(s_pool, 8)
            def batch(b, first):
                def ln_wait(k):
                    dve.wait_ge(s_ln, b * LNS + k)

                def part_wait(k):
                    dve.wait_ge(s_part, b * PRT + k)

                dve.wait_ge(s_xin, b * 16 + 16)
                for t in range(NB):
                    last = nc.vector.bn_stats(stats[:, t, :], xin[:, t, :])
                last.then_inc(s_ln, 1)
                wait_alone(dve, s_ln, b * LNS + 1, s_alone)
                for t in range(NB):
                    last = nc.vector.bn_aggr(mv[:, t, :], stats[:, t, :])
                last.then_inc(s_ln, 1)
                ln_wait(2)
                nc.vector.tensor_scalar(var_e[:, :], mv[:, :, 1], EPS, None, ALU.add).then_inc(s_ln, 1)
                dve.wait_ge(s_std, b + 1)
                nc.vector.reciprocal(rstd[:, :], std[:, :]).then_inc(s_ln, 1)
                ln_wait(4)
                nc.vector.scalar_tensor_tensor(out=nmr[:, :], in0=mv[:, :, 0], scalar=-1.0, in1=rstd[:, :],
                                               op0=ALU.mult, op1=ALU.mult).then_inc(s_ln, 1)
                ln_wait(5)
                if not first:
                    dve.wait_ge(s_tr, b * 2)
                for t in range(NB):
                    last = nc.vector.tensor_scalar(xh[:, t, :], xin[:, t, :], rstd[:, t:t + 1], nmr[:, t:t + 1],
                                                   ALU.mult, ALU.add)
                last.then_inc(s_xh, 1)
                dve.wait_ge(s_kf, b + 1)
                nc.vector.tensor_reduce(out=k_ext[:, 0:1], in_=kf[:, :], op=ALU.max, axis=AX.X).then_inc(s_part, 1)
                nc.vector.tensor_reduce(out=k_ext[:, 1:2], in_=kf[:, :], op=ALU.min, axis=AX.X).then_inc(s_part, 1)
                dve.wait_ge(s_qf, b + 1)
                nc.vector.tensor_scalar(q_pos[:, :], qf[:, :], 0.0, None, ALU.max).then_inc(s_part, 1)
                nc.vector.tensor_scalar(q_neg[:, :], qf[:, :], 0.0, None, ALU.min).then_inc(s_part, 1)
                part_wait(2)
                nc.vector.tensor_tensor(k_ext[:, :], k_ext[:, :], g_ext[:, :], ALU.add).then_inc(s_part, 1)
                part_wait(5)
                for e in range(2):
                    last = nc.vector.tensor_scalar(k_sel[:, e, :], hmask[:, :], k_ext[:, e:e + 1], None, ALU.mult)
                last.then_inc(s_part, 1)
                dve.wait_ge(s_v, b + 1)
                if not first:
                    dve.wait_ge(s_vout, b * (16 * BG))
                nc.vector.tensor_tensor(v_st[:, :, :, 0:HD], p_v[:, :].rearrange("p (n h d) -> p n h d", n=NB, h=H),
                                        bv_b[:, :, :].rearrange("p n (h d) -> p n h d", h=H), ALU.add).then_inc(s_vst, 1)
                dve.wait_ge(s_hi, b * 6 + 2)
                nc.vector.tensor_tensor(q_rest[:, :], qf[:, :], q_parts[:, 0, :], ALU.subtract).then_inc(s_part, 1)
                nc.vector.tensor_tensor(k_rest[:, :], kf[:, :], k_parts[:, 0, :], ALU.subtract).then_inc(s_part, 1)
                dve.wait_ge(s_hi, b * 6 + 4)
                nc.vector.tensor_tensor(q_parts[:, 2, :], q_rest[:, :], q_parts[:, 1, :], ALU.subtract)
                nc.vector.tensor_tensor(k_parts[:, 2, :], k_rest[:, :], k_parts[:, 1, :], ALU.subtract).then_inc(s_part, 1)
                dve.wait_ge(s_hi, b * 6 + 6)
                if not first:
                    dve.wait_ge(s_mst, b * (16 * BG))
                nc.vector.tensor_copy(m_parts[:, 0, :], m_neg[:, :]).then_inc(s_part, 1)
                part_wait(10)
                nc.vector.tensor_tensor(m_rest[:, :], m_neg[:, :], m_parts[:, 0, :], ALU.subtract).then_inc(s_part, 1)
                part_wait(11)
                nc.vector.tensor_copy(m_parts[:, 1, :], m_rest[:, :]).then_inc(s_part, 1)
                part_wait(12)
                nc.vector.tensor_tensor(m_rest[:, :], m_rest[:, :], m_parts[:, 1, :], ALU.subtract).then_inc(s_part, 1)
                part_wait(13)
                nc.vector.tensor_copy(m_parts[:, 2, :], m_rest[:, :]).then_inc(s_part, 1)

            turns(dve, B, batch)

        @block.scalar
        def _(act):
            act.wait_ge(s_gs, 1)
            act.wait_ge(s_par, 8 * 16)
            def batch(b, first):
                act.wait_ge(s_ln, b * LNS + 3)
                nc.scalar.activation(std[:, :], var_e[:, :], ACT.Sqrt).then_inc(s_std, 1)
                if not first:
                    act.wait_ge(s_v, b)
                for j in range(2):
                    act.wait_ge(s_tr, b * 2 + j + 1)
                    nc.scalar.activation(xT[:, j * 512:(j + 1) * 512], p_tr[:, j * 512:(j + 1) * 512],
                                         ACT.Identity).then_inc(s_xT, 1)
                act.wait_ge(s_q, b + 1)
                if not first:
                    act.wait_ge(s_part, b * PRT)
                nc.scalar.activation(qf[:, :], p_q[:, :], ACT.Identity, bias=bq_c[:, 0:1]).then_inc(s_qf, 1)
                act.wait_ge(s_k, b + 1)
                nc.scalar.activation(kf[:, :], p_k[:, :], ACT.Identity, bias=kb_c[:, 0:1]).then_inc(s_kf, 1)
                if not first:
                    act.wait_ge(s_qst, b * (16 * PARTS * BG))
                if not first:
                    act.wait_ge(s_kst, b * (16 * PARTS * BG))
                act.wait_ge(s_qf, b + 1)
                nc.scalar.activation(q_parts[:, 0, :], qf[:, :], ACT.Identity).then_inc(s_hi, 1)
                act.wait_ge(s_kf, b + 1)
                nc.scalar.activation(k_parts[:, 0, :], kf[:, :], ACT.Identity).then_inc(s_hi, 1)
                act.wait_ge(s_part, b * PRT + 7)
                nc.scalar.activation(q_parts[:, 1, :], q_rest[:, :], ACT.Identity).then_inc(s_hi, 1)
                act.wait_ge(s_part, b * PRT + 8)
                nc.scalar.activation(k_parts[:, 1, :], k_rest[:, :], ACT.Identity).then_inc(s_hi, 1)
                for j in range(2):
                    act.wait_ge(s_u, b * 2 + j + 1)
                    last = nc.scalar.activation(m_neg[:, j * 512:(j + 1) * 512], p_tr[0:H, j * 512:(j + 1) * 512],
                                                ACT.Identity, scale=-1.0)
                    last.then_inc(s_hi, 1)

            turns(act, B, batch)

        @block.tensor
        def _(pe):
            pe.wait_ge(s_par, 8 * 16)
            pe.wait_ge(s_pool, 8)
            def batch(b, first):
                pe.wait_ge(s_xh, b + 1)
                if not first:
                    pe.wait_ge(s_hi, b * 6)
                for t in range(NB):
                    last = nc.tensor.transpose(p_tr[:, t * 128:(t + 1) * 128], xh[:, t, :], ident[:, :])
                    if t % 4 == 3:
                        last.then_inc(s_tr, 1)
                pe.wait_ge(s_xT, b * 2 + 2)
                if not first:
                    pe.wait_ge(s_qf, b)
                for j in range(2):
                    last = nc.tensor.matmul(p_q[:, j * 512:(j + 1) * 512], wq_sb[:, :], xT[:, j * 512:(j + 1) * 512],
                                            start=True, stop=True)
                last.then_inc(s_q, 1)
                if not first:
                    pe.wait_ge(s_kf, b)
                for j in range(2):
                    last = nc.tensor.matmul(p_k[:, j * 512:(j + 1) * 512], wk_sb[:, :], xT[:, j * 512:(j + 1) * 512],
                                            start=True, stop=True)
                last.then_inc(s_k, 1)
                if not first:
                    pe.wait_ge(s_vst, b)
                for t in range(NB):
                    last = nc.tensor.matmul(p_v[:, t * 128:(t + 1) * 128], xT[:, t * 128:(t + 1) * 128], wv_sb[:, :],
                                            start=True, stop=True)
                last.then_inc(s_v, 1)
                pe.wait_ge(s_part, b * PRT + 6)
                for j in range(2):
                    c = slice(j * 512, (j + 1) * 512)
                    nc.tensor.matmul(p_tr[0:H, c], k_sel[:, 0, :], q_pos[:, c], start=True, stop=False)
                    nc.tensor.matmul(p_tr[0:H, c], k_sel[:, 1, :], q_neg[:, c], start=False, stop=True).then_inc(s_u, 1)

            turns(pe, B, batch)
    pone.close()
    one.close()

    two = ExitStack()
    q_sb = [sb(f"q_sb{p}", [KROWS, HG * S], BF16, two) for p in range(2)]
    k_sb = [sb(f"k_sb{p}", [KROWS, HG * S], BF16, two) for p in range(2)]
    v_sb = [sb(f"v_sb{p}", [128, NB, HG * 32], F32, two) for p in range(2)]
    bias = [sb(f"bias{p}", [128, BIASCOLS + 512], F32, two) for p in range(2)]
    probs = [sb(f"probs{p}", [128, HG, 1024], F32, two) for p in range(2)]
    o_raw = sb("o_raw", [128, S], F32, two)
    o_rcp = sb("o_rcp", [128, QB], F32, two)
    ptwo = ExitStack()
    p_s = [ps(f"p_s{p}", [128, 1024], ptwo) for p in range(2)]
    p_o = ps("p_o", [128, S], ptwo)
    p_b = [ps(f"p_b{p}", [128, 512], ptwo) for p in range(2)]

    t_alone = sem("t_alone")
    t_ones = sem("t_ones")
    t_q = [sem(f"t_q{p}") for p in range(2)]
    t_k = [sem(f"t_k{p}") for p in range(2)]
    t_v = [sem(f"t_v{p}") for p in range(2)]
    t_s = sem("t_s")
    t_add = sem("t_add")
    t_exp = sem("t_exp")
    t_pv = sem("t_pv")
    t_bmm = sem("t_bmm")
    t_bev = sem("t_bev")
    t_beva = sem("t_beva")
    t_far = sem("t_far")
    t_near = sem("t_near")
    t_oraw = sem("t_oraw")
    t_otr = sem("t_otr")
    t_rcp = sem("t_rcp")
    t_o = sem("t_o")
    ACT_CH = set(range(HALF, HALF + 4))
    NDVE = CHUNKS - len(ACT_CH)

    def dve_count(c):
        return sum(1 for k in range(c + 1) if k not in ACT_CH)

    def act_count(c):
        return sum(1 for k in range(c + 1) if k in ACT_CH)

    def tile_cols(g):
        col, got = 0, []
        for j in GROUPS[g]:
            got.append((j, col, NB - j))
            col += (NB - j) * BLK
        return got

    def pv_pieces(g):
        got = []
        for j, col, _ in tile_cols(g):
            i = j * BLK
            while i < S:
                end = min(S, (i // 512 + 1) * 512)
                got.append((j, col + i - j * BLK, i, end))
                i = end
        return got

    def bias_q(buf, kind, c):
        r = (c % HALF) * RCH
        return bias[buf][:, 0:BIASCOLS].rearrange("p (q k r) -> p k q r", k=KINDS, r=BLK)[:, kind, :, r:r + RCH]

    with nc.Block() as block:
        @block.sync
        def _(sp):
            def load_qk(u, p):
                sp.dma_start(q_sb[p][0:ROWS, :], ap(q_dram, u * UNIT_QK,
                             [[HG * S, PARTS * HD], [0, PARTS], [1, HG * S]])).then_inc(t_q[p], 16)
                sp.dma_start(q_sb[p][ROWS:ROWS + PARTS, :], ap(m_dram, u * (HG * PARTS * S),
                             [[HG * S, PARTS], [1, HG * S]])).then_inc(t_q[p], 16)
                sp.dma_start(k_sb[p][0:ROWS, :], ap(k_dram, u * UNIT_QK,
                             [[0, PARTS], [HG * S, PARTS * HD], [1, HG * S]])).then_inc(t_k[p], 16)

            def load_v(u, p):
                sp.dma_start(v_sb[p][:, :, :], ap(v_dram, u * (128 * NB * HG * 32),
                             [[NB * HG * 32, 128], [HG * 32, NB], [1, HG * 32]])).then_inc(t_v[p], 16)

            sp.wait_ge(t_ones, 4)
            for p in range(2):
                load_qk(p, p)
                load_v(p, p)
            with sp.Fori(0, UNITS // 2 - 1) as i:
                for p in range(2):
                    sp.wait_ge(t_s, i * (2 * STEPS) + (p + 1) * STEPS)
                    load_qk(i * 2 + p + 2, p)
                    sp.wait_ge(t_pv, i * (2 * NG) + (p + 1) * NG)
                    load_v(i * 2 + p + 2, p)

        @block.gpsimd
        def _(pool):
            for p in range(2):
                nc.gpsimd.memset(q_sb[p][64:KROWS, :], 0.0).then_inc(t_ones, 1)
                pool.wait_ge(t_ones, 2 * p + 1)
                nc.gpsimd.memset(k_sb[p][64:KROWS, :], 1.0).then_inc(t_ones, 1)
                pool.wait_ge(t_ones, 2 * p + 2)

            def masks(n, buf, c):
                r = c * RCH
                wait_alone(pool, t_bev, n[0], t_alone)
                nc.gpsimd.affine_select(out=bias_q(buf, 2, c), in_=bias_q(buf, 0, c), compare_op=ALU.is_ge, fill=0.0,
                                        base=-1 - r, pattern=[[0, QB], [-1, RCH]], channel_multiplier=1).then_inc(t_far, 1)
                wait_alone(pool, t_far, n[1], t_alone)
                nc.gpsimd.affine_select(out=bias_q(buf, 0, c), in_=bias_q(buf, 0, c), compare_op=ALU.is_ge, fill=MASKED,
                                        base=r, pattern=[[0, QB], [1, RCH]], channel_multiplier=-1).then_inc(t_near, 1)

            for c in range(HALF):
                masks((dve_count(c), c + 1), 0, c)
            with pool.Fori(0, UNITS // 2 - 1) as i:
                for p in range(2):
                    for c in range(HALF):
                        masks((i * (2 * NDVE) + (p + 1) * NDVE + dve_count(c), i * (2 * HALF) + (p + 1) * HALF + c + 1),
                              1 - p, c)
            for c in range(HALF):
                masks(((UNITS - 1) * NDVE + dve_count(c), (UNITS - 1) * HALF + c + 1), 1, c)

        @block.tensor
        def _(pe):
            def scores(T, p, s, first=False):
                g, h = divmod(s, HG)
                if not first:
                    pe.wait_ge(t_exp, T - 1)
                tile = p_s[s % 2]
                for j, col, n in tile_cols(g):
                    i, c = j * BLK, col
                    while i < S:
                        w = min(S - i, 512 - c % 512)
                        last = nc.tensor.matmul(tile[:, c:c + w], k_sb[p][:, h * S + j * BLK:h * S + (j + 1) * BLK],
                                                q_sb[p][:, h * S + i:h * S + i + w], start=True, stop=True)
                        i, c = i + w, c + w
                last.then_inc(t_s, 1)

            def relative(before, p, c, first=False):
                if not first:
                    pe.wait_ge(t_bev, before[0])
                    pe.wait_ge(t_beva, before[1])
                q = q_sb[p][:, :].rearrange("k (q r) -> k r q", r=BLK)
                bank = p_b[c % 2]
                for k in range(RCH):
                    r = (c % HALF) * RCH + k
                    w0 = P - 1 - r if c < HALF else BLK - 1 - r
                    last = nc.tensor.matmul(bank[:, k * QB:(k + 1) * QB], rel_w[:, w0:w0 + BLK], q[:, r, :],
                                            start=True, stop=True)
                last.then_inc(t_bmm, 1)

            def copies(u_dve, u_act, c):
                if c >= 2:
                    return u_dve + dve_count(c - 2), u_act + act_count(c - 2)
                k = CHUNKS - 2 + c
                return u_dve - NDVE + dve_count(k), u_act - len(ACT_CH) + act_count(k)

            def values(need_exp, p, g, piece):
                pieces = pv_pieces(g)
                if piece >= len(pieces):
                    return
                if piece == 0:
                    pe.wait_ge(t_exp, need_exp)
                j, c, i, end = pieces[piece]
                for h in range(HG):
                    last = nc.tensor.matmul(p_o[32 * h:32 * h + 32, i:end], v_sb[p][:, j, h * 32:(h + 1) * 32],
                                            probs[(p + g) % 2][:, h, c:c + end - i],
                                            start=(j == 0), stop=(j == (3 if end <= 512 else 4)))
                if piece == len(pieces) - 1:
                    last.then_inc(t_pv, 1)

            def unit(u, p, last_unit):
                T0 = u * STEPS
                for s in range(HG, STEPS):
                    g, h = divmod(s, HG)
                    scores(T0 + s, p, s)
                    if g == 1 and h == 1:
                        pe.wait_ge(t_v[p], loads(u, p))
                        if not is_first(u):
                            pe.wait_ge(t_o, u)
                    if h >= 1:
                        values(T0 + g * HG, p, g - 1, h - 1)
                    if not last_unit:
                        c = s - HG
                        if c == 0:
                            pe.wait_ge(t_q[1 - p], 2 * loads_next(u, p))
                        relative(copies((u + 1) * NDVE, (u + 1) * len(ACT_CH), c), 1 - p, c)
                if last_unit:
                    values(T0 + STEPS, p, NG - 1, 0)
                else:
                    pe.wait_ge(t_k[1 - p], loads_next(u, p))
                    for s in range(HG):
                        scores(T0 + STEPS + s, 1 - p, s)
                        if s == 1:
                            values(T0 + STEPS, p, NG - 1, 0)
                pe.wait_ge(t_oraw, u + 1)
                for n in range(NB):
                    last = nc.tensor.transpose(p_o[:, n * BLK:(n + 1) * BLK], o_raw[:, n * BLK:(n + 1) * BLK], ident[:, :])
                last.then_inc(t_otr, 1)

            turn = [None]

            def loads(u, p):
                return turn[0] * 16 + 16

            def loads_next(u, p):
                return turn[0] * 16 + 16 + 16 * p

            pe.wait_ge(t_q[0], 32)
            for c in range(CHUNKS):
                relative(copies(0, 0, c) if c >= 2 else None, 0, c, first=c < 2)
            pe.wait_ge(t_k[0], 16)
            for s in range(HG):
                scores(s, 0, s, first=s < 2)
            turn[0] = 0
            unit(0, 0, False)
            unit(1, 1, False)
            with pe.Fori(1, UNITS // 2 - 1) as i:
                turn[0] = i
                for p in range(2):
                    unit(i * 2 + p, p, False)
            turn[0] = UNITS // 2 - 1
            unit(UNITS - 2, 0, False)
            unit(UNITS - 1, 1, True)

        @block.vector
        def _(dve):
            def add(T, p, s):
                g, h = divmod(s, HG)
                dve.wait_ge(t_s, T + 1)
                for j, col, n in tile_cols(g):
                    nb = min(KINDS, n)
                    start = h * (NB * KINDS * BLK) + j * (KINDS * BLK)
                    term = bias[p][:, start:start + nb * 512].rearrange("p (k x) -> p k x", x=512)[:, :, 0:BLK]
                    cols = p_s[s % 2][:, col:col + nb * BLK].rearrange("p (k x) -> p k x", x=BLK)
                    last = nc.vector.tensor_tensor(cols, cols, term, ALU.add)
                last.then_inc(t_add, 1)

            def copy_bank(n, buf, c):
                dve.wait_ge(t_bmm, n)
                nc.vector.tensor_copy(bias_q(buf, 0 if c < HALF else 1, c),
                                      p_b[c % 2][:, :].rearrange("p (r q) -> p q r", q=QB)).then_inc(t_bev, 1)

            def ready(u):
                dve.wait_ge(t_near, u * HALF + HALF)
                dve.wait_ge(t_bev, u * NDVE + NDVE)
                dve.wait_ge(t_beva, u * len(ACT_CH) + len(ACT_CH))

            def unit(u, p, last_unit):
                for s in range(HG, STEPS):
                    add(u * STEPS + s, p, s)
                    c = s - HG
                    if not last_unit and c not in ACT_CH:
                        copy_bank((u + 1) * CHUNKS + c + 1, 1 - p, c)
                if not last_unit:
                    ready(u + 1)
                    for s in range(HG):
                        add((u + 1) * STEPS + s, 1 - p, s)
                dve.wait_ge(t_otr, u + 1)
                o_t = p_o[:, :].rearrange("p (q d) -> p q d", d=32)
                nc.vector.reciprocal(o_rcp[:, :], o_t[:, :, HD]).then_inc(t_rcp, 1)
                dve.wait_ge(t_rcp, u + 1)
                dst = o_all[:, bass.ds(u * (QB * HD), QB * HD)]
                nc.vector.tensor_tensor(dst.rearrange("p (q d) -> p q d", d=HD), o_t[:, :, 0:HD],
                                        o_rcp[:, :].unsqueeze(2).broadcast_to([128, QB, HD]), ALU.mult).then_inc(t_o, 1)

            for c in range(CHUNKS):
                if c not in ACT_CH:
                    copy_bank(c + 1, 0, c)
            ready(0)
            for s in range(HG):
                add(s, 0, s)
            unit(0, 0, False)
            unit(1, 1, False)
            with dve.Fori(1, UNITS // 2 - 1) as i:
                for p in range(2):
                    unit(i * 2 + p, p, False)
            unit(UNITS - 2, 0, False)
            unit(UNITS - 1, 1, True)

        @block.scalar
        def _(act):
            def exps(u, p, s):
                g, h = divmod(s, HG)
                act.wait_ge(t_add, u * STEPS + s + 1)
                width = sum(n for _, _, n in tile_cols(g)) * BLK
                nc.scalar.activation(probs[(p + g) % 2][:, h, 0:width], p_s[s % 2][:, 0:width], ACT.Exp,
                                     scale=SCALE).then_inc(t_exp, 1)

            def copy_bank(n, buf, c):
                act.wait_ge(t_bmm, n)
                nc.scalar.activation(bias_q(buf, 1, c), p_b[c % 2][:, :].rearrange("p (r q) -> p q r", q=QB),
                                     ACT.Copy).then_inc(t_beva, 1)

            def unit(u, p, last_unit):
                for s in range(HG, STEPS):
                    g, h = divmod(s, HG)
                    if h == 0 and not (is_first(u) and g == 1):
                        act.wait_ge(t_pv, u * NG + g - 1)
                    exps(u, p, s)
                    c = s - HG
                    if not last_unit and c in ACT_CH:
                        copy_bank((u + 1) * CHUNKS + c + 1, 1 - p, c)
                if not last_unit:
                    act.wait_ge(t_pv, u * NG + NG - 1)
                    exps(u + 1, 1 - p, 0)
                    exps(u + 1, 1 - p, 1)
                act.wait_ge(t_pv, u * NG + NG)
                if not is_first(u):
                    act.wait_ge(t_otr, u)
                nc.scalar.activation(o_raw[:, :], p_o[:, :], ACT.Copy).then_inc(t_oraw, 1)
                if not last_unit:
                    exps(u + 1, 1 - p, 2)
                    exps(u + 1, 1 - p, 3)

            for c in sorted(ACT_CH):
                copy_bank(c + 1, 0, c)
            for s in range(HG):
                exps(0, 0, s)
            unit(0, 0, False)
            unit(1, 1, False)
            with act.Fori(1, UNITS // 2 - 1) as i:
                for p in range(2):
                    unit(i * 2 + p, p, False)
            unit(UNITS - 2, 0, False)
            unit(UNITS - 1, 1, True)
    ptwo.close()
    two.close()

    stage3(nc, ctx, sb, ps, sem, ident, o_all, x, Wo, bo, w1, s1, w2, s2, h1, sh1, h2, sh2, w3, s3, out)


def stage3(nc, ctx, sb, ps, sem, ident, o_all, x, Wo, bo, w1, s1, w2, s2, h1, sh1, h2, sh2, w3, s3, out):
    wo_sb = sb("wo_sb", [128, 128])
    bo_b = sb("bo_b", [128, NB, 128])
    s1_c, s2_c, sh1_c, sh2_c = (sb(n, [128, HC]) for n in ("s1_c", "s2_c", "sh1_c", "sh2_c"))
    s3_c = sb("s3_c", [128, 1])
    WEIGHTS = [("w1", w1, HC, E), ("w2", w2, HC, E), ("h1", h1, HC, HID), ("h2", h2, HC, HID), ("w3", w3, 1, HID)]
    wnat = [sb(f"{n}_nat", [128, rows, cols]) for n, _, rows, cols in WEIGHTS]
    whi = [sb(f"{n}_hi", [128, cols // 128, rows * 128], F32R) for n, _, rows, cols in WEIGHTS]
    wlo = [sb(f"{n}_lo", [128, cols // 128, rows * 128], F32R) for n, _, rows, cols in WEIGHTS]
    x1_all = sb("x1_all", [128, TOK])
    x1T_hi = sb("x1T_hi", [128, TOK], F32R)
    x1T_lo = sb("x1T_lo", [128, TOK], F32R)
    big = ExitStack()
    xres = sb("xres", [128, NB, 128], F32, big)
    o_cur = sb("o_cur", [128, NB, 128], F32, big)
    oT = sb("oT", [128, S], F32, big)
    y = sb("y", [128, NB, 128], F32, big)
    x1c = sb("x1c", [128, NB, 128], F32, big)
    st3 = sb("st3", [128, NB, 6], F32, big)
    mv3 = sb("mv3", [128, NB, 2], F32, big)
    ve3, sd3, rs3, nm3 = (sb(n, [128, NB], F32, big) for n in ("ve3", "sd3", "rs3", "nm3"))
    pb = ExitStack()
    p_w = [ps(f"p_w{k}", [128, 512], pb) for k in range(4)]
    p_a = ps("p_a", [128, S], pb)
    p_y = ps("p_y", [128, S], pb)

    a_alone = sem("a_alone")
    a_ld = sem("a_ld")
    a_w = sem("a_w")
    a_whi, a_wlo = sem("a_whi"), sem("a_wlo")
    a_x = sem("a_x")
    a_oc = sem("a_oc")
    a_tr = sem("a_tr")
    a_oT = sem("a_oT")
    a_y = sem("a_y")
    a_ln = sem("a_ln")
    a_sd = sem("a_sd")
    a_keep = sem("a_keep")
    a_xtr = sem("a_xtr")
    a_hi, a_lo = sem("a_hi"), sem("a_lo")
    LNS = 14

    wbanks = []
    for w, (_, _, rows, cols) in enumerate(WEIGHTS):
        for k in range(cols // 128):
            wbanks.append((w, k, rows))

    with nc.Block() as block:
        @block.sync
        def _(sp):
            loads = [(wo_sb[:, :], Wo), (bo_b[:, :, :], ap(bo.tensor, 0, [[0, 128], [0, NB], [1, 128]])),
                     (s3_c[:, :], s3.rearrange("(p a) -> p a", a=1))]
            loads += [(d[:, :], ap(v.tensor, 0, [[1, 128], [128, HC]]))
                      for d, v in ((s1_c, s1), (s2_c, s2), (sh1_c, sh1), (sh2_c, sh2))]
            loads += [(d[:, :, :], v.rearrange("(r p) c -> p r c", p=128)) for d, (_, v, _, _) in zip(wnat, WEIGHTS)]
            for dst, src in loads:
                sp.dma_start(dst, src).then_inc(a_ld, 16)
            def batch(b, first):
                if not first:
                    sp.wait_ge(a_ln, b * LNS)
                sp.dma_start(xres[:, :, :], ap(x.tensor, b * (S * E), [[E, 128], [128 * E, NB], [1, E]])).then_inc(a_x, 16)

            turns(sp, B, batch)

        @block.tensor
        def _(pe):
            pe.wait_ge(a_ld, 12 * 16)
            for n, (w, k, rows) in enumerate(wbanks):
                if n >= 4:
                    pe.wait_ge(a_whi, n - 3)
                    pe.wait_ge(a_wlo, n - 3)
                for r in range(rows):
                    last = nc.tensor.transpose(p_w[n % 4][:, r * 128:(r + 1) * 128],
                                               wnat[w][:, r, k * 128:(k + 1) * 128], ident[:, :])
                last.then_inc(a_w, 1)
            def batch(b, first):
                pe.wait_ge(a_oc, b + 1)
                if not first:
                    pe.wait_ge(a_lo, b)
                for t in range(NB):
                    last = nc.tensor.transpose(p_a[:, t * 128:(t + 1) * 128], o_cur[:, t, :], ident[:, :])
                last.then_inc(a_tr, 1)
                pe.wait_ge(a_oT, b + 1)
                for t in range(NB):
                    last = nc.tensor.matmul(p_y[:, t * 128:(t + 1) * 128], oT[:, t * 128:(t + 1) * 128], wo_sb[:, :],
                                            start=True, stop=True)
                last.then_inc(a_y, 1)
                pe.wait_ge(a_ln, b * LNS + 14)
                for t in range(NB):
                    last = nc.tensor.transpose(p_a[:, t * 128:(t + 1) * 128], y[:, t, :], ident[:, :])
                last.then_inc(a_xtr, 1)

            turns(pe, B, batch)

        @block.scalar
        def _(act):
            for n, (w, k, rows) in enumerate(wbanks):
                act.wait_ge(a_w, n + 1)
                nc.scalar.activation(whi[w][:, k, :], p_w[n % 4][:, 0:rows * 128], ACT.Copy).then_inc(a_whi, 1)
            def batch(b, first):
                if not first:
                    act.wait_ge(a_tr, b)
                src = o_all[:, bass.ds(b * (NB * 128), NB * 128)].rearrange("p (g n d) -> p n g d", g=BG, n=NB)
                nc.scalar.activation(o_cur[:, :, :].rearrange("p n (g d) -> p n g d", g=BG), src,
                                     ACT.Copy).then_inc(a_oc, 1)
                act.wait_ge(a_tr, b + 1)
                if not first:
                    act.wait_ge(a_y, b)
                nc.scalar.activation(oT[:, :], p_a[:, :], ACT.Copy).then_inc(a_oT, 1)
                act.wait_ge(a_ln, b * LNS + 4)
                nc.scalar.activation(sd3[:, :], ve3[:, :], ACT.Sqrt).then_inc(a_sd, 1)
                act.wait_ge(a_ln, b * LNS + 8)
                nc.scalar.activation(x1_all[:, bass.ds(b * S, S)], x1c[:, :, :].rearrange("p n e -> p (n e)"),
                                     ACT.Copy).then_inc(a_keep, 1)
                act.wait_ge(a_ln, b * LNS + 11)
                nc.scalar.activation(sd3[:, :], ve3[:, :], ACT.Sqrt).then_inc(a_sd, 1)
                act.wait_ge(a_xtr, b + 1)
                nc.scalar.activation(x1T_hi[:, bass.ds(b * S, S)], p_a[:, :], ACT.Copy).then_inc(a_hi, 1)

            turns(act, B, batch)

        @block.vector
        def _(dve):
            for n, (w, k, rows) in enumerate(wbanks):
                dve.wait_ge(a_whi, n + 1)
                nc.vector.tensor_tensor(wlo[w][:, k, :], p_w[n % 4][:, 0:rows * 128],
                                        whi[w][:, k, :].bitcast(F32), ALU.subtract).then_inc(a_wlo, 1)
            dve.wait_ge(a_ld, 12 * 16)
            def batch(b, first):
                def step(ins, k):
                    ins.then_inc(a_ln, 1)
                    dve.wait_ge(a_ln, b * LNS + k)

                def norm(src, k, sd):
                    for t in range(NB):
                        last = nc.vector.bn_stats(st3[:, t, :], src[:, t, :])
                    last.then_inc(a_ln, 1)
                    wait_alone(dve, a_ln, b * LNS + k + 1, a_alone)
                    for t in range(NB):
                        last = nc.vector.bn_aggr(mv3[:, t, :], st3[:, t, :])
                    step(last, k + 2)
                    nc.vector.tensor_scalar(ve3[:, :], mv3[:, :, 1], EPS, None, ALU.add).then_inc(a_ln, 1)
                    dve.wait_ge(a_sd, b * 2 + sd)
                    step(nc.vector.reciprocal(rs3[:, :], sd3[:, :]), k + 4)
                    step(nc.vector.scalar_tensor_tensor(out=nm3[:, :], in0=mv3[:, :, 0], scalar=-1.0, in1=rs3[:, :],
                                                        op0=ALU.mult, op1=ALU.mult), k + 5)

                dve.wait_ge(a_y, b + 1)
                if not first:
                    dve.wait_ge(a_xtr, b)
                step(nc.vector.tensor_tensor(y[:, :, :], p_y[:, :].rearrange("p (n e) -> p n e", n=NB), bo_b[:, :, :],
                                             ALU.add), 1)
                norm(y, 1, 1)
                for t in range(NB):
                    last = nc.vector.tensor_scalar(y[:, t, :], y[:, t, :], rs3[:, t:t + 1], nm3[:, t:t + 1],
                                                   ALU.mult, ALU.add)
                step(last, 7)
                dve.wait_ge(a_x, b * 16 + 16)
                if not first:
                    dve.wait_ge(a_keep, b)
                step(nc.vector.tensor_tensor(x1c[:, :, :], y[:, :, :], xres[:, :, :], ALU.add), 8)
                norm(x1c, 8, 2)
                for t in range(NB):
                    last = nc.vector.tensor_scalar(y[:, t, :], x1c[:, t, :], rs3[:, t:t + 1], nm3[:, t:t + 1],
                                                   ALU.mult, ALU.add)
                last.then_inc(a_ln, 1)
                dve.wait_ge(a_hi, b + 1)
                nc.vector.tensor_tensor(x1T_lo[:, bass.ds(b * S, S)], p_a[:, :],
                                        x1T_hi[:, bass.ds(b * S, S)].bitcast(F32), ALU.subtract).then_inc(a_lo, 1)

            turns(dve, B, batch)
    pb.close()
    big.close()

    act_f = sb("act_f", [128, HC, FC])
    prod = sb("prod", [128, HC, FC])
    hid_hi = [sb(f"hid{k}_hi", [128, HC, FC], F32R) for k in range(2)]
    hid_lo = [sb(f"hid{k}_lo", [128, HC, FC], F32R) for k in range(2)]
    zT = sb("zT", [128, FC])
    NT = FC // 128
    st4 = sb("st4", [128, NT, 6])
    mv4 = sb("mv4", [128, NT, 2])
    ve4, sd4, rs4, nm4 = (sb(n, [128, NT]) for n in ("ve4", "sd4", "rs4", "nm4"))
    yn = sb("yn", [128, NT, 128])
    res = sb("res", [128, NT, 128])
    p_z = [ps(f"p_z{k}", [128, FC]) for k in range(6)]
    p_t = ps("p_t", [128, FC])

    f_alone = sem("f_alone")
    f_z = sem("f_z")
    f_act = sem("f_act")
    f_mul = sem("f_mul")
    f_hi = sem("f_hi")
    f_lo = sem("f_lo")
    f_zT = sem("f_zT")
    f_tr = sem("f_tr")
    f_ln = sem("f_ln")
    f_sd = sem("f_sd")
    f_out = sem("f_out")
    ZT = 4 * HC + 1
    FLN = 6

    with nc.Block() as block:
        @block.sync
        def _(sp):
            def chunk(c, first):
                sp.wait_ge(f_ln, c * FLN + FLN)
                sp.dma_start(ap(out.tensor, c * (FC * E), [[E, 128], [128 * E, NT], [1, E]]),
                             res[:, :, :]).then_inc(f_out, 16)

            turns(sp, NFC, chunk)
            sp.wait_ge(f_out, 16 * NFC)

        @block.tensor
        def _(pe):
            def chunk(c, first):
                def layer(tile, w, o, hi, lo):
                    bank = p_z[tile % 6]
                    cols = slice(o * 128, (o + 1) * 128)
                    n = len(hi)
                    for k in range(n):
                        nc.tensor.matmul(bank[:, :], whi[w][:, k, cols], hi[k], start=(k == 0), stop=False)
                        nc.tensor.matmul(bank[:, :], whi[w][:, k, cols], lo[k], start=False, stop=False)
                        last = nc.tensor.matmul(bank[:, :], wlo[w][:, k, cols], hi[k], start=False, stop=(k == n - 1))
                    last.then_inc(f_z, 1)

                xin_hi, xin_lo = [x1T_hi[:, bass.ds(c * FC, FC)]], [x1T_lo[:, bass.ds(c * FC, FC)]]
                for o in range(HC):
                    for w in range(2):
                        tile = 2 * o + w
                        if tile == 4:
                            if not first:
                                pe.wait_ge(f_zT, c)
                        if tile == 6:
                            pe.wait_ge(f_act, c * (3 * HC) + 1)
                        if tile == 7:
                            pe.wait_ge(f_mul, c * HC + 1)
                        layer(tile, w, o, xin_hi, xin_lo)
                for l in range(2):
                    pe.wait_ge(f_lo, c * (3 * HC) + (l + 1) * HC)
                    hi, lo = ([t[l % 2][:, k, :] for k in range(HC)] for t in (hid_hi, hid_lo))
                    for o in range(HC):
                        layer((2 + l) * HC + o, 2 + l, o, hi, lo)
                pe.wait_ge(f_lo, c * (3 * HC) + 3 * HC)
                layer(4 * HC, 4, 0, *([t[0][:, k, :] for k in range(HC)] for t in (hid_hi, hid_lo)))
                pe.wait_ge(f_zT, c + 1)
                if not first:
                    pe.wait_ge(f_ln, c * FLN)
                for t in range(NT):
                    last = nc.tensor.transpose(p_t[:, t * 128:(t + 1) * 128], zT[:, t * 128:(t + 1) * 128], ident[:, :])
                last.then_inc(f_tr, 1)

            turns(pe, NFC, chunk)

        @block.scalar
        def _(act):
            def chunk(c, first):
                for o in range(HC):
                    act.wait_ge(f_z, c * ZT + 2 * o + 1)
                    if not first:
                        act.wait_ge(f_lo, c * (3 * HC))
                    nc.scalar.activation(act_f[:, o, :], p_z[(2 * o) % 6][:, :], ACT.Silu,
                                         scale=s1_c[:, o:o + 1]).then_inc(f_act, 1)
                for l, sc in ((0, sh1_c), (1, sh2_c)):
                    for o in range(HC):
                        tile = (2 + l) * HC + o
                        act.wait_ge(f_z, c * ZT + tile + 1)
                        nc.scalar.activation(act_f[:, o, :], p_z[tile % 6][:, :], ACT.Gelu,
                                             scale=sc[:, o:o + 1]).then_inc(f_act, 1)
                act.wait_ge(f_z, c * ZT + ZT)
                nc.scalar.activation(zT[:, :], p_z[(4 * HC) % 6][:, :], ACT.Copy, scale=s3_c[:, 0:1]).then_inc(f_zT, 1)
                act.wait_ge(f_ln, c * FLN + 3)
                nc.scalar.activation(sd4[:, :], ve4[:, :], ACT.Sqrt).then_inc(f_sd, 1)

            turns(act, NFC, chunk)

        @block.vector
        def _(dve):
            def chunk(c, first):
                def split(src, l, o, k):
                    nc.vector.tensor_copy(hid_hi[l][:, o, :], src).then_inc(f_hi, 1)
                    dve.wait_ge(f_hi, c * (3 * HC) + k + 1)
                    nc.vector.tensor_tensor(hid_lo[l][:, o, :], src, hid_hi[l][:, o, :].bitcast(F32),
                                            ALU.subtract).then_inc(f_lo, 1)

                def step(ins, k):
                    ins.then_inc(f_ln, 1)
                    dve.wait_ge(f_ln, c * FLN + k)

                if not first:
                    dve.wait_ge(f_z, c * ZT)
                for o in range(HC):
                    dve.wait_ge(f_z, c * ZT + 2 * o + 2)
                    dve.wait_ge(f_act, c * (3 * HC) + o + 1)
                    nc.vector.scalar_tensor_tensor(out=prod[:, o, :], in0=p_z[(2 * o + 1) % 6][:, :],
                                                   scalar=s2_c[:, o:o + 1], in1=act_f[:, o, :],
                                                   op0=ALU.mult, op1=ALU.mult).then_inc(f_mul, 1)
                    dve.wait_ge(f_mul, c * HC + o + 1)
                    split(prod[:, o, :], 0, o, o)
                for l in range(2):
                    for o in range(HC):
                        dve.wait_ge(f_act, c * (3 * HC) + (l + 1) * HC + o + 1)
                        split(act_f[:, o, :], 1 - l, o, (l + 1) * HC + o)
                dve.wait_ge(f_tr, c + 1)
                for t in range(NT):
                    last = nc.vector.bn_stats(st4[:, t, :], p_t[:, t * 128:(t + 1) * 128])
                last.then_inc(f_ln, 1)
                wait_alone(dve, f_ln, c * FLN + 1, f_alone)
                for t in range(NT):
                    last = nc.vector.bn_aggr(mv4[:, t, :], st4[:, t, :])
                step(last, 2)
                nc.vector.tensor_scalar(ve4[:, :], mv4[:, :, 1], EPS, None, ALU.add).then_inc(f_ln, 1)
                dve.wait_ge(f_sd, c + 1)
                step(nc.vector.reciprocal(rs4[:, :], sd4[:, :]), 4)
                for t in range(NT):
                    last = nc.vector.tensor_scalar(yn[:, t, :], p_t[:, t * 128:(t + 1) * 128], mv4[:, t, 0:1],
                                                   rs4[:, t:t + 1], ALU.subtract, ALU.mult)
                step(last, 5)
                if not first:
                    dve.wait_ge(f_out, c * 16)
                nc.vector.tensor_tensor(res[:, :, :], yn[:, :, :],
                                        x1_all[:, bass.ds(c * FC, FC)].rearrange("p (n e) -> p n e", n=NT),
                                        ALU.add).then_inc(f_ln, 1)

            turns(dve, NFC, chunk)


_INS = ['L0_attn_x', 'L0_attn_Wq', 'L0_attn_bq', 'L0_attn_Wk', 'L0_attn_bk', 'L0_attn_Wv', 'L0_attn_bv', 'L0_attn_Wo',
        'L0_attn_bo', 'L0_attn_rel_key', 'L0_ffn_w1_w', 'L0_ffn_w1_s', 'L0_ffn_w2_w', 'L0_ffn_w2_s', 'L0_ffn_h1_w',
        'L0_ffn_h1_s', 'L0_ffn_h2_w', 'L0_ffn_h2_s', 'L0_ffn_w3_w', 'L0_ffn_w3_s']


def kernel(**inputs):
    import numpy as _np
    import concourse.bacc as _bacc
    from concourse import mybir as _mybir
    from concourse.bass_utils import run_bass_kernel_spmd as _run

    nc = _bacc.Bacc("TRN2", target_bir_lowering=False, num_devices=1)
    arrays, args = {}, []
    for name in _INS:
        a = _np.ascontiguousarray(inputs[name])
        arrays[f"in_{name}_dram"] = a
        args.append(nc.dram_tensor(f"in_{name}_dram", a.shape, _mybir.dt.from_np(a.dtype), kind="ExternalInput").ap())
    args.append(nc.dram_tensor("out_dram", (B, S, E), _mybir.dt.float32, kind="ExternalOutput").ap())
    attention_ffn(nc, *args)
    r = _run(nc, [arrays], core_ids=[0])
    return r.results[0]["out_dram"]
```

```python
import concourse.bass as bass
from concourse import mybir
from contextlib import ExitStack

F32 = mybir.dt.float32
F32R = mybir.dt.float32r
BF16 = mybir.dt.bfloat16
ALU = mybir.AluOpType
ACT = mybir.ActivationFunctionType
AX = mybir.AxisListType

B, S, E = 4, 1024, 128
HD, H = 8, 16
P = 256
HID = 512
TOK = B * S
BLK = 128
NB = S // BLK
HG = 4
UNITS = B * H // HG
PARTS = 3
ROWS = PARTS * PARTS * HD
KROWS = 96
EPS = 1e-5
SCALE = float(HD) ** -0.5
MASKED = -1.0e30
GROUPS = [(0,), (1, 7), (2, 6), (3, 5), (4,)]
NG = len(GROUPS)
STEPS = NG * HG
RCH = 16
CHUNKS = 2 * BLK // RCH
HALF = CHUNKS // 2
QB = HG * NB
BG = H // HG
UNIT_QK = PARTS * HD * HG * S
KINDS = 3
BIASCOLS = QB * KINDS * BLK
FC = 512
NC = S // FC
NT = FC // 128
NZ = 4
HC = HID // 128


def is_first(u):
    return isinstance(u, int) and u == 0


def ap(handle, offset, dims):
    return bass.AP(handle, offset, dims)


def wait_alone(eng, sem, value, passed):
    eng.wait_ge(sem, value)
    eng.sem_inc(passed, 1)


def turns(eng, n, body):
    body(0, True)
    with eng.Fori(1, n) as i:
        body(i, False)


def attention_ffn(nc, x, Wq, bq, Wk, bk, Wv, bv, Wo, bo, rel, w1, s1, w2, s2, h1, sh1, h2, sh2, w3, s3, out):
    with ExitStack() as ctx:
        ctx.enter_context(nc.allow_non_contiguous_dma(reason="small parameters"))
        build(nc, ctx, x, Wq, bq, Wk, bk, Wv, bv, Wo, bo, rel, w1, s1, w2, s2, h1, sh1, h2, sh2, w3, s3, out)


def build(nc, ctx, x, Wq, bq, Wk, bk, Wv, bv, Wo, bo, rel, w1, s1, w2, s2, h1, sh1, h2, sh2, w3, s3, out):
    def sb(name, shape, dt=F32, where=ctx):
        return where.enter_context(nc.sbuf_tensor(name, shape, dt))

    def ps(name, shape, where=ctx):
        return where.enter_context(nc.psum_tensor(name, shape, F32))

    def sem(name):
        return ctx.enter_context(nc.semaphore(name))

    q_dram = nc.dram_tensor("q_dram", [UNITS, PARTS, HD, HG, S], BF16, kind="Internal")
    k_dram = nc.dram_tensor("k_dram", [UNITS, HD, PARTS, HG, S], BF16, kind="Internal")
    m_dram = nc.dram_tensor("m_dram", [UNITS, PARTS, HG, S], BF16, kind="Internal")
    v_dram = nc.dram_tensor("v_dram", [B, BG, 128, NB, HG, 32], F32, kind="Internal")
    g_dram = nc.dram_tensor("g_dram", [HD, PARTS, P], BF16, kind="Internal")
    gx_dram = nc.dram_tensor("gx_dram", [HD, 2], F32, kind="Internal")

    ident = sb("ident", [128, 128])
    rel_w = sb("rel_w", [KROWS, P + BLK], BF16)
    o_all = sb("o_all", [128, UNITS * NB * 32])

    one = ExitStack()
    wq_sb, wk_sb, wv_sb = (sb(n, [128, 128], F32, one) for n in ("wq_sb", "wk_sb", "wv_sb"))
    bq_c, bk_c, r0_c, kb_c = (sb(n, [128, 1], F32, one) for n in ("bq_c", "bk_c", "r0_c", "kb_c"))
    bv_b = sb("bv_b", [128, NB, 128], F32, one)
    rel_t = sb("rel_t", [HD, P], F32, one)
    rel_s = sb("rel_s", [HD, P], F32, one)
    rel_r = sb("rel_r", [HD, P], F32, one)
    rel_p = sb("rel_p", [HD, PARTS, P], BF16, one)
    gx = sb("gx", [HD, 2], F32, one)
    g_ext = sb("g_ext", [128, 2], F32, one)
    hmask = sb("hmask", [128, H], F32, one)
    xin = sb("xin", [128, NB, 128], F32, one)
    xh = sb("xh", [128, NB, 128], F32, one)
    stats = sb("stats", [128, NB, 6], F32, one)
    mv = sb("mv", [128, NB, 2], F32, one)
    var_e, std, rstd, nmr = (sb(n, [128, NB], F32, one) for n in ("var_e", "std", "rstd", "nmr"))
    xT = sb("xT", [128, S], F32, one)
    qf, kf, q_rest, k_rest = (sb(n, [128, S], F32, one) for n in ("qf", "kf", "q_rest", "k_rest"))
    q_parts, k_parts = (sb(n, [128, PARTS, S], BF16, one) for n in ("q_parts", "k_parts"))
    q_pos, q_neg = (sb(n, [128, S], F32, one) for n in ("q_pos", "q_neg"))
    k_ext = sb("k_ext", [128, 2], F32, one)
    k_sel = sb("k_sel", [128, 2, H], F32, one)
    m_neg, m_rest = (sb(n, [H, S], F32, one) for n in ("m_neg", "m_rest"))
    m_parts = sb("m_parts", [H, PARTS, S], BF16, one)
    v_st = sb("v_st", [128, NB, H, 32], F32, one)
    pone = ExitStack()
    p_tr, p_q, p_k, p_v = (ps(n, [128, S], pone) for n in ("p_tr", "p_q", "p_k", "p_v"))

    s_alone = sem("s_alone")
    s_par = sem("s_par")
    s_gs = sem("s_gs")
    s_gst = sem("s_gst")
    s_gld = sem("s_gld")
    s_rw = sem("s_rw")
    s_pool = sem("s_pool")
    s_xin = sem("s_xin")
    s_ln = sem("s_ln")
    s_std = sem("s_std")
    s_xh = sem("s_xh")
    s_tr = sem("s_tr")
    s_xT = sem("s_xT")
    s_q, s_k, s_v = sem("s_q"), sem("s_k"), sem("s_v")
    s_qf, s_kf = sem("s_qf"), sem("s_kf")
    s_part = sem("s_part")
    s_hi = sem("s_hi")
    s_vst = sem("s_vst")
    s_qst, s_kst, s_mst, s_vout = sem("s_qst"), sem("s_kst"), sem("s_mst"), sem("s_vout")
    s_u = sem("s_u")
    LNS = 5
    PRT = 14

    with nc.Block() as block:
        @block.sync
        def _(sp):
            for dst, src in ((wq_sb[:, :], Wq), (wk_sb[:, :], Wk), (wv_sb[:, :], Wv),
                             (bq_c[:, :], bq.rearrange("(p a) -> p a", a=1)),
                             (bk_c[:, :], bk.rearrange("(p a) -> p a", a=1)),
                             (r0_c[:, :], ap(rel.tensor, 0, [[0, H], [1, HD], [1, 1]])),
                             (bv_b[:, :, :], ap(bv.tensor, 0, [[0, 128], [0, NB], [1, 128]])),
                             (rel_t[:, :], ap(rel.tensor, 0, [[1, HD], [HD, P]]))):
                sp.dma_start(dst, src).then_inc(s_par, 16)
            sp.dma_start(xin[:, :, :], ap(x.tensor, 0, [[E, 128], [128 * E, NB], [1, E]])).then_inc(s_xin, 16)
            sp.wait_ge(s_gs, 8)
            sp.dma_start(g_dram.ap(), rel_p[:, :, :]).then_inc(s_gst, 16)
            sp.dma_start(gx_dram.ap(), gx[:, :]).then_inc(s_gst, 16)
            sp.wait_ge(s_gst, 32)
            sp.dma_start(g_ext[:, :], ap(gx_dram, 0, [[0, H], [2, HD], [1, 2]])).then_inc(s_gld, 16)
            sp.wait_ge(s_pool, 1)
            sp.dma_start(rel_w[0:ROWS, 0:P], ap(g_dram, 0, [[0, PARTS], [P, HD * PARTS], [1, P]])).then_inc(s_rw, 16)
            sp.dma_start(rel_w[0:ROWS, P:P + BLK],
                         ap(g_dram, 0, [[0, PARTS], [P, HD * PARTS], [1, BLK]])).then_inc(s_rw, 16)
            sp.wait_ge(s_rw, 32)
            def batch(b, first):
                sp.wait_ge(s_xh, b + 1)
                nxt = (b + 1) % B
                sp.dma_start(xin[:, :, :], ap(x.tensor, nxt * (S * E), [[E, 128], [128 * E, NB], [1, E]])).then_inc(s_xin, 16)
                sp.wait_ge(s_vst, b + 1)
                for g in range(BG):
                    sp.dma_start(ap(v_dram, b * (128 * NB * H * 32) + g * (128 * NB * HG * 32),
                                    [[NB * HG * 32, 128], [HG * 32, NB], [1, HG * 32]]),
                                 v_st[:, :, g * HG:(g + 1) * HG, :].rearrange("p n h d -> p n (h d)")).then_inc(s_vout, 16)
                sp.wait_ge(s_part, b * PRT + 9)
                for g in range(BG):
                    rows = slice(g * HG * HD, (g + 1) * HG * HD)
                    for part in range(PARTS):
                        sp.dma_start(ap(q_dram, b * (BG * UNIT_QK) + g * UNIT_QK + part * (HD * HG * S),
                                        [[S, HG], [HG * S, HD], [1, S]]), q_parts[rows, part, :]).then_inc(s_qst, 16)
                        sp.dma_start(ap(k_dram, b * (BG * UNIT_QK) + g * UNIT_QK + part * (HG * S),
                                        [[S, HG], [PARTS * HG * S, HD], [1, S]]), k_parts[rows, part, :]).then_inc(s_kst, 16)
                sp.wait_ge(s_part, b * PRT + PRT)
                for g in range(BG):
                    sp.dma_start(ap(m_dram, b * (H * PARTS * S) + g * (HG * PARTS * S), [[S, HG], [HG * S, PARTS], [1, S]]),
                                 m_parts[g * HG:(g + 1) * HG, :, :]).then_inc(s_mst, 16)

            turns(sp, B, batch)
            sp.wait_ge(s_xin, 16 * (B + 1))
            sp.wait_ge(s_vout, 16 * (BG) * B)
            sp.wait_ge(s_qst, 16 * PARTS * BG * B)
            sp.wait_ge(s_kst, 16 * PARTS * BG * B)
            sp.wait_ge(s_mst, 16 * BG * B)

        @block.gpsimd
        def _(pool):
            def step(ins, n):
                ins.then_inc(s_pool, 1)
                pool.wait_ge(s_pool, n)

            step(nc.gpsimd.memset(rel_w[64:KROWS, :], 0.0), 1)
            step(nc.gpsimd.memset(ident[:, :], 0.0), 2)
            step(nc.gpsimd.memset(hmask[:, :], 1.0), 3)
            step(nc.gpsimd.memset(v_st[:, :, :, HD:32], 0.0), 4)
            step(nc.gpsimd.affine_select(out=ident[:, :], in_=ident[:, :], compare_op=ALU.not_equal, fill=1.0,
                                         base=0, pattern=[[-1, 128]], channel_multiplier=1), 5)
            step(nc.gpsimd.affine_select(out=hmask[:, :], in_=hmask[:, :], compare_op=ALU.is_ge, fill=0.0,
                                         base=0, pattern=[[-HD, H]], channel_multiplier=1), 6)
            step(nc.gpsimd.affine_select(out=hmask[:, :], in_=hmask[:, :], compare_op=ALU.is_ge, fill=0.0,
                                         base=HD - 1, pattern=[[HD, H]], channel_multiplier=-1), 7)
            step(nc.gpsimd.memset(v_st[:, :, :, HD:HD + 1], 1.0), 8)

        @block.vector
        def _(dve):
            dve.wait_ge(s_par, 8 * 16)
            nc.vector.tensor_tensor(kb_c[:, :], bk_c[:, :], r0_c[:, :], ALU.add).then_inc(s_gs, 1)
            nc.vector.tensor_scalar(rel_s[:, :], rel_t[:, :], rel_t[:, 0:1], None, ALU.subtract).then_inc(s_gs, 1)
            dve.wait_ge(s_gs, 2)
            nc.vector.tensor_reduce(out=gx[:, 0:1], in_=rel_s[:, :], op=ALU.max, axis=AX.X).then_inc(s_gs, 1)
            nc.vector.tensor_reduce(out=gx[:, 1:2], in_=rel_s[:, :], op=ALU.min, axis=AX.X).then_inc(s_gs, 1)
            nc.vector.tensor_copy(rel_p[:, 0, :], rel_s[:, :]).then_inc(s_gs, 1)
            dve.wait_ge(s_gs, 5)
            nc.vector.tensor_tensor(rel_r[:, :], rel_s[:, :], rel_p[:, 0, :], ALU.subtract).then_inc(s_gs, 1)
            dve.wait_ge(s_gs, 6)
            nc.vector.tensor_copy(rel_p[:, 1, :], rel_r[:, :]).then_inc(s_gs, 1)
            dve.wait_ge(s_gs, 7)
            nc.vector.tensor_tensor(rel_p[:, 2, :], rel_r[:, :], rel_p[:, 1, :], ALU.subtract).then_inc(s_gs, 1)
            dve.wait_ge(s_gld, 16)
            dve.wait_ge(s_pool, 8)
            def batch(b, first):
                def ln_wait(k):
                    dve.wait_ge(s_ln, b * LNS + k)

                def part_wait(k):
                    dve.wait_ge(s_part, b * PRT + k)

                dve.wait_ge(s_xin, b * 16 + 16)
                for t in range(NB):
                    last = nc.vector.bn_stats(stats[:, t, :], xin[:, t, :])
                last.then_inc(s_ln, 1)
                wait_alone(dve, s_ln, b * LNS + 1, s_alone)
                for t in range(NB):
                    last = nc.vector.bn_aggr(mv[:, t, :], stats[:, t, :])
                last.then_inc(s_ln, 1)
                ln_wait(2)
                nc.vector.tensor_scalar(var_e[:, :], mv[:, :, 1], EPS, None, ALU.add).then_inc(s_ln, 1)
                dve.wait_ge(s_std, b + 1)
                nc.vector.reciprocal(rstd[:, :], std[:, :]).then_inc(s_ln, 1)
                ln_wait(4)
                nc.vector.scalar_tensor_tensor(out=nmr[:, :], in0=mv[:, :, 0], scalar=-1.0, in1=rstd[:, :],
                                               op0=ALU.mult, op1=ALU.mult).then_inc(s_ln, 1)
                ln_wait(5)
                if not first:
                    dve.wait_ge(s_tr, b * 2)
                for t in range(NB):
                    last = nc.vector.tensor_scalar(xh[:, t, :], xin[:, t, :], rstd[:, t:t + 1], nmr[:, t:t + 1],
                                                   ALU.mult, ALU.add)
                last.then_inc(s_xh, 1)
                dve.wait_ge(s_kf, b + 1)
                nc.vector.tensor_reduce(out=k_ext[:, 0:1], in_=kf[:, :], op=ALU.max, axis=AX.X).then_inc(s_part, 1)
                nc.vector.tensor_reduce(out=k_ext[:, 1:2], in_=kf[:, :], op=ALU.min, axis=AX.X).then_inc(s_part, 1)
                dve.wait_ge(s_qf, b + 1)
                nc.vector.tensor_scalar(q_pos[:, :], qf[:, :], 0.0, None, ALU.max).then_inc(s_part, 1)
                nc.vector.tensor_scalar(q_neg[:, :], qf[:, :], 0.0, None, ALU.min).then_inc(s_part, 1)
                part_wait(2)
                nc.vector.tensor_tensor(k_ext[:, :], k_ext[:, :], g_ext[:, :], ALU.add).then_inc(s_part, 1)
                part_wait(5)
                for e in range(2):
                    last = nc.vector.tensor_scalar(k_sel[:, e, :], hmask[:, :], k_ext[:, e:e + 1], None, ALU.mult)
                last.then_inc(s_part, 1)
                dve.wait_ge(s_v, b + 1)
                if not first:
                    dve.wait_ge(s_vout, b * (16 * BG))
                nc.vector.tensor_tensor(v_st[:, :, :, 0:HD], p_v[:, :].rearrange("p (n h d) -> p n h d", n=NB, h=H),
                                        bv_b[:, :, :].rearrange("p n (h d) -> p n h d", h=H), ALU.add).then_inc(s_vst, 1)
                dve.wait_ge(s_hi, b * 6 + 2)
                nc.vector.tensor_tensor(q_rest[:, :], qf[:, :], q_parts[:, 0, :], ALU.subtract).then_inc(s_part, 1)
                nc.vector.tensor_tensor(k_rest[:, :], kf[:, :], k_parts[:, 0, :], ALU.subtract).then_inc(s_part, 1)
                dve.wait_ge(s_hi, b * 6 + 4)
                nc.vector.tensor_tensor(q_parts[:, 2, :], q_rest[:, :], q_parts[:, 1, :], ALU.subtract)
                nc.vector.tensor_tensor(k_parts[:, 2, :], k_rest[:, :], k_parts[:, 1, :], ALU.subtract).then_inc(s_part, 1)
                dve.wait_ge(s_hi, b * 6 + 6)
                if not first:
                    dve.wait_ge(s_mst, b * (16 * BG))
                nc.vector.tensor_copy(m_parts[:, 0, :], m_neg[:, :]).then_inc(s_part, 1)
                part_wait(10)
                nc.vector.tensor_tensor(m_rest[:, :], m_neg[:, :], m_parts[:, 0, :], ALU.subtract).then_inc(s_part, 1)
                part_wait(11)
                nc.vector.tensor_copy(m_parts[:, 1, :], m_rest[:, :]).then_inc(s_part, 1)
                part_wait(12)
                nc.vector.tensor_tensor(m_rest[:, :], m_rest[:, :], m_parts[:, 1, :], ALU.subtract).then_inc(s_part, 1)
                part_wait(13)
                nc.vector.tensor_copy(m_parts[:, 2, :], m_rest[:, :]).then_inc(s_part, 1)

            turns(dve, B, batch)

        @block.scalar
        def _(act):
            act.wait_ge(s_gs, 1)
            act.wait_ge(s_par, 8 * 16)
            def batch(b, first):
                act.wait_ge(s_ln, b * LNS + 3)
                nc.scalar.activation(std[:, :], var_e[:, :], ACT.Sqrt).then_inc(s_std, 1)
                if not first:
                    act.wait_ge(s_v, b)
                for j in range(2):
                    act.wait_ge(s_tr, b * 2 + j + 1)
                    nc.scalar.activation(xT[:, j * 512:(j + 1) * 512], p_tr[:, j * 512:(j + 1) * 512],
                                         ACT.Identity).then_inc(s_xT, 1)
                act.wait_ge(s_q, b + 1)
                if not first:
                    act.wait_ge(s_part, b * PRT)
                nc.scalar.activation(qf[:, :], p_q[:, :], ACT.Identity, bias=bq_c[:, 0:1]).then_inc(s_qf, 1)
                act.wait_ge(s_k, b + 1)
                nc.scalar.activation(kf[:, :], p_k[:, :], ACT.Identity, bias=kb_c[:, 0:1]).then_inc(s_kf, 1)
                if not first:
                    act.wait_ge(s_qst, b * (16 * PARTS * BG))
                if not first:
                    act.wait_ge(s_kst, b * (16 * PARTS * BG))
                act.wait_ge(s_qf, b + 1)
                nc.scalar.activation(q_parts[:, 0, :], qf[:, :], ACT.Identity).then_inc(s_hi, 1)
                act.wait_ge(s_kf, b + 1)
                nc.scalar.activation(k_parts[:, 0, :], kf[:, :], ACT.Identity).then_inc(s_hi, 1)
                act.wait_ge(s_part, b * PRT + 7)
                nc.scalar.activation(q_parts[:, 1, :], q_rest[:, :], ACT.Identity).then_inc(s_hi, 1)
                act.wait_ge(s_part, b * PRT + 8)
                nc.scalar.activation(k_parts[:, 1, :], k_rest[:, :], ACT.Identity).then_inc(s_hi, 1)
                for j in range(2):
                    act.wait_ge(s_u, b * 2 + j + 1)
                    last = nc.scalar.activation(m_neg[:, j * 512:(j + 1) * 512], p_tr[0:H, j * 512:(j + 1) * 512],
                                                ACT.Identity, scale=-1.0)
                    last.then_inc(s_hi, 1)

            turns(act, B, batch)

        @block.tensor
        def _(pe):
            pe.wait_ge(s_par, 8 * 16)
            pe.wait_ge(s_pool, 8)
            def batch(b, first):
                pe.wait_ge(s_xh, b + 1)
                if not first:
                    pe.wait_ge(s_hi, b * 6)
                for t in range(NB):
                    last = nc.tensor.transpose(p_tr[:, t * 128:(t + 1) * 128], xh[:, t, :], ident[:, :])
                    if t % 4 == 3:
                        last.then_inc(s_tr, 1)
                pe.wait_ge(s_xT, b * 2 + 2)
                if not first:
                    pe.wait_ge(s_qf, b)
                for j in range(2):
                    last = nc.tensor.matmul(p_q[:, j * 512:(j + 1) * 512], wq_sb[:, :], xT[:, j * 512:(j + 1) * 512],
                                            start=True, stop=True)
                last.then_inc(s_q, 1)
                if not first:
                    pe.wait_ge(s_kf, b)
                for j in range(2):
                    last = nc.tensor.matmul(p_k[:, j * 512:(j + 1) * 512], wk_sb[:, :], xT[:, j * 512:(j + 1) * 512],
                                            start=True, stop=True)
                last.then_inc(s_k, 1)
                if not first:
                    pe.wait_ge(s_vst, b)
                for t in range(NB):
                    last = nc.tensor.matmul(p_v[:, t * 128:(t + 1) * 128], xT[:, t * 128:(t + 1) * 128], wv_sb[:, :],
                                            start=True, stop=True)
                last.then_inc(s_v, 1)
                pe.wait_ge(s_part, b * PRT + 6)
                for j in range(2):
                    c = slice(j * 512, (j + 1) * 512)
                    nc.tensor.matmul(p_tr[0:H, c], k_sel[:, 0, :], q_pos[:, c], start=True, stop=False)
                    nc.tensor.matmul(p_tr[0:H, c], k_sel[:, 1, :], q_neg[:, c], start=False, stop=True).then_inc(s_u, 1)

            turns(pe, B, batch)
    pone.close()
    one.close()

    two = ExitStack()
    q_sb = [sb(f"q_sb{p}", [KROWS, HG * S], BF16, two) for p in range(2)]
    k_sb = [sb(f"k_sb{p}", [KROWS, HG * S], BF16, two) for p in range(2)]
    v_sb = [sb(f"v_sb{p}", [128, NB, HG * 32], F32, two) for p in range(2)]
    bias = [sb(f"bias{p}", [128, BIASCOLS + 512], F32, two) for p in range(2)]
    probs = [sb(f"probs{p}", [128, HG, 1024], F32, two) for p in range(2)]
    o_raw = sb("o_raw", [128, S], F32, two)
    o_rcp = sb("o_rcp", [128, QB], F32, two)
    ptwo = ExitStack()
    p_s = [ps(f"p_s{p}", [128, 1024], ptwo) for p in range(2)]
    p_o = ps("p_o", [128, S], ptwo)
    p_b = [ps(f"p_b{p}", [128, 512], ptwo) for p in range(2)]

    t_alone = sem("t_alone")
    t_ones = sem("t_ones")
    t_q = [sem(f"t_q{p}") for p in range(2)]
    t_k = [sem(f"t_k{p}") for p in range(2)]
    t_v = [sem(f"t_v{p}") for p in range(2)]
    t_s = sem("t_s")
    t_add = sem("t_add")
    t_exp = sem("t_exp")
    t_pv = sem("t_pv")
    t_bmm = sem("t_bmm")
    t_bev = sem("t_bev")
    t_beva = sem("t_beva")
    t_far = sem("t_far")
    t_near = sem("t_near")
    t_oraw = sem("t_oraw")
    t_otr = sem("t_otr")
    t_rcp = sem("t_rcp")
    t_o = sem("t_o")
    ACT_CH = set(range(HALF, HALF + 4))
    NDVE = CHUNKS - len(ACT_CH)

    def dve_count(c):
        return sum(1 for k in range(c + 1) if k not in ACT_CH)

    def act_count(c):
        return sum(1 for k in range(c + 1) if k in ACT_CH)

    def tile_cols(g):
        col, got = 0, []
        for j in GROUPS[g]:
            got.append((j, col, NB - j))
            col += (NB - j) * BLK
        return got

    def pv_pieces(g):
        got = []
        for j, col, _ in tile_cols(g):
            i = j * BLK
            while i < S:
                end = min(S, (i // 512 + 1) * 512)
                got.append((j, col + i - j * BLK, i, end))
                i = end
        return got

    def bias_q(buf, kind, c):
        r = (c % HALF) * RCH
        return bias[buf][:, 0:BIASCOLS].rearrange("p (q k r) -> p k q r", k=KINDS, r=BLK)[:, kind, :, r:r + RCH]

    with nc.Block() as block:
        @block.sync
        def _(sp):
            def load_qk(u, p):
                sp.dma_start(q_sb[p][0:ROWS, :], ap(q_dram, u * UNIT_QK,
                             [[HG * S, PARTS * HD], [0, PARTS], [1, HG * S]])).then_inc(t_q[p], 16)
                sp.dma_start(q_sb[p][ROWS:ROWS + PARTS, :], ap(m_dram, u * (HG * PARTS * S),
                             [[HG * S, PARTS], [1, HG * S]])).then_inc(t_q[p], 16)
                sp.dma_start(k_sb[p][0:ROWS, :], ap(k_dram, u * UNIT_QK,
                             [[0, PARTS], [HG * S, PARTS * HD], [1, HG * S]])).then_inc(t_k[p], 16)

            def load_v(u, p):
                sp.dma_start(v_sb[p][:, :, :], ap(v_dram, u * (128 * NB * HG * 32),
                             [[NB * HG * 32, 128], [HG * 32, NB], [1, HG * 32]])).then_inc(t_v[p], 16)

            sp.wait_ge(t_ones, 4)
            for p in range(2):
                load_qk(p, p)
                load_v(p, p)
            with sp.Fori(0, UNITS // 2 - 1) as i:
                for p in range(2):
                    sp.wait_ge(t_s, i * (2 * STEPS) + (p + 1) * STEPS)
                    load_qk(i * 2 + p + 2, p)
                    sp.wait_ge(t_pv, i * (2 * NG) + (p + 1) * NG)
                    load_v(i * 2 + p + 2, p)

        @block.gpsimd
        def _(pool):
            for p in range(2):
                nc.gpsimd.memset(q_sb[p][64:KROWS, :], 0.0).then_inc(t_ones, 1)
                pool.wait_ge(t_ones, 2 * p + 1)
                nc.gpsimd.memset(k_sb[p][64:KROWS, :], 1.0).then_inc(t_ones, 1)
                pool.wait_ge(t_ones, 2 * p + 2)

            def masks(n, buf, c):
                r = c * RCH
                wait_alone(pool, t_bev, n[0], t_alone)
                nc.gpsimd.affine_select(out=bias_q(buf, 2, c), in_=bias_q(buf, 0, c), compare_op=ALU.is_ge, fill=0.0,
                                        base=-1 - r, pattern=[[0, QB], [-1, RCH]], channel_multiplier=1).then_inc(t_far, 1)
                wait_alone(pool, t_far, n[1], t_alone)
                nc.gpsimd.affine_select(out=bias_q(buf, 0, c), in_=bias_q(buf, 0, c), compare_op=ALU.is_ge, fill=MASKED,
                                        base=r, pattern=[[0, QB], [1, RCH]], channel_multiplier=-1).then_inc(t_near, 1)

            for c in range(HALF):
                masks((dve_count(c), c + 1), 0, c)
            with pool.Fori(0, UNITS // 2 - 1) as i:
                for p in range(2):
                    for c in range(HALF):
                        masks((i * (2 * NDVE) + (p + 1) * NDVE + dve_count(c), i * (2 * HALF) + (p + 1) * HALF + c + 1),
                              1 - p, c)
            for c in range(HALF):
                masks(((UNITS - 1) * NDVE + dve_count(c), (UNITS - 1) * HALF + c + 1), 1, c)

        @block.tensor
        def _(pe):
            def scores(T, p, s, first=False):
                g, h = divmod(s, HG)
                if not first:
                    pe.wait_ge(t_exp, T - 1)
                tile = p_s[s % 2]
                for j, col, n in tile_cols(g):
                    i, c = j * BLK, col
                    while i < S:
                        w = min(S - i, 512 - c % 512)
                        last = nc.tensor.matmul(tile[:, c:c + w], k_sb[p][:, h * S + j * BLK:h * S + (j + 1) * BLK],
                                                q_sb[p][:, h * S + i:h * S + i + w], start=True, stop=True)
                        i, c = i + w, c + w
                last.then_inc(t_s, 1)

            def relative(before, p, c, first=False):
                if not first:
                    pe.wait_ge(t_bev, before[0])
                    pe.wait_ge(t_beva, before[1])
                q = q_sb[p][:, :].rearrange("k (q r) -> k r q", r=BLK)
                bank = p_b[c % 2]
                for k in range(RCH):
                    r = (c % HALF) * RCH + k
                    w0 = P - 1 - r if c < HALF else BLK - 1 - r
                    last = nc.tensor.matmul(bank[:, k * QB:(k + 1) * QB], rel_w[:, w0:w0 + BLK], q[:, r, :],
                                            start=True, stop=True)
                last.then_inc(t_bmm, 1)

            def copies(u_dve, u_act, c):
                if c >= 2:
                    return u_dve + dve_count(c - 2), u_act + act_count(c - 2)
                k = CHUNKS - 2 + c
                return u_dve - NDVE + dve_count(k), u_act - len(ACT_CH) + act_count(k)

            def values(need_exp, p, g, piece):
                pieces = pv_pieces(g)
                if piece >= len(pieces):
                    return
                if piece == 0:
                    pe.wait_ge(t_exp, need_exp)
                j, c, i, end = pieces[piece]
                for h in range(HG):
                    last = nc.tensor.matmul(p_o[32 * h:32 * h + 32, i:end], v_sb[p][:, j, h * 32:(h + 1) * 32],
                                            probs[(p + g) % 2][:, h, c:c + end - i],
                                            start=(j == 0), stop=(j == (3 if end <= 512 else 4)))
                if piece == len(pieces) - 1:
                    last.then_inc(t_pv, 1)

            def unit(u, p, last_unit):
                T0 = u * STEPS
                for s in range(HG, STEPS):
                    g, h = divmod(s, HG)
                    scores(T0 + s, p, s)
                    if g == 1 and h == 1:
                        pe.wait_ge(t_v[p], loads(u, p))
                        if not is_first(u):
                            pe.wait_ge(t_o, u)
                    if h >= 1:
                        values(T0 + g * HG, p, g - 1, h - 1)
                    if not last_unit:
                        c = s - HG
                        if c == 0:
                            pe.wait_ge(t_q[1 - p], 2 * loads_next(u, p))
                        relative(copies((u + 1) * NDVE, (u + 1) * len(ACT_CH), c), 1 - p, c)
                if last_unit:
                    values(T0 + STEPS, p, NG - 1, 0)
                else:
                    pe.wait_ge(t_k[1 - p], loads_next(u, p))
                    for s in range(HG):
                        scores(T0 + STEPS + s, 1 - p, s)
                        if s == 1:
                            values(T0 + STEPS, p, NG - 1, 0)
                pe.wait_ge(t_oraw, u + 1)
                for n in range(NB):
                    last = nc.tensor.transpose(p_o[:, n * BLK:(n + 1) * BLK], o_raw[:, n * BLK:(n + 1) * BLK], ident[:, :])
                last.then_inc(t_otr, 1)

            turn = [None]

            def loads(u, p):
                return turn[0] * 16 + 16

            def loads_next(u, p):
                return turn[0] * 16 + 16 + 16 * p

            pe.wait_ge(t_q[0], 32)
            for c in range(CHUNKS):
                relative(copies(0, 0, c) if c >= 2 else None, 0, c, first=c < 2)
            pe.wait_ge(t_k[0], 16)
            for s in range(HG):
                scores(s, 0, s, first=s < 2)
            turn[0] = 0
            unit(0, 0, False)
            unit(1, 1, False)
            with pe.Fori(1, UNITS // 2 - 1) as i:
                turn[0] = i
                for p in range(2):
                    unit(i * 2 + p, p, False)
            turn[0] = UNITS // 2 - 1
            unit(UNITS - 2, 0, False)
            unit(UNITS - 1, 1, True)

        @block.vector
        def _(dve):
            def add(T, p, s):
                g, h = divmod(s, HG)
                dve.wait_ge(t_s, T + 1)
                for j, col, n in tile_cols(g):
                    nb = min(KINDS, n)
                    start = h * (NB * KINDS * BLK) + j * (KINDS * BLK)
                    term = bias[p][:, start:start + nb * 512].rearrange("p (k x) -> p k x", x=512)[:, :, 0:BLK]
                    cols = p_s[s % 2][:, col:col + nb * BLK].rearrange("p (k x) -> p k x", x=BLK)
                    last = nc.vector.tensor_tensor(cols, cols, term, ALU.add)
                last.then_inc(t_add, 1)

            def copy_bank(n, buf, c):
                dve.wait_ge(t_bmm, n)
                nc.vector.tensor_copy(bias_q(buf, 0 if c < HALF else 1, c),
                                      p_b[c % 2][:, :].rearrange("p (r q) -> p q r", q=QB)).then_inc(t_bev, 1)

            def ready(u):
                dve.wait_ge(t_near, u * HALF + HALF)
                dve.wait_ge(t_bev, u * NDVE + NDVE)
                dve.wait_ge(t_beva, u * len(ACT_CH) + len(ACT_CH))

            def unit(u, p, last_unit):
                for s in range(HG, STEPS):
                    add(u * STEPS + s, p, s)
                    c = s - HG
                    if not last_unit and c not in ACT_CH:
                        copy_bank((u + 1) * CHUNKS + c + 1, 1 - p, c)
                if not last_unit:
                    ready(u + 1)
                    for s in range(HG):
                        add((u + 1) * STEPS + s, 1 - p, s)
                dve.wait_ge(t_otr, u + 1)
                o_t = p_o[:, :].rearrange("p (q d) -> p q d", d=32)
                nc.vector.reciprocal(o_rcp[:, :], o_t[:, :, HD]).then_inc(t_rcp, 1)
                dve.wait_ge(t_rcp, u + 1)
                dst = o_all[:, bass.ds(u * (QB * HD), QB * HD)]
                nc.vector.tensor_tensor(dst.rearrange("p (q d) -> p q d", d=HD), o_t[:, :, 0:HD],
                                        o_rcp[:, :].unsqueeze(2).broadcast_to([128, QB, HD]), ALU.mult).then_inc(t_o, 1)

            for c in range(CHUNKS):
                if c not in ACT_CH:
                    copy_bank(c + 1, 0, c)
            ready(0)
            for s in range(HG):
                add(s, 0, s)
            unit(0, 0, False)
            unit(1, 1, False)
            with dve.Fori(1, UNITS // 2 - 1) as i:
                for p in range(2):
                    unit(i * 2 + p, p, False)
            unit(UNITS - 2, 0, False)
            unit(UNITS - 1, 1, True)

        @block.scalar
        def _(act):
            def exps(u, p, s):
                g, h = divmod(s, HG)
                act.wait_ge(t_add, u * STEPS + s + 1)
                width = sum(n for _, _, n in tile_cols(g)) * BLK
                nc.scalar.activation(probs[(p + g) % 2][:, h, 0:width], p_s[s % 2][:, 0:width], ACT.Exp,
                                     scale=SCALE).then_inc(t_exp, 1)

            def copy_bank(n, buf, c):
                act.wait_ge(t_bmm, n)
                nc.scalar.activation(bias_q(buf, 1, c), p_b[c % 2][:, :].rearrange("p (r q) -> p q r", q=QB),
                                     ACT.Copy).then_inc(t_beva, 1)

            def unit(u, p, last_unit):
                for s in range(HG, STEPS):
                    g, h = divmod(s, HG)
                    if h == 0 and not (is_first(u) and g == 1):
                        act.wait_ge(t_pv, u * NG + g - 1)
                    exps(u, p, s)
                    c = s - HG
                    if not last_unit and c in ACT_CH:
                        copy_bank((u + 1) * CHUNKS + c + 1, 1 - p, c)
                if not last_unit:
                    act.wait_ge(t_pv, u * NG + NG - 1)
                    exps(u + 1, 1 - p, 0)
                    exps(u + 1, 1 - p, 1)
                act.wait_ge(t_pv, u * NG + NG)
                if not is_first(u):
                    act.wait_ge(t_otr, u)
                nc.scalar.activation(o_raw[:, :], p_o[:, :], ACT.Copy).then_inc(t_oraw, 1)
                if not last_unit:
                    exps(u + 1, 1 - p, 2)
                    exps(u + 1, 1 - p, 3)

            for c in sorted(ACT_CH):
                copy_bank(c + 1, 0, c)
            for s in range(HG):
                exps(0, 0, s)
            unit(0, 0, False)
            unit(1, 1, False)
            with act.Fori(1, UNITS // 2 - 1) as i:
                for p in range(2):
                    unit(i * 2 + p, p, False)
            unit(UNITS - 2, 0, False)
            unit(UNITS - 1, 1, True)
    ptwo.close()
    two.close()

    stage3(nc, ctx, sb, ps, sem, ident, o_all, x, Wo, bo, w1, s1, w2, s2, h1, sh1, h2, sh2, w3, s3, out)


def stage3(nc, ctx, sb, ps, sem, ident, o_all, x, Wo, bo, w1, s1, w2, s2, h1, sh1, h2, sh2, w3, s3, out):
    wo_sb = sb("wo_sb", [128, 128])
    bo_b = sb("bo_b", [128, NC * NT, 128])
    s1_c, s2_c, sh1_c, sh2_c = (sb(n, [128, HC]) for n in ("s1_c", "s2_c", "sh1_c", "sh2_c"))
    s3_c = sb("s3_c", [128, 1])
    WEIGHTS = [("w1", w1, HC, E), ("w2", w2, HC, E), ("h1", h1, HC, HID), ("h2", h2, HC, HID), ("w3", w3, 1, HID)]
    whi = [sb(f"{n}_hi", [128, cols // 128, rows * 128], F32R) for n, _, rows, cols in WEIGHTS]
    wlo = [sb(f"{n}_lo", [128, cols // 128, rows * 128], F32R) for n, _, rows, cols in WEIGHTS]
    x1_all = sb("x1_all", [128, TOK])
    x1T_hi = sb("x1T_hi", [128, S], F32R)
    x1T_lo = sb("x1T_lo", [128, S], F32R)
    act_f = [sb(f"act_f{k}", [128, HC, FC]) for k in range(NC)]
    xres = sb("xres", [128, NB, 128])
    o_cur = sb("o_cur", [128, NB, 128])
    oT = sb("oT", [128, S])
    y = sb("y", [128, NB, 128])
    zT = sb("zT", [128, S])
    res = sb("res", [128, NB, 128])
    st3, st4 = (sb(n, [128, NB, 6]) for n in ("st3", "st4"))
    mv3, mv4 = (sb(n, [128, NB, 2]) for n in ("mv3", "mv4"))
    ve3, sd3, rs3, nm3, ve4, sd4, rs4 = (sb(n, [128, NB]) for n in ("ve3", "sd3", "rs3", "nm3", "ve4", "sd4", "rs4"))
    nat = ExitStack()
    wnat = [sb(f"{n}_nat", [128, rows, cols], F32, nat) for n, _, rows, cols in WEIGHTS]
    nat.close()
    hid_hi = [[sb(f"hid{k}_{l}_hi", [128, HC, FC], F32R) for l in range(2)] for k in range(NC)]
    hid_lo = [[sb(f"hid{k}_{l}_lo", [128, HC, FC], F32R) for l in range(2)] for k in range(NC)]
    p_z = [ps(f"p_z{k}", [128, FC]) for k in range(NZ)]
    p_pre = [ps(f"p_pre{k}", [128, FC]) for k in range(NC)]
    p_post = [ps(f"p_post{k}", [128, FC]) for k in range(NC)]

    a_alone = sem("a_alone")
    a_small = sem("a_small")
    a_wl = [sem(f"a_wl{n}") for n in range(len(WEIGHTS))]
    a_w = sem("a_w")
    a_whi, a_wlo = sem("a_whi"), sem("a_wlo")
    r_x = sem("r_x")
    r_oc = sem("r_oc")
    r_otr, r_oT = sem("r_otr"), sem("r_oT")
    r_y = sem("r_y")
    r_dv = sem("r_dv")
    r_sd = sem("r_sd")
    r_xtr, r_hi, r_lo = sem("r_xtr"), sem("r_hi"), sem("r_lo")
    f_z = sem("f_z")
    f_act = sem("f_act")
    f_mul = sem("f_mul")
    f_hi, f_lo = sem("f_hi"), sem("f_lo")
    w_zT, w_tr, w_dv, w_sd, w_out = sem("w_zT"), sem("w_tr"), sem("w_dv"), sem("w_sd"), sem("w_out")
    PRE, POST = 15, 6
    ACTS = 3 * HC * NC
    ZT = NC * (2 * HC + 2 * HC + 1)

    TILES = [(0, k, w, o) for k in range(NC) for o in range(HC) for w in range(2)]
    TILES += [(l, k, l + 1, o) for l in (1, 2) for k in range(NC) for o in range(HC)]
    TILES += [(3, k, 4, 0) for k in range(NC)]
    assert len(TILES) == ZT

    def split_of(l, k, o):
        return (l * NC + k) * HC + o

    def reader(idx):
        l, k, w, o = TILES[idx]
        if l == 3:
            return w_zT, NC, k
        if l == 0 and w == 1:
            return f_mul, NC * HC, k * HC + o
        return f_act, ACTS, split_of(l, k, o)

    wbanks = [(w, k, rows) for w, (_, _, rows, cols) in enumerate(WEIGHTS) for k in range(cols // 128)]

    with nc.Block() as block:
        @block.sync
        def _(sp):
            def weight(n):
                sp.dma_start(wnat[n][:, :, :], WEIGHTS[n][1].rearrange("(r p) c -> p r c", p=128)).then_inc(a_wl[n], 16)

            weight(0)
            weight(1)
            for dst, src in [(wo_sb[:, :], Wo), (bo_b[:, :, :], ap(bo.tensor, 0, [[0, 128], [0, NB], [1, 128]])),
                             (s3_c[:, :], s3.rearrange("(p a) -> p a", a=1))] + \
                    [(d[:, :], ap(v.tensor, 0, [[1, 128], [128, HC]]))
                     for d, v in ((s1_c, s1), (s2_c, s2), (sh1_c, sh1), (sh2_c, sh2))]:
                sp.dma_start(dst, src).then_inc(a_small, 16)

            def tokens(n):
                sp.dma_start(xres[:, :, :], ap(x.tensor, n * (S * E), [[E, 128], [128 * E, NB], [1, E]])).then_inc(r_x, 16)

            def store(n):
                sp.wait_ge(w_dv, n * POST + POST)
                sp.dma_start(ap(out.tensor, n * (S * E), [[E, 128], [128 * E, NB], [1, E]]),
                             res[:, :, :]).then_inc(w_out, 16)

            tokens(0)
            for n in range(2, len(WEIGHTS)):
                weight(n)
            sp.wait_ge(r_dv, 9)
            tokens(1)

            def turn(n):
                sp.wait_ge(r_dv, n * PRE + 9)
                tokens(n + 1)
                store(n - 1)

            with sp.Fori(1, B - 1) as n:
                turn(n)
            store(B - 2)
            store(B - 1)
            sp.wait_ge(w_out, 16 * B)

        @block.gpsimd
        def _(pool):
            def gather(n, first):
                if not first:
                    pool.wait_ge(r_otr, n * NC)
                src = o_all[:, bass.ds(n * (NB * 128), NB * 128)].rearrange("p (g n d) -> p n g d", g=BG, n=NB)
                nc.gpsimd.tensor_copy(o_cur[:, :, :].rearrange("p n (g d) -> p n g d", g=BG), src).then_inc(r_oc, 1)

            turns(pool, B, gather)

        @block.tensor
        def _(pe):
            def weight_bank(i):
                w, k, rows = wbanks[i]
                if k == 0:
                    pe.wait_ge(a_wl[w], 16)
                if i >= NZ:
                    pe.wait_ge(a_whi, i - NZ + 1)
                    pe.wait_ge(a_wlo, i - NZ + 1)
                for r in range(rows):
                    last = nc.tensor.transpose(p_z[i % NZ][:, r * 128:(r + 1) * 128],
                                               wnat[w][:, r, k * 128:(k + 1) * 128], ident[:, :])
                last.then_inc(a_w, 1)

            def transposes(dst, src, t0):
                for t in range(NT):
                    last = nc.tensor.transpose(dst[:, t * 128:(t + 1) * 128], src(t0 + t), ident[:, :])
                return last

            def pre_outputs(n, first):
                pe.wait_ge(r_oc, n + 1)
                if not first:
                    pe.wait_ge(r_lo, n * NC)
                for k in range(NC):
                    transposes(p_pre[k], lambda t: o_cur[:, t, :], k * NT).then_inc(r_otr, 1)

            def pre_project(n):
                for k in range(NC):
                    pe.wait_ge(r_oT, n * NC + k + 1)
                    for t in range(NT):
                        c = (k * NT + t) * 128
                        last = nc.tensor.matmul(p_pre[k][:, t * 128:(t + 1) * 128], oT[:, c:c + 128], wo_sb[:, :],
                                                start=True, stop=True)
                    last.then_inc(r_y, 1)

            def pre_hidden(n):
                pe.wait_ge(r_dv, n * PRE + PRE)
                for k in range(NC):
                    transposes(p_pre[k], lambda t: y[:, t, :], k * NT).then_inc(r_xtr, 1)

            def post_transpose(n, first):
                for k in range(NC):
                    pe.wait_ge(w_zT, n * NC + k + 1)
                    if k == 0 and not first:
                        pe.wait_ge(w_dv, n * POST)
                    transposes(p_post[k], lambda t: zT[:, t * 128:(t + 1) * 128], k * NT).then_inc(w_tr, 1)

            def layer(n, l, k, first):
                if l == 0:
                    if k == 0:
                        pe.wait_ge(r_lo, n * NC + NC)
                    hi, lo = [x1T_hi[:, k * FC:(k + 1) * FC]], [x1T_lo[:, k * FC:(k + 1) * FC]]
                else:
                    pe.wait_ge(f_lo, n * ACTS + split_of(l - 1, k, HC - 1) + 1)
                    hi, lo = ([t[k][(l + 1) % 2][:, j, :] for j in range(HC)] for t in (hid_hi, hid_lo))
                for idx, (tl, tk, w, o) in enumerate(TILES):
                    if (tl, tk) != (l, k):
                        continue
                    if idx >= NZ:
                        s, per, place = reader(idx - NZ)
                        pe.wait_ge(s, n * per + place + 1)
                    elif not first:
                        s, per, place = reader(max(i for i in range(ZT) if i % NZ == idx))
                        pe.wait_ge(s, n * per + place + 1 - per)
                    bank = p_z[idx % NZ]
                    cols = slice(o * 128, (o + 1) * 128)
                    for j in range(len(hi)):
                        nc.tensor.matmul(bank[:, :], whi[w][:, j, cols], hi[j], start=(j == 0), stop=False)
                        nc.tensor.matmul(bank[:, :], whi[w][:, j, cols], lo[j], start=False, stop=False)
                        last = nc.tensor.matmul(bank[:, :], wlo[w][:, j, cols], hi[j], start=False,
                                                stop=(j == len(hi) - 1))
                    last.then_inc(f_z, 1)

            pe.wait_ge(a_small, 7 * 16)
            weight_bank(0)
            weight_bank(1)
            pre_outputs(0, True)
            pre_project(0)
            for i in range(2, len(wbanks)):
                weight_bank(i)
            pe.wait_ge(a_wlo, len(wbanks))
            pre_hidden(0)

            def turn(n, first, last):
                if not last:
                    pre_outputs(n + 1, False)
                layer(n, 0, 0, first)
                if not first:
                    post_transpose(n - 1, isinstance(n, int) and n == 1)
                if not last:
                    pre_project(n + 1)
                layer(n, 0, 1, first)
                for l in (1, 2):
                    for k in range(NC):
                        layer(n, l, k, first)
                if not last:
                    pre_hidden(n + 1)
                for k in range(NC):
                    layer(n, 3, k, first)

            turn(0, True, False)
            turn(1, False, False)
            with pe.Fori(2, B - 1) as n:
                turn(n, False, False)
            turn(B - 1, False, True)
            post_transpose(B - 1, False)

        @block.scalar
        def _(act):
            def weight_bank(i):
                w, k, rows = wbanks[i]
                act.wait_ge(a_w, i + 1)
                nc.scalar.activation(whi[w][:, k, :], p_z[i % NZ][:, 0:rows * 128], ACT.Copy).then_inc(a_whi, 1)

            def pre_oT(n, first):
                if not first:
                    act.wait_ge(r_y, n * NC)
                for k in range(NC):
                    act.wait_ge(r_otr, n * NC + k + 1)
                    nc.scalar.activation(oT[:, k * FC:(k + 1) * FC], p_pre[k][:, :], ACT.Copy).then_inc(r_oT, 1)

            def pre_root(n, which):
                act.wait_ge(r_dv, n * PRE + (5, 12)[which])
                nc.scalar.activation(sd3[:, :], ve3[:, :], ACT.Sqrt).then_inc(r_sd, 1)

            def pre_hi(n, first):
                if not first:
                    act.wait_ge(f_z, (n - 1) * ZT + 2 * HC * NC)
                for k in range(NC):
                    act.wait_ge(r_xtr, n * NC + k + 1)
                    nc.scalar.activation(x1T_hi[:, k * FC:(k + 1) * FC], p_pre[k][:, :], ACT.Copy).then_inc(r_hi, 1)

            def activations(n, l, k, first):
                fn, sc = ((ACT.Silu, s1_c), (ACT.Gelu, sh1_c), (ACT.Gelu, sh2_c))[l]
                if l == 0 and not first:
                    act.wait_ge(f_lo, n * ACTS + split_of(2, k, HC - 1) + 1 - ACTS)
                for idx, (tl, tk, w, o) in enumerate(TILES):
                    if (tl, tk) == (l, k) and not (l == 0 and w == 1):
                        act.wait_ge(f_z, n * ZT + idx + 1)
                        nc.scalar.activation(act_f[k][:, o, :], p_z[idx % NZ][:, :], fn,
                                             scale=sc[:, o:o + 1]).then_inc(f_act, 1)

            def outputs(n, first):
                if not first:
                    act.wait_ge(w_tr, n * NC)
                for k in range(NC):
                    idx = ZT - NC + k
                    act.wait_ge(f_z, n * ZT + idx + 1)
                    nc.scalar.activation(zT[:, k * FC:(k + 1) * FC], p_z[idx % NZ][:, :], ACT.Copy,
                                         scale=s3_c[:, 0:1]).then_inc(w_zT, 1)

            def post_root(n):
                act.wait_ge(w_dv, n * POST + 3)
                nc.scalar.activation(sd4[:, :], ve4[:, :], ACT.Sqrt).then_inc(w_sd, 1)

            act.wait_ge(a_small, 7 * 16)
            weight_bank(0)
            weight_bank(1)
            pre_oT(0, True)
            pre_root(0, 0)
            for i in range(2, 6):
                weight_bank(i)
            pre_root(0, 1)
            for i in range(6, len(wbanks)):
                weight_bank(i)
            pre_hi(0, True)

            def turn(n, first, last):
                activations(n, 0, 0, first)
                if not last:
                    pre_oT(n + 1, False)
                activations(n, 0, 1, first)
                if not last:
                    pre_root(n + 1, 0)
                if not first:
                    post_root(n - 1)
                activations(n, 1, 0, first)
                activations(n, 1, 1, first)
                if not last:
                    pre_root(n + 1, 1)
                activations(n, 2, 0, first)
                activations(n, 2, 1, first)
                if not last:
                    pre_hi(n + 1, False)
                outputs(n, first)

            turn(0, True, False)
            with act.Fori(1, B - 1) as n:
                turn(n, False, False)
            turn(B - 1, False, True)
            post_root(B - 1)

        @block.vector
        def _(dve):
            def weight_bank(i):
                w, k, rows = wbanks[i]
                dve.wait_ge(a_whi, i + 1)
                nc.vector.tensor_tensor(wlo[w][:, k, :], p_z[i % NZ][:, 0:rows * 128],
                                        whi[w][:, k, :].bitcast(F32), ALU.subtract).then_inc(a_wlo, 1)

            def statistics(st, mv, ve, src, chain, base, k):
                for t in range(NB):
                    last = nc.vector.bn_stats(st[:, t, :], src(t))
                last.then_inc(chain, 1)
                wait_alone(dve, chain, base + k, a_alone)
                for t in range(NB):
                    last = nc.vector.bn_aggr(mv[:, t, :], st[:, t, :])
                last.then_inc(chain, 1)
                dve.wait_ge(chain, base + k + 1)
                nc.vector.tensor_scalar(ve[:, :], mv[:, :, 1], EPS, None, ALU.add).then_inc(chain, 1)

            def pre_step(ins, n, k):
                ins.then_inc(r_dv, 1)
                dve.wait_ge(r_dv, n * PRE + k)

            def scale_shift(n, k):
                pre_step(nc.vector.reciprocal(rs3[:, :], sd3[:, :]), n, k)
                pre_step(nc.vector.scalar_tensor_tensor(out=nm3[:, :], in0=mv3[:, :, 0], scalar=-1.0, in1=rs3[:, :],
                                                        op0=ALU.mult, op1=ALU.mult), n, k + 1)

            def x1_rows(n):
                return x1_all[:, bass.ds(n * S, S)].rearrange("p (t e) -> p t e", e=E)

            def pre_y(n, first):
                if not first:
                    dve.wait_ge(r_xtr, n * NC)
                for k in range(NC):
                    dve.wait_ge(r_y, n * NC + k + 1)
                    nc.vector.tensor_tensor(y[:, k * NT:(k + 1) * NT, :], p_pre[k][:, :].rearrange("p (t e) -> p t e", e=E),
                                            bo_b[:, k * NT:(k + 1) * NT, :], ALU.add).then_inc(r_dv, 1)
                dve.wait_ge(r_dv, n * PRE + 2)
                statistics(st3, mv3, ve3, lambda t: y[:, t, :], r_dv, n * PRE, 3)

            def pre_x1(n):
                dve.wait_ge(r_sd, n * 2 + 1)
                scale_shift(n, 6)
                for t in range(NB):
                    last = nc.vector.tensor_scalar(y[:, t, :], y[:, t, :], rs3[:, t:t + 1], nm3[:, t:t + 1],
                                                   ALU.mult, ALU.add)
                pre_step(last, n, 8)
                dve.wait_ge(r_x, n * 16 + 16)
                pre_step(nc.vector.tensor_tensor(x1_rows(n), y[:, :, :], xres[:, :, :], ALU.add), n, 9)
                statistics(st3, mv3, ve3, lambda t: x1_all[:, bass.ds(n * S + t * E, E)], r_dv, n * PRE, 10)

            def pre_xh(n):
                dve.wait_ge(r_sd, n * 2 + 2)
                scale_shift(n, 13)
                for t in range(NB):
                    last = nc.vector.tensor_scalar(y[:, t, :], x1_all[:, bass.ds(n * S + t * E, E)], rs3[:, t:t + 1],
                                                   nm3[:, t:t + 1], ALU.mult, ALU.add)
                last.then_inc(r_dv, 1)

            def pre_lo(n):
                for k in range(NC):
                    c = slice(k * FC, (k + 1) * FC)
                    dve.wait_ge(r_hi, n * NC + k + 1)
                    nc.vector.tensor_tensor(x1T_lo[:, c], p_pre[k][:, :], x1T_hi[:, c].bitcast(F32),
                                            ALU.subtract).then_inc(r_lo, 1)

            def post_statistics(n):
                for k in range(NC):
                    dve.wait_ge(w_tr, n * NC + k + 1)
                statistics(st4, mv4, ve4, lambda t: p_post[t // NT][:, (t % NT) * 128:(t % NT + 1) * 128],
                           w_dv, n * POST, 1)

            def post_out(n, first):
                dve.wait_ge(w_sd, n + 1)
                nc.vector.reciprocal(rs4[:, :], sd4[:, :]).then_inc(w_dv, 1)
                dve.wait_ge(w_dv, n * POST + 4)
                if not first:
                    dve.wait_ge(w_out, n * 16)
                for t in range(NB):
                    last = nc.vector.tensor_scalar(res[:, t, :], p_post[t // NT][:, (t % NT) * 128:(t % NT + 1) * 128],
                                                   mv4[:, t, 0:1], rs4[:, t:t + 1], ALU.subtract, ALU.mult)
                last.then_inc(w_dv, 1)
                dve.wait_ge(w_dv, n * POST + 5)
                nc.vector.tensor_tensor(res[:, :, :], res[:, :, :], x1_rows(n), ALU.add).then_inc(w_dv, 1)

            def split(n, l, k, o):
                src, place = act_f[k][:, o, :], split_of(l, k, o)
                nc.vector.tensor_copy(hid_hi[k][l % 2][:, o, :], src).then_inc(f_hi, 1)
                dve.wait_ge(f_hi, n * ACTS + place + 1)
                nc.vector.tensor_tensor(hid_lo[k][l % 2][:, o, :], src, hid_hi[k][l % 2][:, o, :].bitcast(F32),
                                        ALU.subtract).then_inc(f_lo, 1)

            def gated(n, k):
                for o in range(HC):
                    idx = TILES.index((0, k, 1, o))
                    dve.wait_ge(f_z, n * ZT + idx + 1)
                    dve.wait_ge(f_act, n * ACTS + split_of(0, k, o) + 1)
                    nc.vector.scalar_tensor_tensor(out=act_f[k][:, o, :], in0=p_z[idx % NZ][:, :],
                                                   scalar=s2_c[:, o:o + 1], in1=act_f[k][:, o, :],
                                                   op0=ALU.mult, op1=ALU.mult).then_inc(f_mul, 1)
                    dve.wait_ge(f_mul, n * (NC * HC) + k * HC + o + 1)
                    split(n, 0, k, o)

            def splits(n, l, k):
                for o in range(HC):
                    dve.wait_ge(f_act, n * ACTS + split_of(l, k, o) + 1)
                    split(n, l, k, o)

            dve.wait_ge(a_small, 7 * 16)
            weight_bank(0)
            weight_bank(1)
            pre_y(0, True)
            pre_x1(0)
            for i in range(2, 6):
                weight_bank(i)
            pre_xh(0)
            for i in range(6, len(wbanks)):
                weight_bank(i)
            pre_lo(0)

            def turn(n, first, last):
                gated(n, 0)
                if not last:
                    pre_y(n + 1, False)
                gated(n, 1)
                if not first:
                    post_statistics(n - 1)
                splits(n, 1, 0)
                if not last:
                    pre_x1(n + 1)
                if not first:
                    post_out(n - 1, isinstance(n, int) and n == 1)
                splits(n, 1, 1)
                splits(n, 2, 0)
                if not last:
                    pre_xh(n + 1)
                splits(n, 2, 1)
                if not last:
                    pre_lo(n + 1)

            turn(0, True, False)
            turn(1, False, False)
            with dve.Fori(2, B - 1) as n:
                turn(n, False, False)
            turn(B - 1, False, True)
            post_statistics(B - 1)
            post_out(B - 1, False)


_INS = ['L0_attn_x', 'L0_attn_Wq', 'L0_attn_bq', 'L0_attn_Wk', 'L0_attn_bk', 'L0_attn_Wv', 'L0_attn_bv', 'L0_attn_Wo',
        'L0_attn_bo', 'L0_attn_rel_key', 'L0_ffn_w1_w', 'L0_ffn_w1_s', 'L0_ffn_w2_w', 'L0_ffn_w2_s', 'L0_ffn_h1_w',
        'L0_ffn_h1_s', 'L0_ffn_h2_w', 'L0_ffn_h2_s', 'L0_ffn_w3_w', 'L0_ffn_w3_s']


def kernel(**inputs):
    import numpy as _np
    import concourse.bacc as _bacc
    from concourse import mybir as _mybir
    from concourse.bass_utils import run_bass_kernel_spmd as _run

    nc = _bacc.Bacc("TRN2", target_bir_lowering=False, num_devices=1)
    arrays, args = {}, []
    for name in _INS:
        a = _np.ascontiguousarray(inputs[name])
        arrays[f"in_{name}_dram"] = a
        args.append(nc.dram_tensor(f"in_{name}_dram", a.shape, _mybir.dt.from_np(a.dtype), kind="ExternalInput").ap())
    args.append(nc.dram_tensor("out_dram", (B, S, E), _mybir.dt.float32, kind="ExternalOutput").ap())
    attention_ffn(nc, *args)
    r = _run(nc, [arrays], core_ids=[0])
    return r.results[0]["out_dram"]
```

```python
import concourse.bass as bass
from concourse import mybir
from contextlib import ExitStack


F32 = mybir.dt.float32
F32R = mybir.dt.float32r
BF16 = mybir.dt.bfloat16
ALU = mybir.AluOpType
ACT = mybir.ActivationFunctionType
AX = mybir.AxisListType

B, S, E = 4, 1024, 128
HD, H = 8, 16
P = 256
HID = 512
TOK = B * S
BLK = 128
NB = S // BLK
HG = 4
UNITS = B * H // HG
PARTS = 3
ROWS = PARTS * PARTS * HD
KROWS = 96
EPS = 1e-5
SCALE = float(HD) ** -0.5
LIMIT = 60.0 / SCALE
GAP = 32
MASKED = -1.0e30
GROUPS = [[(0, 0, 4)], [(0, 4, 4)], [(1, 1, 3), (7, 7, 1)], [(1, 4, 4)], [(2, 2, 2), (6, 6, 2)], [(2, 4, 4)],
          [(5, 5, 3), (3, 3, 1)], [(3, 4, 4)], [(4, 4, 4)]]
ORDER = [(g + k, h) for g in (0, 2, 4, 6) for h in range(HG) for k in range(2)] + [(8, h) for h in range(HG)]
PRODUCTS = [(10, 0, 0), (12, 1, 0), (18, 2, 0), (19, 2, 1), (20, 3, 0), (26, 4, 0), (27, 4, 1), (28, 5, 0), (34, 6, 0),
            (34, 6, 1), (35, 7, 0), (38, 8, 0)]
BUFFER = [0, 1, 2, 3, 0, 2, 1, 3, 2]
FINAL = [(3, 3, 1), (4, 4, 4)]
TCOLS = 4 * BLK
SLOTS = 4
PBUFS = 4
NG = len(GROUPS)
STEPS = NG * HG
RCH = 16
CHUNKS = 2 * BLK // RCH
HALF = CHUNKS // 2
MBANKS = 4
MASKS = HALF // MBANKS
QB = HG * NB
BG = H // HG
DROW = B * H * S
DVROW = B * H * 32
KINDS = 3
BIASCOLS = QB * KINDS * BLK
FC = 512
NC = S // FC
NT = FC // 128
NZ = 4
HC = HID // 128


def is_first(u):
    return isinstance(u, int) and u == 0


def ap(handle, offset, dims):
    return bass.AP(handle, offset, dims)


def wait_alone(eng, sem, value, passed):
    eng.wait_ge(sem, value)
    eng.sem_inc(passed, 1)


def turns(eng, n, body):
    body(0, True)
    with eng.Fori(1, n) as i:
        body(i, False)


def attention_ffn(nc, x, Wq, bq, Wk, bk, Wv, bv, Wo, bo, rel, w1, s1, w2, s2, h1, sh1, h2, sh2, w3, s3, out):
    with ExitStack() as ctx:
        ctx.enter_context(nc.allow_non_contiguous_dma(reason="small parameters"))
        build(nc, ctx, x, Wq, bq, Wk, bk, Wv, bv, Wo, bo, rel, w1, s1, w2, s2, h1, sh1, h2, sh2, w3, s3, out)


def build(nc, ctx, x, Wq, bq, Wk, bk, Wv, bv, Wo, bo, rel, w1, s1, w2, s2, h1, sh1, h2, sh2, w3, s3, out):
    def sb(name, shape, dt=F32, where=ctx):
        return where.enter_context(nc.sbuf_tensor(name, shape, dt))

    def ps(name, shape, where=ctx):
        return where.enter_context(nc.psum_tensor(name, shape, F32))

    def sem(name):
        return ctx.enter_context(nc.semaphore(name))

    q_dram = nc.dram_tensor("q_dram", [PARTS, HD, B * H, S], BF16, kind="Internal")
    k_dram = nc.dram_tensor("k_dram", [HD, PARTS, B * H, S], BF16, kind="Internal")
    m_dram = nc.dram_tensor("m_dram", [PARTS, B * H, S], BF16, kind="Internal")
    v_dram = nc.dram_tensor("v_dram", [128, NB, B * H, 32], F32, kind="Internal")
    g_dram = nc.dram_tensor("g_dram", [HD, PARTS, P], BF16, kind="Internal")
    gx_dram = nc.dram_tensor("gx_dram", [HD, 3], F32, kind="Internal")
    r_dram = nc.dram_tensor("r_dram", [NB, BLK, 4 * BLK], F32, kind="Internal")

    ident = sb("ident", [128, 128])
    rel_w = sb("rel_w", [KROWS, P + BLK], BF16)
    o_all = sb("o_all", [128, UNITS * NB * 32])
    wo_sb = sb("wo_sb", [128, 128])
    bo_b = sb("bo_b", [128, NB, 128])
    s1_c, s2_c, sh1_c, sh2_c = (sb(n, [128, HC]) for n in ("s1_c", "s2_c", "sh1_c", "sh2_c"))
    s3_c = sb("s3_c", [128, 1])
    WEIGHTS = [("w1", w1, HC, E), ("w2", w2, HC, E), ("h1", h1, HC, HID), ("h2", h2, HC, HID), ("w3", w3, 1, HID)]
    EARLY = (0, 1, 4)
    wnat = [sb(f"{n}_nat", [128, rows, cols]) if w in EARLY else None for w, (n, _, rows, cols) in enumerate(WEIGHTS)]
    a_small = sem("a_small")
    a_wl = [sem(f"a_wl{n}") for n in range(len(WEIGHTS))]

    def load_weight(n):
        nc.sync.dma_start(wnat[n][:, :, :], WEIGHTS[n][1].rearrange("(r p) c -> p r c", p=128)).then_inc(a_wl[n], 16)

    far_flag = sb("far_flag", [1, 1], mybir.dt.int32)
    operands = ExitStack()
    q_sb = [sb(f"q_sb{p}", [KROWS, HG * S], BF16, operands) for p in range(2)]
    k_sb = [sb(f"k_sb{p}", [KROWS, HG * S], BF16, operands) for p in range(2)]
    v_sb = [sb(f"v_sb{p}", [128, NB, HG * 32], F32, operands) for p in range(2)]

    one = ExitStack()
    wq_sb, wk_sb, wv_sb = (sb(n, [128, 128], F32, one) for n in ("wq_sb", "wk_sb", "wv_sb"))
    bq_c, bk_c, r0_c, kb_c = (sb(n, [128, 1], F32, one) for n in ("bq_c", "bk_c", "r0_c", "kb_c"))
    bv_b = sb("bv_b", [128, NB, 128], F32, one)
    rel_t = sb("rel_t", [HD, P], F32, one)
    rel_s = sb("rel_s", [HD, P], F32, one)
    rel_r = sb("rel_r", [HD, P], F32, one)
    rel_p = sb("rel_p", [HD, PARTS, P], BF16, one)
    gx = sb("gx", [HD, 3], F32, one)
    g_ext = sb("g_ext", [128, 3], F32, one)
    hmask = sb("hmask", [128, 2 * GAP], F32, one)
    hneg = sb("hneg", [128, 2 * GAP], F32, one)
    own = sb("own", [128, S], F32, one)
    gap_max = sb("gap_max", [128, B], F32, one)
    gap_one = sb("gap_one", [128, 1], F32, one)
    gap_any = sb("gap_any", [128, 1], F32, one)
    x_all = sb("x_all", [128, TOK], F32, one)
    xh = sb("xh", [128, NB, 128], F32, one)
    stats = sb("stats", [128, NB, 6], F32, one)
    mv = sb("mv", [128, NB, 2], F32, one)
    var_e, std, rstd, nmr = (sb(n, [128, NB], F32, one) for n in ("var_e", "std", "rstd", "nmr"))
    xT = sb("xT", [128, S], F32, one)
    qf, kf, q_rest, k_rest = (sb(n, [128, S], F32, one) for n in ("qf", "kf", "q_rest", "k_rest"))
    q_parts, k_parts = (sb(n, [128, PARTS, S], BF16, one) for n in ("q_parts", "k_parts"))
    q_pos = sb("q_pos", [128, S], F32, one)
    k_ext = sb("k_ext", [128, 2], F32, one)
    k_sel = sb("k_sel", [128, 2, 2 * GAP], F32, one)
    m_neg, m_rest = (sb(n, [H, S], F32, one) for n in ("m_neg", "m_rest"))
    m_parts = sb("m_parts", [H, PARTS, S], BF16, one)
    v_st = sb("v_st", [128, NB, H, 32], F32, one)
    pone = ExitStack()
    p_tr, p_q, p_k, p_v = (ps(n, [128, S], pone) for n in ("p_tr", "p_q", "p_k", "p_v"))

    s_alone = sem("s_alone")
    s_par = sem("s_par")
    s_gs = sem("s_gs")
    s_gst = sem("s_gst")
    s_gld = sem("s_gld")
    s_rw = sem("s_rw")
    s_pool = sem("s_pool")
    s_xin = sem("s_xin")
    s_ln = sem("s_ln")
    s_std = sem("s_std")
    s_xh = sem("s_xh")
    s_tr = sem("s_tr")
    s_xT = sem("s_xT")
    s_q, s_k, s_v = sem("s_q"), sem("s_k"), sem("s_v")
    s_qf, s_kf = sem("s_qf"), sem("s_kf")
    s_kx = sem("s_kx")
    s_sel = sem("s_sel")
    s_hi = sem("s_hi")
    s_rest = sem("s_rest")
    s_mid = sem("s_mid")
    s_low = sem("s_low")
    s_pos = sem("s_pos")
    s_u = sem("s_u")
    s_own = sem("s_own")
    s_gap = sem("s_gap")
    s_gsum = sem("s_gsum")
    s_mneg = sem("s_mneg")
    s_mhi = sem("s_mhi")
    s_mr = sem("s_mr")
    s_vst = sem("s_vst")
    s_qst, s_kst, s_mst, s_vout = sem("s_qst"), sem("s_kst"), sem("s_mst"), sem("s_vout")
    t_q = [sem(f"t_q{p}") for p in range(2)]
    t_k = [sem(f"t_k{p}") for p in range(2)]
    t_v = [sem(f"t_v{p}") for p in range(2)]
    LNS = 5
    KX = 4

    def batches(eng, body):
        body(0, True, False)
        with eng.Fori(1, B - 1) as b:
            body(b, False, False)
        body(B - 1, False, True)

    sp = nc.sync

    def load_qk(u, p):
        at = u * (HG * S)
        sp.dma_start(q_sb[p][0:ROWS, :], ap(q_dram, at,
                     [[DROW, PARTS * HD], [0, PARTS], [1, HG * S]])).then_inc(t_q[p], 16)
        sp.dma_start(q_sb[p][ROWS:ROWS + PARTS, :], ap(m_dram, at,
                     [[DROW, PARTS], [1, HG * S]])).then_inc(t_q[p], 16)
        sp.dma_start(k_sb[p][0:ROWS, :], ap(k_dram, at,
                     [[0, PARTS], [DROW, PARTS * HD], [1, HG * S]])).then_inc(t_k[p], 16)

    def load_v(u, p):
        sp.dma_start(v_sb[p][:, :, :], ap(v_dram, u * (HG * 32),
                     [[NB * DVROW, 128], [DVROW, NB], [1, HG * 32]])).then_inc(t_v[p], 16)

    with nc.Block() as block:
        @block.sync
        def _(sp):
            def tokens(b):
                sp.dma_start(x_all[:, b * S:(b + 1) * S].rearrange("p (t e) -> p t e", e=E),
                             ap(x.tensor, b * (S * E), [[E, 128], [128 * E, NB], [1, E]])).then_inc(s_xin, 16)

            tokens(0)
            for dst, src in ((wq_sb[:, :], Wq), (wk_sb[:, :], Wk), (wv_sb[:, :], Wv),
                             (bq_c[:, :], bq.rearrange("(p a) -> p a", a=1)),
                             (bk_c[:, :], bk.rearrange("(p a) -> p a", a=1)),
                             (r0_c[:, :], ap(rel.tensor, 0, [[0, H], [1, HD], [1, 1]])),
                             (bv_b[:, :, :], ap(bv.tensor, 0, [[0, 128], [0, NB], [1, 128]])),
                             (rel_t[:, :], ap(rel.tensor, 0, [[1, HD], [HD, P]]))):
                sp.dma_start(dst, src).then_inc(s_par, 16)
            sp.wait_ge(s_xin, 16)
            tokens(1)
            sp.wait_ge(s_gs, 9)
            sp.dma_start(g_dram.ap(), rel_p[:, :, :]).then_inc(s_gst, 16)
            sp.dma_start(gx_dram.ap(), gx[:, :]).then_inc(s_gst, 16)
            sp.wait_ge(s_gst, 32)
            sp.dma_start(g_ext[:, :], ap(gx_dram, 0, [[0, H], [3, HD], [1, 3]])).then_inc(s_gld, 16)
            sp.wait_ge(s_pool, 3)
            sp.dma_start(rel_w[0:ROWS, 0:P], ap(g_dram, 0, [[0, PARTS], [P, HD * PARTS], [1, P]])).then_inc(s_rw, 16)
            sp.dma_start(rel_w[0:ROWS, P:P + BLK],
                         ap(g_dram, 0, [[0, PARTS], [P, HD * PARTS], [1, BLK]])).then_inc(s_rw, 16)
            for b in range(2, B):
                sp.wait_ge(s_xin, b * 16)
                tokens(b)
            sp.wait_ge(s_rw, 32)

            def shift(b):
                sp.wait_ge(s_mr, b * 2 + 2)
                sp.dma_start(ap(m_dram, b * (H * S), [[S, H], [DROW, PARTS], [1, S]]), m_parts[:, :, :]).then_inc(s_mst, 16)

            def batch(b, first, last):
                if last:
                    sp.wait_ge(s_pool, 14)
                    sp.wait_ge(s_vout, 16 * b)
                    sp.wait_ge(s_qst, 16 * PARTS * b)
                    sp.wait_ge(s_kst, 16 * PARTS * b)
                    sp.wait_ge(s_mst, 16 * (b - 1))
                    load_qk(0, 0)
                    load_v(0, 0)
                if not first:
                    shift(b - 1)
                for part, made in enumerate((s_hi, s_mid, s_low)):
                    sp.wait_ge(made, b * 2 + 2)
                    sp.dma_start(ap(q_dram, part * (HD * DROW) + b * (H * S), [[S, H], [DROW, HD], [1, S]]),
                                 q_parts[:, part, :]).then_inc(s_qst, 16)
                    sp.dma_start(ap(k_dram, part * DROW + b * (H * S), [[S, H], [PARTS * DROW, HD], [1, S]]),
                                 k_parts[:, part, :]).then_inc(s_kst, 16)
                    if part == 1:
                        sp.wait_ge(s_vst, b + 1)
                        sp.dma_start(ap(v_dram, b * (H * 32), [[NB * DVROW, 128], [DVROW, NB], [1, H * 32]]),
                                     v_st[:, :, :, :].rearrange("p n h d -> p n (h d)")).then_inc(s_vout, 16)

            batches(sp, batch)
            shift(B - 1)
            sp.wait_ge(s_vout, 16 * B)
            sp.wait_ge(s_qst, 16 * PARTS * B)
            sp.wait_ge(s_kst, 16 * PARTS * B)
            sp.wait_ge(s_mst, 16 * B)

        @block.gpsimd
        def _(pool):
            def step(ins, n):
                ins.then_inc(s_pool, 1)
                pool.wait_ge(s_pool, n)

            step(nc.gpsimd.memset(ident[:, :], 0.0), 1)
            step(nc.gpsimd.affine_select(out=ident[:, :], in_=ident[:, :], compare_op=ALU.not_equal, fill=1.0,
                                         base=0, pattern=[[-1, 128]], channel_multiplier=1), 2)
            step(nc.gpsimd.memset(rel_w[64:KROWS, :], 0.0), 3)
            step(nc.gpsimd.memset(hmask[:, :], 1.0), 4)
            step(nc.gpsimd.affine_select(out=hmask[:, :], in_=hmask[:, :], compare_op=ALU.is_ge, fill=0.0,
                                         base=0, pattern=[[0, 2], [-HD, GAP]], channel_multiplier=1), 5)
            step(nc.gpsimd.affine_select(out=hmask[:, :], in_=hmask[:, :], compare_op=ALU.is_ge, fill=0.0,
                                         base=HD - 1, pattern=[[0, 2], [HD, GAP]], channel_multiplier=-1), 6)
            step(nc.gpsimd.memset(v_st[:, :, :, HD:32], 0.0), 7)
            step(nc.gpsimd.memset(v_st[:, :, :, HD:HD + 1], 1.0), 8)
            step(nc.gpsimd.memset(hneg[:, :], 0.0), 9)
            step(nc.gpsimd.memset(gap_one[:, :], 0.0), 10)
            for p in range(2):
                step(nc.gpsimd.memset(q_sb[p][64:KROWS, :], 0.0), 11 + 2 * p)
                step(nc.gpsimd.memset(k_sb[p][64:KROWS, :], 1.0), 12 + 2 * p)

        @block.vector
        def _(dve):
            def layernorm(b, first, meanwhile=None):
                tile = lambda t: x_all[:, b * S + t * E:b * S + (t + 1) * E] if isinstance(b, int) \
                    else x_all[:, bass.ds(b * S + t * E, E)]
                dve.wait_ge(s_xin, b * 16 + 16)
                for t in range(NB):
                    last = nc.vector.bn_stats(stats[:, t, :], tile(t))
                last.then_inc(s_ln, 1)
                wait_alone(dve, s_ln, b * LNS + 1, s_alone)
                for t in range(NB):
                    last = nc.vector.bn_aggr(mv[:, t, :], stats[:, t, :])
                last.then_inc(s_ln, 1)
                dve.wait_ge(s_ln, b * LNS + 2)
                nc.vector.tensor_scalar(var_e[:, :], mv[:, :, 1], EPS, None, ALU.add).then_inc(s_ln, 1)
                if meanwhile:
                    meanwhile()
                dve.wait_ge(s_std, b + 1)
                nc.vector.reciprocal(rstd[:, :], std[:, :]).then_inc(s_ln, 1)
                dve.wait_ge(s_ln, b * LNS + 4)
                nc.vector.scalar_tensor_tensor(out=nmr[:, :], in0=mv[:, :, 0], scalar=-1.0, in1=rstd[:, :],
                                               op0=ALU.mult, op1=ALU.mult).then_inc(s_ln, 1)
                dve.wait_ge(s_ln, b * LNS + 5)
                if not first:
                    dve.wait_ge(s_tr, b * 2)
                for t in range(NB):
                    last = nc.vector.tensor_scalar(xh[:, t, :], tile(t), rstd[:, t:t + 1], nmr[:, t:t + 1],
                                                   ALU.mult, ALU.add)
                last.then_inc(s_xh, 1)

            def gap(b):
                dve.wait_ge(s_u, b * 2 + 2)
                nc.vector.tensor_reduce(out=gap_max[GAP:GAP + H, bass.ds(b, 1)], in_=p_tr[GAP:GAP + H, :], op=ALU.max,
                                        axis=AX.X).then_inc(s_gap, 1)

            def shift_rest(b):
                dve.wait_ge(s_mhi, b * 2 + 1)
                nc.vector.tensor_tensor(m_rest[:, :], m_neg[:, :], m_parts[:, 0, :], ALU.subtract).then_inc(s_mr, 1)

            def shift_low(b):
                dve.wait_ge(s_mhi, b * 2 + 2)
                nc.vector.tensor_tensor(m_parts[:, 2, :], m_rest[:, :], m_parts[:, 1, :], ALU.subtract).then_inc(s_mr, 1)

            def batch(b, first, last_batch):
                if not last_batch:
                    layernorm(b + 1, False, None if first else lambda: gap(b - 1))
                elif not first:
                    gap(b - 1)
                if not first:
                    shift_rest(b - 1)
                dve.wait_ge(s_kf, b + 1)
                nc.vector.tensor_reduce(out=k_ext[:, 0:1], in_=kf[:, :], op=ALU.max, axis=AX.X).then_inc(s_kx, 1)
                nc.vector.tensor_reduce(out=k_ext[:, 1:2], in_=kf[:, :], op=ALU.min, axis=AX.X).then_inc(s_kx, 1)
                dve.wait_ge(s_kx, b * KX + 2)
                nc.vector.tensor_tensor(k_ext[:, :], k_ext[:, :], g_ext[:, 0:2], ALU.add).then_inc(s_kx, 1)
                dve.wait_ge(s_kx, b * KX + 3)
                nc.vector.tensor_tensor(k_ext[:, 0:1], k_ext[:, 0:1], k_ext[:, 1:2], ALU.subtract).then_inc(s_kx, 1)
                dve.wait_ge(s_kx, b * KX + 4)
                if not first:
                    dve.wait_ge(s_u, b * 2)
                for e in range(2):
                    last = nc.vector.tensor_scalar(k_sel[:, e, :], hmask[:, :], k_ext[:, e:e + 1], None, ALU.mult)
                last.then_inc(s_sel, 1)
                dve.wait_ge(s_qf, b + 1)
                nc.vector.scalar_tensor_tensor(out=own[:, :], in0=kf[:, :], scalar=g_ext[:, 2:3], in1=qf[:, :],
                                               op0=ALU.add, op1=ALU.mult).then_inc(s_own, 1)
                dve.wait_ge(s_hi, b * 2 + 1)
                nc.vector.tensor_tensor(q_rest[:, :], qf[:, :], q_parts[:, 0, :], ALU.subtract).then_inc(s_rest, 1)
                dve.wait_ge(s_hi, b * 2 + 2)
                nc.vector.tensor_tensor(k_rest[:, :], kf[:, :], k_parts[:, 0, :], ALU.subtract).then_inc(s_rest, 1)
                dve.wait_ge(s_v, b + 1)
                if not first:
                    dve.wait_ge(s_vout, b * 16)
                nc.vector.tensor_tensor(v_st[:, :, :, 0:HD], p_v[:, :].rearrange("p (n h d) -> p n h d", n=NB, h=H),
                                        bv_b[:, :, :].rearrange("p n (h d) -> p n h d", h=H), ALU.add).then_inc(s_vst, 1)
                if not first:
                    shift_low(b - 1)
                dve.wait_ge(s_mid, b * 2 + 1)
                nc.vector.tensor_tensor(q_parts[:, 2, :], q_rest[:, :], q_parts[:, 1, :], ALU.subtract).then_inc(s_low, 1)
                dve.wait_ge(s_mid, b * 2 + 2)
                nc.vector.tensor_tensor(k_parts[:, 2, :], k_rest[:, :], k_parts[:, 1, :], ALU.subtract).then_inc(s_low, 1)

            layernorm(0, True)
            dve.wait_ge(s_par, 8 * 16)
            nc.vector.tensor_tensor(kb_c[:, :], bk_c[:, :], r0_c[:, :], ALU.add).then_inc(s_gs, 1)
            nc.vector.tensor_scalar(rel_s[:, :], rel_t[:, :], rel_t[:, 0:1], None, ALU.subtract).then_inc(s_gs, 1)
            dve.wait_ge(s_gs, 2)
            nc.vector.tensor_reduce(out=gx[:, 0:1], in_=rel_s[:, :], op=ALU.max, axis=AX.X).then_inc(s_gs, 1)
            nc.vector.tensor_reduce(out=gx[:, 1:2], in_=rel_s[:, :], op=ALU.min, axis=AX.X).then_inc(s_gs, 1)
            nc.vector.tensor_copy(rel_p[:, 0, :], rel_s[:, :]).then_inc(s_gs, 1)
            dve.wait_ge(s_gs, 5)
            nc.vector.tensor_tensor(rel_r[:, :], rel_s[:, :], rel_p[:, 0, :], ALU.subtract).then_inc(s_gs, 1)
            dve.wait_ge(s_gs, 6)
            nc.vector.tensor_copy(rel_p[:, 1, :], rel_r[:, :]).then_inc(s_gs, 1)
            dve.wait_ge(s_gs, 7)
            nc.vector.tensor_tensor(rel_p[:, 2, :], rel_r[:, :], rel_p[:, 1, :], ALU.subtract).then_inc(s_gs, 1)
            nc.vector.tensor_copy(gx[:, 2:3], rel_s[:, P - 1:P]).then_inc(s_gs, 1)
            dve.wait_ge(s_gld, 16)
            dve.wait_ge(s_pool, 10)
            nc.vector.tensor_scalar(hneg[:, GAP:GAP + H], hmask[:, GAP:GAP + H], -1.0, None, ALU.mult).then_inc(s_gs, 1)
            batches(dve, batch)
            gap(B - 1)
            shift_rest(B - 1)
            dve.wait_ge(s_gap, B)
            nc.vector.tensor_reduce(out=gap_one[GAP:GAP + H, :], in_=gap_max[GAP:GAP + H, :], op=ALU.max,
                                    axis=AX.X).then_inc(s_gap, 1)
            dve.wait_ge(s_gap, B + 1)
            nc.vector.tensor_scalar(gap_any[:, :], gap_one[:, :], LIMIT, None, ALU.is_gt).then_inc(s_gap, 1)
            shift_low(B - 1)
            dve.wait_ge(s_gsum, 1)
            nc.vector.tensor_reduce(out=far_flag[:, :], in_=p_tr[0:1, 0:128], op=ALU.max, axis=AX.X).then_inc(s_gap, 1)

        @block.scalar
        def _(act):
            def root(b):
                act.wait_ge(s_ln, b * LNS + 3)
                nc.scalar.activation(std[:, :], var_e[:, :], ACT.Sqrt).then_inc(s_std, 1)

            def transposed(b, first):
                if not first:
                    act.wait_ge(s_v, b)
                for j in range(2):
                    act.wait_ge(s_tr, b * 2 + j + 1)
                    nc.scalar.activation(xT[:, j * 512:(j + 1) * 512], p_tr[:, j * 512:(j + 1) * 512],
                                         ACT.Identity).then_inc(s_xT, 1)

            def shift_mid(b):
                act.wait_ge(s_mr, b * 2 + 1)
                nc.scalar.activation(m_parts[:, 1, :], m_rest[:, :], ACT.Identity).then_inc(s_mhi, 1)

            def batch(b, first, last_batch):
                if not last_batch:
                    root(b + 1)
                act.wait_ge(s_q, b + 1)
                if not first:
                    act.wait_ge(s_rest, b * 2)
                    act.wait_ge(s_u, b * 2)
                nc.scalar.activation(qf[:, :], p_q[:, :], ACT.Identity, bias=bq_c[:, 0:1]).then_inc(s_qf, 1)
                act.wait_ge(s_k, b + 1)
                nc.scalar.activation(kf[:, :], p_k[:, :], ACT.Identity, bias=kb_c[:, 0:1]).then_inc(s_kf, 1)
                if not last_batch:
                    transposed(b + 1, False)
                if not first:
                    act.wait_ge(s_qst, b * (16 * PARTS))
                    act.wait_ge(s_kst, b * (16 * PARTS))
                act.wait_ge(s_qf, b + 1)
                nc.scalar.activation(q_parts[:, 0, :], qf[:, :], ACT.Identity).then_inc(s_hi, 1)
                act.wait_ge(s_kf, b + 1)
                nc.scalar.activation(k_parts[:, 0, :], kf[:, :], ACT.Identity).then_inc(s_hi, 1)
                nc.scalar.activation(q_pos[:, :], qf[:, :], ACT.Relu).then_inc(s_pos, 1)
                if not first:
                    shift_mid(b - 1)
                act.wait_ge(s_rest, b * 2 + 1)
                nc.scalar.activation(q_parts[:, 1, :], q_rest[:, :], ACT.Identity).then_inc(s_mid, 1)
                act.wait_ge(s_rest, b * 2 + 2)
                nc.scalar.activation(k_parts[:, 1, :], k_rest[:, :], ACT.Identity).then_inc(s_mid, 1)
                for j in range(2):
                    act.wait_ge(s_u, b * 2 + j + 1)
                    nc.scalar.activation(m_neg[:, j * 512:(j + 1) * 512], p_tr[0:H, j * 512:(j + 1) * 512],
                                         ACT.Identity, scale=-1.0).then_inc(s_mneg, 1)
                act.wait_ge(s_mneg, b * 2 + 2)
                if not first:
                    act.wait_ge(s_mst, b * 16)
                nc.scalar.activation(m_parts[:, 0, :], m_neg[:, :], ACT.Identity).then_inc(s_mhi, 1)

            root(0)
            transposed(0, True)
            act.wait_ge(s_par, 8 * 16)
            act.wait_ge(s_gs, 1)
            batches(act, batch)
            shift_mid(B - 1)

        @block.tensor
        def _(pe):
            pe.wait_ge(s_pool, 2)

            def transposes(b, first):
                pe.wait_ge(s_xh, b + 1)
                if isinstance(b, int) and b == 1:
                    pe.wait_ge(s_xT, 2)
                elif not first:
                    pe.wait_ge(s_mneg, b * 2 - 2)
                    pe.wait_ge(s_gap, b - 1)
                for t in range(NB):
                    last = nc.tensor.transpose(p_tr[:, t * 128:(t + 1) * 128], xh[:, t, :], ident[:, :])
                    if t % 4 == 3:
                        last.then_inc(s_tr, 1)

            def project_qk(b, first):
                pe.wait_ge(s_xT, b * 2 + 2)
                for bank, w, done, left in ((p_q, wq_sb, s_q, s_qf), (p_k, wk_sb, s_k, s_kf)):
                    if not first:
                        pe.wait_ge(left, b)
                    for j in range(2):
                        last = nc.tensor.matmul(bank[:, j * 512:(j + 1) * 512], w[:, :], xT[:, j * 512:(j + 1) * 512],
                                                start=True, stop=True)
                    last.then_inc(done, 1)

            def project_v(b, first):
                if not first:
                    pe.wait_ge(s_vst, b)
                for t in range(NB):
                    last = nc.tensor.matmul(p_v[:, t * 128:(t + 1) * 128], xT[:, t * 128:(t + 1) * 128], wv_sb[:, :],
                                            start=True, stop=True)
                last.then_inc(s_v, 1)

            def bound(b):
                pe.wait_ge(s_sel, b + 1)
                pe.wait_ge(s_pos, b + 1)
                pe.wait_ge(s_own, b + 1)
                for j in range(2):
                    c = slice(j * 512, (j + 1) * 512)
                    nc.tensor.matmul(p_tr[0:2 * GAP, c], k_sel[:, 0, :], q_pos[:, c], start=True, stop=False)
                    nc.tensor.matmul(p_tr[0:2 * GAP, c], k_sel[:, 1, :], qf[:, c], start=False, stop=False)
                    nc.tensor.matmul(p_tr[0:2 * GAP, c], hneg[:, :], own[:, c], start=False, stop=True).then_inc(s_u, 1)

            def batch(b, first, last_batch):
                if not last_batch:
                    transposes(b + 1, False)
                    project_qk(b + 1, False)
                bound(b)
                if not last_batch:
                    project_v(b + 1, False)

            transposes(0, True)
            pe.wait_ge(s_par, 8 * 16)
            project_qk(0, True)
            project_v(0, True)
            pe.wait_ge(s_gs, 10)
            batches(pe, batch)
            pe.wait_ge(s_mneg, B * 2)
            pe.wait_ge(s_gap, B + 2)
            nc.tensor.matmul(p_tr[0:1, 0:128], gap_any[:, :], ident[:, :], start=True, stop=True).then_inc(s_gsum, 1)
    pone.close()
    one.close()

    largest_scores(nc, sem, ident, rel_w, far_flag, q_sb, q_dram, k_dram, m_dram, r_dram)

    two = ExitStack()
    bias = [sb(f"bias{p}", [128, BIASCOLS], F32, two) for p in range(2)]
    probs = [sb(f"probs{p}", [128, HG, TCOLS], F32, two) for p in range(PBUFS)]
    o_raw = sb("o_raw", [128, S], F32, two)
    o_rcp = sb("o_rcp", [128, QB], F32, two)
    ptwo = ExitStack()
    p_s = [ps(f"p_s{p}", [128, TCOLS], ptwo) for p in range(SLOTS)]
    p_o = ps("p_o", [128, S], ptwo)
    p_b = [ps(f"p_b{p}", [128, 512], ptwo) for p in range(2)]

    t_alone = sem("t_alone")
    t_s = sem("t_s")
    t_add = sem("t_add")
    t_exp = sem("t_exp")
    t_pv = sem("t_pv")
    t_bmm = sem("t_bmm")
    t_bev = sem("t_bev")
    t_beva = sem("t_beva")
    t_far = sem("t_far")
    t_near = sem("t_near")
    t_oraw = sem("t_oraw")
    t_otr = sem("t_otr")
    t_rcp = sem("t_rcp")
    t_o = sem("t_o")
    ACT_CH = {9, 11, 12, 13, 15}
    OUT_AT = 7
    NPV = len(PRODUCTS)
    EXP_FIRST = 2
    ADDS = sum(HG for g in range(NG) if any(i - j < KINDS for j, i, _ in GROUPS[g]))
    CH_STEP = [5, 7, 8, 10, 12, 13, 15, 16, 18, 20, 22, 23, 25, 28, 32, 33]
    NDVE = CHUNKS - len(ACT_CH)

    def dve_count(c):
        return sum(1 for k in range(c + 1) if k not in ACT_CH)

    def act_count(c):
        return sum(1 for k in range(c + 1) if k in ACT_CH)

    def last_step(g):
        return max(s for s, (k, _) in enumerate(ORDER) if k == g)

    def done_with(g):
        return max(n for n, (_, k, _) in enumerate(PRODUCTS) if k == g) + 1

    def chunk_at(s):
        return CH_STEP.index(s) if s in CH_STEP else None

    def pieces(g):
        got, col = [], 0
        for j, i, n in GROUPS[g]:
            got.append((j, i, n, col))
            col += n * BLK
        return got

    def term_pieces(g):
        return [(j, i - j, min(KINDS - (i - j), n), col) for j, i, n, col in pieces(g) if i - j < KINDS]

    def bias_q(buf, kind, c, banks=1):
        r = (c % HALF) * RCH
        return bias[buf][:, 0:BIASCOLS].rearrange("p (q k r) -> p k q r", k=KINDS, r=BLK)[:, kind, :, r:r + banks * RCH]

    with nc.Block() as block:
        @block.sync
        def _(sp):
            load_qk(1, 1)
            load_v(1, 1)
            for w in EARLY:
                load_weight(w)
            for dst, src in [(wo_sb[:, :], Wo), (bo_b[:, :, :], ap(bo.tensor, 0, [[0, 128], [0, NB], [1, 128]])),
                             (s3_c[:, :], s3.rearrange("(p a) -> p a", a=1))] + \
                    [(d[:, :], ap(v.tensor, 0, [[1, 128], [128, HC]]))
                     for d, v in ((s1_c, s1), (s2_c, s2), (sh1_c, sh1), (sh2_c, sh2))]:
                sp.dma_start(dst, src).then_inc(a_small, 16)
            with sp.Fori(0, UNITS // 2 - 1) as i:
                for p in range(2):
                    sp.wait_ge(t_s, i * (2 * STEPS) + (p + 1) * STEPS)
                    load_qk(i * 2 + p + 2, p)
                    sp.wait_ge(t_pv, i * (2 * NPV) + (p + 1) * NPV)
                    load_v(i * 2 + p + 2, p)

        @block.gpsimd
        def _(pool):
            def masks(copied, made, buf, m):
                c = m * MBANKS
                r = c * RCH
                near, far = (bias_q(buf, kind, c, MBANKS) for kind in (0, 2))
                wait_alone(pool, t_bev, copied, t_alone)
                nc.gpsimd.affine_select(out=far, in_=near, compare_op=ALU.is_ge, fill=0.0, base=-1 - r,
                                        pattern=[[0, QB], [-1, MBANKS * RCH]], channel_multiplier=1).then_inc(t_far, 1)
                wait_alone(pool, t_far, made + 1, t_alone)
                nc.gpsimd.affine_select(out=near, in_=near, compare_op=ALU.is_ge, fill=MASKED, base=r,
                                        pattern=[[0, QB], [1, MBANKS * RCH]], channel_multiplier=-1).then_inc(t_near, 1)

            def unit_masks(u, buf):
                for m in range(MASKS):
                    masks(u * NDVE + dve_count((m + 1) * MBANKS - 1), u * MASKS + m, buf, m)

            unit_masks(0, 0)
            with pool.Fori(0, UNITS // 2 - 1) as i:
                for p in range(2):
                    unit_masks(i * 2 + p + 1, 1 - p)
            unit_masks(UNITS - 1, 1)

        @block.tensor
        def _(pe):
            def scores(T, p, s, first=False):
                g, h = ORDER[s]
                if not first:
                    pe.wait_ge(t_exp, T - SLOTS + 1)
                for j, i, n, c in pieces(g):
                    last = nc.tensor.matmul(p_s[s % SLOTS][:, c:c + n * BLK],
                                            k_sb[p][:, h * S + j * BLK:h * S + (j + 1) * BLK],
                                            q_sb[p][:, h * S + i * BLK:h * S + (i + n) * BLK], start=True, stop=True)
                last.then_inc(t_s, 1)

            def relative(before, p, c, first=False):
                if not first:
                    pe.wait_ge(t_bev, before[0])
                    pe.wait_ge(t_beva, before[1])
                q = q_sb[p][:, :].rearrange("k (q r) -> k r q", r=BLK)
                bank = p_b[c % 2]
                for k in range(RCH):
                    r = (c % HALF) * RCH + k
                    w0 = P - 1 - r if c < HALF else BLK - 1 - r
                    last = nc.tensor.matmul(bank[:, k * QB:(k + 1) * QB], rel_w[:, w0:w0 + BLK], q[:, r, :],
                                            start=True, stop=True)
                last.then_inc(t_bmm, 1)

            def copies(u_dve, u_act, c):
                if c >= 2:
                    return u_dve + dve_count(c - 2), u_act + act_count(c - 2)
                k = CHUNKS - 2 + c
                return u_dve - NDVE + dve_count(k), u_act - len(ACT_CH) + act_count(k)

            def values(u, p, n):
                _, g, piece = PRODUCTS[n]
                if piece == 0:
                    pe.wait_ge(t_exp, u * STEPS + last_step(g) + 1)
                j, i, blocks, c = pieces(g)[piece]
                for h in range(HG):
                    last = nc.tensor.matmul(p_o[32 * h:32 * h + 32, i * BLK:(i + blocks) * BLK],
                                            v_sb[p][:, j, h * 32:(h + 1) * 32],
                                            probs[BUFFER[g]][:, h, c:c + blocks * BLK],
                                            start=(j == 0), stop=((j, i, blocks) in FINAL))
                last.then_inc(t_pv, 1)

            def products_at(u, p, s):
                for n, (at, _, _) in enumerate(PRODUCTS):
                    if at == s:
                        values(u, p, n)

            def outputs(done):
                pe.wait_ge(t_oraw, done)
                for n in range(NB):
                    last = nc.tensor.transpose(p_o[:, n * BLK:(n + 1) * BLK], o_raw[:, n * BLK:(n + 1) * BLK], ident[:, :])
                last.then_inc(t_otr, 1)

            def unit(u, p, last_unit):
                T0 = u * STEPS
                for s in range(HG, STEPS):
                    g, h = ORDER[s]
                    scores(T0 + s, p, s)
                    if s == OUT_AT and not is_first(u):
                        outputs(u)
                    if s == PRODUCTS[0][0]:
                        pe.wait_ge(t_v[p], loads(u, p))
                        if not is_first(u):
                            pe.wait_ge(t_o, u)
                    products_at(u, p, s)
                    c = chunk_at(s)
                    if not last_unit and c is not None:
                        if c == 0:
                            pe.wait_ge(t_q[1 - p], 2 * loads_next(u, p))
                        relative(copies((u + 1) * NDVE, (u + 1) * len(ACT_CH), c), 1 - p, c)
                if last_unit:
                    for s in range(HG):
                        products_at(u, p, STEPS + s)
                else:
                    pe.wait_ge(t_k[1 - p], loads_next(u, p))
                    for s in range(HG):
                        scores(T0 + STEPS + s, 1 - p, s)
                        products_at(u, p, STEPS + s)

            turn = [None]

            def loads(u, p):
                return turn[0] * 16 + 16

            def loads_next(u, p):
                return turn[0] * 16 + 16 + 16 * p

            pe.wait_ge(t_q[0], 32)
            for c in range(CHUNKS):
                relative(copies(0, 0, c) if c >= 2 else None, 0, c, first=c < 2)
            pe.wait_ge(t_k[0], 16)
            for s in range(HG):
                scores(s, 0, s, first=s < SLOTS)
            turn[0] = 0
            unit(0, 0, False)
            unit(1, 1, False)
            with pe.Fori(1, UNITS // 2 - 1) as i:
                turn[0] = i
                for p in range(2):
                    unit(i * 2 + p, p, False)
            turn[0] = UNITS // 2 - 1
            unit(UNITS - 2, 0, False)
            unit(UNITS - 1, 1, True)
            outputs(UNITS)

        @block.vector
        def _(dve):
            def add(T, p, s):
                g, h = ORDER[s]
                terms = term_pieces(g)
                if not terms:
                    return
                dve.wait_ge(t_s, T + 1)
                def term(j, k, dims):
                    return ap(bias[p], h * (NB * KINDS * BLK) + j * (KINDS * BLK) + k * TCOLS,
                              [[BIASCOLS, 128]] + dims + [[1, BLK]])

                j, k, n, col = terms[0]
                if len(terms) == 2 and terms[1][2] == n:
                    cols = p_s[s % SLOTS][:, :].rearrange("p (t k x) -> p t k x", t=2, x=BLK)
                    last = nc.vector.tensor_tensor(cols, cols, term(j, k, [[4 * KINDS * BLK, 2], [TCOLS, n]]), ALU.add)
                else:
                    for j, k, n, col in terms:
                        cols = p_s[s % SLOTS][:, col:col + n * BLK].rearrange("p (k x) -> p k x", x=BLK)
                        last = nc.vector.tensor_tensor(cols, cols, term(j, k, [[TCOLS, n]]), ALU.add)
                last.then_inc(t_add, 1)

            def copy_bank(n, buf, c):
                dve.wait_ge(t_bmm, n)
                nc.vector.tensor_copy(bias_q(buf, 0 if c < HALF else 1, c),
                                      p_b[c % 2][:, :].rearrange("p (r q) -> p q r", q=QB)).then_inc(t_bev, 1)

            def ready(u):
                dve.wait_ge(t_near, u * MASKS + MASKS)
                dve.wait_ge(t_bev, u * NDVE + NDVE)
                dve.wait_ge(t_beva, u * len(ACT_CH) + len(ACT_CH))

            def outputs(done):
                dve.wait_ge(t_otr, done)
                o_t = p_o[:, :].rearrange("p (q d) -> p q d", d=32)
                nc.vector.reciprocal(o_rcp[:, :], o_t[:, :, HD]).then_inc(t_rcp, 1)
                dve.wait_ge(t_rcp, done)
                dst = o_all[:, bass.ds((done - 1) * (QB * HD), QB * HD)]
                nc.vector.tensor_tensor(dst.rearrange("p (q d) -> p q d", d=HD), o_t[:, :, 0:HD],
                                        o_rcp[:, :].unsqueeze(2).broadcast_to([128, QB, HD]), ALU.mult).then_inc(t_o, 1)

            def unit(u, p, last_unit):
                for s in range(HG, STEPS):
                    add(u * STEPS + s, p, s)
                    if s == OUT_AT and not is_first(u):
                        outputs(u)
                    c = chunk_at(s)
                    if not last_unit and c is not None and c not in ACT_CH:
                        copy_bank((u + 1) * CHUNKS + c + 1, 1 - p, c)
                if not last_unit:
                    ready(u + 1)
                    for s in range(HG):
                        add((u + 1) * STEPS + s, 1 - p, s)

            for c in range(CHUNKS):
                if c not in ACT_CH:
                    copy_bank(c + 1, 0, c)
            ready(0)
            for s in range(HG):
                add(s, 0, s)
            unit(0, 0, False)
            unit(1, 1, False)
            with dve.Fori(1, UNITS // 2 - 1) as i:
                for p in range(2):
                    unit(i * 2 + p, p, False)
            unit(UNITS - 2, 0, False)
            unit(UNITS - 1, 1, True)
            outputs(UNITS)

        @block.scalar
        def _(act):
            def exps(u, p, s):
                g, h = ORDER[s]
                if term_pieces(g):
                    act.wait_ge(t_add, u * ADDS + sum(1 for k in range(s + 1) if term_pieces(ORDER[k][0])))
                else:
                    act.wait_ge(t_s, u * STEPS + s + 1)
                nc.scalar.activation(probs[BUFFER[g]][:, h, :], p_s[s % SLOTS][:, :], ACT.Exp, scale=SCALE).then_inc(t_exp, 1)

            def copy_bank(n, buf, c):
                act.wait_ge(t_bmm, n)
                nc.scalar.activation(bias_q(buf, 1, c), p_b[c % 2][:, :].rearrange("p (r q) -> p q r", q=QB),
                                     ACT.Copy).then_inc(t_beva, 1)

            def buffer_free(u, s):
                g, h = ORDER[s]
                if h > 0:
                    return
                earlier = [k for k in range(g) if BUFFER[k] == BUFFER[g]]
                if earlier:
                    act.wait_ge(t_pv, u * NPV + done_with(earlier[-1]))
                elif not is_first(u):
                    k = max(k for k in range(NG) if BUFFER[k] == BUFFER[g])
                    act.wait_ge(t_pv, (u - 1) * NPV + done_with(k))

            def unit(u, p, last_unit):
                for s in range(HG, STEPS):
                    g, h = ORDER[s]
                    buffer_free(u, s)
                    exps(u, p, s)
                    c = chunk_at(s)
                    if not last_unit and c in ACT_CH:
                        copy_bank((u + 1) * CHUNKS + c + 1, 1 - p, c)
                if not last_unit:
                    for s in range(EXP_FIRST):
                        buffer_free(u + 1, s)
                        exps(u + 1, 1 - p, s)
                act.wait_ge(t_pv, u * NPV + NPV)
                if not is_first(u):
                    act.wait_ge(t_otr, u)
                nc.scalar.activation(o_raw[:, :], p_o[:, :], ACT.Copy).then_inc(t_oraw, 1)
                if not last_unit:
                    for s in range(EXP_FIRST, HG):
                        buffer_free(u + 1, s)
                        exps(u + 1, 1 - p, s)

            for c in sorted(ACT_CH):
                copy_bank(c + 1, 0, c)
            for s in range(HG):
                exps(0, 0, s)
            unit(0, 0, False)
            unit(1, 1, False)
            with act.Fori(1, UNITS // 2 - 1) as i:
                for p in range(2):
                    unit(i * 2 + p, p, False)
            unit(UNITS - 2, 0, False)
            unit(UNITS - 1, 1, True)
    ptwo.close()
    two.close()
    operands.close()

    stage3(nc, sb, ps, sem, ident, o_all, x, out, WEIGHTS, EARLY, wnat, load_weight, a_wl, a_small, wo_sb, bo_b,
           s1_c, s2_c, sh1_c, sh2_c, s3_c)


def largest_scores(nc, sem, ident, rel_w, far_flag, q_sb, q_dram, k_dram, m_dram, r_dram):
    W = 4 * BLK
    got = ExitStack()
    q_h = got.enter_context(nc.sbuf_tensor("q_h", [ROWS, S], BF16))
    k_h = got.enter_context(nc.sbuf_tensor("k_h", [ROWS, S], BF16))
    terms = got.enter_context(nc.sbuf_tensor("terms", [BLK, NB, W], F32))
    skewed = got.enter_context(nc.sbuf_tensor("skewed", [BLK, NB, 3 * BLK], F32))
    neg_max = got.enter_context(nc.sbuf_tensor("neg_max", [BLK, NB], F32))
    rest = [got.enter_context(nc.sbuf_tensor(f"rest{i}", [NB, BLK], F32)) for i in range(PARTS - 1)]
    parts = got.enter_context(nc.sbuf_tensor("parts", [NB, PARTS, BLK], BF16))
    p_w = [got.enter_context(nc.psum_tensor(f"p_w{i}", [BLK, 2, W], F32)) for i in range(4)]

    e_alone = sem("e_alone")
    e_zero = sem("e_zero")
    e_load = sem("e_load")
    e_rel = sem("e_rel")
    e_copy = sem("e_copy")
    e_skew = sem("e_skew")
    e_mask = sem("e_mask")
    e_score = sem("e_score")
    e_max = sem("e_max")
    e_tr = sem("e_tr")
    e_part = sem("e_part")
    e_out = sem("e_out")
    e_back = sem("e_back")
    HEADS = B * H

    def taken(eng):
        return eng.value_load(far_flag[0:1, 0:1], min_val=0, max_val=1) > 0

    with nc.Block() as block:
        @block.sync
        def _(sp):
            def head(g, first):
                if not first:
                    sp.wait_ge(e_part, g * 5)
                sp.dma_start(q_h[:, :], ap(q_dram, g * S, [[DROW, PARTS * HD], [0, PARTS], [1, S]])).then_inc(e_load, 16)
                sp.dma_start(k_h[:, :], ap(k_dram, g * S, [[0, PARTS], [DROW, PARTS * HD], [1, S]])).then_inc(e_load, 16)
                sp.wait_ge(e_copy, g + 1)
                sp.dma_start(ap(r_dram, 0, [[W, BLK], [BLK * W, NB], [1, W]]), terms[:, :, :]).then_inc(e_skew, 16)
                sp.wait_ge(e_skew, g * 32 + 16)
                sp.dma_start(skewed[:, :, :], ap(r_dram, BLK - 1, [[W - 1, BLK], [BLK * W, NB], [1, 3 * BLK]])).then_inc(e_skew, 16)
                sp.wait_ge(e_part, g * 5 + 5)
                sp.dma_start(ap(m_dram, g * S, [[BLK, NB], [DROW, PARTS], [1, BLK]]), parts[:, :, :]).then_inc(e_out, 16)

            with sp.If(taken(sp)):
                sp.wait_ge(e_zero, 1)
                turns(sp, HEADS, head)
                sp.wait_ge(e_out, 16 * HEADS)
                sp.dma_start(q_sb[0][ROWS:ROWS + PARTS, :], ap(m_dram, 0, [[DROW, PARTS], [1, HG * S]])).then_inc(e_back, 16)
                sp.wait_ge(e_back, 16)

        @block.gpsimd
        def _(pool):
            def head(g, first):
                wait_alone(pool, e_skew, g * 32 + 32, e_alone)
                nc.gpsimd.affine_select(out=skewed[:, :, :], in_=skewed[:, :, :], compare_op=ALU.is_ge, fill=MASKED,
                                        base=2 * BLK, pattern=[[0, NB], [-1, 3 * BLK]], channel_multiplier=1).then_inc(e_mask, 1)

            with pool.If(taken(pool)):
                turns(pool, HEADS, head)

        @block.tensor
        def _(pe):
            def head(g, first):
                pe.wait_ge(e_load, g * 32 + 32)
                if not first:
                    pe.wait_ge(e_part, g * 5)
                for i in range(NB):
                    last = nc.tensor.matmul(p_w[i // 2][:, i % 2, 0:P + BLK], q_h[:, i * BLK:(i + 1) * BLK],
                                            rel_w[0:ROWS, :], start=True, stop=True)
                last.then_inc(e_rel, 1)
                pe.wait_ge(e_copy, g + 1)
                for i in range(NB):
                    if i >= 4:
                        pe.wait_ge(e_max, g * (2 * NB) + (i - 4) * 2 + 2)
                    for c in range(0, (i + 1) * BLK, 512):
                        w = min(512, (i + 1) * BLK - c)
                        last = nc.tensor.matmul(p_w[i % 4][:, c // 512, 0:w], q_h[:, i * BLK:(i + 1) * BLK],
                                                k_h[:, c:c + w], start=True, stop=True)
                    last.then_inc(e_score, 1)
                pe.wait_ge(e_max, g * (2 * NB) + 2 * NB)
                nc.tensor.transpose(p_w[0][0:NB, 0, 0:BLK], neg_max[:, :], ident[:, :]).then_inc(e_tr, 1)

            with pe.If(taken(pe)):
                turns(pe, HEADS, head)

        @block.vector
        def _(dve):
            def head(g, first):
                dve.wait_ge(e_rel, g + 1)
                if not first:
                    dve.wait_ge(e_skew, g * 32)
                for i in range(NB):
                    last = nc.vector.tensor_copy(terms[:, i, BLK:W], p_w[i // 2][:, i % 2, 0:P + BLK])
                last.then_inc(e_copy, 1)
                dve.wait_ge(e_mask, g + 1)
                for i in range(NB):
                    step = g * (2 * NB) + i * 2
                    tile = p_w[i % 4][:, :, :].rearrange("p t w -> p (t w)")
                    near = min(3, i + 1)
                    end = (i + 1) * BLK
                    dve.wait_ge(e_score, g * NB + i + 1)
                    nc.vector.tensor_tensor(tile[:, end - near * BLK:end], tile[:, end - near * BLK:end],
                                            skewed[:, i, (3 - near) * BLK:3 * BLK], ALU.add).then_inc(e_max, 1)
                    dve.wait_ge(e_max, step + 1)
                    nc.vector.tensor_reduce(out=neg_max[:, i:i + 1], in_=tile[:, 0:end], op=ALU.max, axis=AX.X,
                                            negate=True).then_inc(e_max, 1)
                dve.wait_ge(e_tr, g + 1)
                if not first:
                    dve.wait_ge(e_out, g * 16)
                source = p_w[0][0:NB, 0, 0:BLK]
                for part in range(PARTS):
                    nc.vector.tensor_copy(parts[:, part, :], source).then_inc(e_part, 1)
                    if part < PARTS - 1:
                        dve.wait_ge(e_part, g * 5 + 2 * part + 1)
                        nc.vector.tensor_tensor(rest[part][:, :], source, parts[:, part, :], ALU.subtract).then_inc(e_part, 1)
                        dve.wait_ge(e_part, g * 5 + 2 * part + 2)
                        source = rest[part][:, :]

            with dve.If(taken(dve)):
                nc.vector.memset(terms[:, :, 0:BLK], 0.0).then_inc(e_zero, 1)
                turns(dve, HEADS, head)
    got.close()


def stage3(nc, sb, ps, sem, ident, o_all, x, out, WEIGHTS, EARLY, wnat, load_weight, a_wl, a_small, wo_sb, bo_b,
           s1_c, s2_c, sh1_c, sh2_c, s3_c):
    whi = [sb(f"{n}_hi", [128, cols // 128, rows * 128], F32R) for n, _, rows, cols in WEIGHTS]
    wlo = [sb(f"{n}_lo", [128, cols // 128, rows * 128], F32R) for n, _, rows, cols in WEIGHTS]
    x1_all = sb("x1_all", [128, TOK])
    x1T_hi = sb("x1T_hi", [128, S], F32R)
    x1T_lo = sb("x1T_lo", [128, S], F32R)
    act_f = [sb(f"act_f{k}", [128, HC, FC]) for k in range(NC)]
    xres = sb("xres", [128, NB, 128])
    o_cur = sb("o_cur", [128, NB, 128])
    oT = sb("oT", [128, S])
    y = sb("y", [128, NB, 128])
    zT = sb("zT", [128, S])
    res = sb("res", [128, NB, 128])
    st3, st4 = (sb(n, [128, NB, 6]) for n in ("st3", "st4"))
    mv3, mv4 = (sb(n, [128, NB, 2]) for n in ("mv3", "mv4"))
    low_max = sb("low_max", [128, len(WEIGHTS)])
    low_any = sb("low_any", [128, 1])
    low_flag = sb("low_flag", [1, 1], mybir.dt.int32)
    ve3, sd3, rs3, nm3, ve4, sd4, rs4 = (sb(n, [128, NB]) for n in ("ve3", "sd3", "rs3", "nm3", "ve4", "sd4", "rs4"))
    nat = ExitStack()
    for w, (n, _, rows, cols) in enumerate(WEIGHTS):
        if wnat[w] is None:
            wnat[w] = sb(f"{n}_nat", [128, rows, cols], F32, nat)
    nat.close()
    hid_hi = [[sb(f"hid{k}_{l}_hi", [128, HC, FC], F32R) for l in range(2)] for k in range(NC)]
    hid_lo = [[sb(f"hid{k}_{l}_lo", [128, HC, FC], F32R) for l in range(2)] for k in range(NC)]
    p_z = [ps(f"p_z{k}", [128, FC]) for k in range(NZ)]
    p_pre = [ps(f"p_pre{k}", [128, FC]) for k in range(NC)]
    p_post = [ps(f"p_post{k}", [128, FC]) for k in range(NC)]

    a_alone = sem("a_alone")
    a_w = sem("a_w")
    a_whi, a_wlo = sem("a_whi"), sem("a_wlo")
    a_low = sem("a_low")
    a_lowa = sem("a_lowa")
    a_sum = sem("a_sum")
    r_x = sem("r_x")
    r_oc0 = sem("r_oc0")
    r_oc = sem("r_oc")
    r_otr, r_oT = sem("r_otr"), sem("r_oT")
    r_y = sem("r_y")
    r_dv = sem("r_dv")
    r_sd = sem("r_sd")
    r_xtr, r_hi, r_lo = sem("r_xtr"), sem("r_hi"), sem("r_lo")
    f_z = sem("f_z")
    f_act = sem("f_act")
    f_mul = sem("f_mul")
    f_hi, f_lo = sem("f_hi"), sem("f_lo")
    f_ghi = sem("f_ghi")
    w_zT, w_tr, w_dv, w_sd, w_out = sem("w_zT"), sem("w_tr"), sem("w_dv"), sem("w_sd"), sem("w_out")
    PRE, POST = 15, 6
    ACTS = 3 * HC * NC
    GHI = 2 * HC * NC
    ZT = NC * (2 * HC + 2 * HC + 1)

    TILES = [(0, k, w, o) for k in range(NC) for o in range(HC) for w in range(2)]
    TILES += [(l, k, l + 1, o) for l in (1, 2) for k in range(NC) for o in range(HC)]
    TILES += [(3, k, 4, 0) for k in range(NC)]
    assert len(TILES) == ZT

    def split_of(l, k, o):
        return (l * NC + k) * HC + o

    def reader(idx):
        l, k, w, o = TILES[idx]
        if l == 3:
            return w_zT, NC, k
        if l == 0 and w == 1:
            return f_mul, NC * HC, k * HC + o
        if l == 0:
            return f_act, ACTS, split_of(l, k, o)
        return f_ghi, GHI, split_of(l, k, o) - NC * HC

    def heads_of(n):
        return o_all[:, bass.ds(n * (NB * 128), NB * 128)].rearrange("p (g n d) -> p n g d", g=BG, n=NB)

    wbanks = [(w, k, rows) for w, (_, _, rows, cols) in enumerate(WEIGHTS) for k in range(cols // 128)]

    with nc.Block() as block:
        @block.sync
        def _(sp):
            def tokens(n):
                sp.dma_start(xres[:, :, :], ap(x.tensor, n * (S * E), [[E, 128], [128 * E, NB], [1, E]])).then_inc(r_x, 16)

            def store(n):
                sp.wait_ge(w_dv, n * POST + POST)
                sp.dma_start(ap(out.tensor, n * (S * E), [[E, 128], [128 * E, NB], [1, E]]),
                             res[:, :, :]).then_inc(w_out, 16)

            for n in range(len(WEIGHTS)):
                if n not in EARLY:
                    load_weight(n)
            tokens(0)
            sp.wait_ge(r_dv, 9)
            tokens(1)

            def turn(n):
                sp.wait_ge(r_dv, n * PRE + 9)
                tokens(n + 1)
                store(n - 1)

            with sp.Fori(1, B - 1) as n:
                turn(n)
            store(B - 2)
            store(B - 1)
            sp.wait_ge(w_out, 16 * B)

        @block.gpsimd
        def _(pool):
            def gather(n):
                pool.wait_ge(r_otr, n * NC)
                src = heads_of(n)
                nc.gpsimd.tensor_copy(o_cur[:, :, :].rearrange("p n (g d) -> p n g d", g=BG), src).then_inc(r_oc, 1)

            gather(1)
            with pool.Fori(2, B) as n:
                gather(n)

        @block.tensor
        def _(pe):
            def weight_bank(i):
                w, k, rows = wbanks[i]
                if k == 0:
                    pe.wait_ge(a_wl[w], 16)
                if i >= NZ:
                    pe.wait_ge(a_whi, i - NZ + 1)
                    pe.wait_ge(a_wlo, i - NZ + 1)
                for r in range(rows):
                    last = nc.tensor.transpose(p_z[i % NZ][:, r * 128:(r + 1) * 128],
                                               wnat[w][:, r, k * 128:(k + 1) * 128], ident[:, :])
                last.then_inc(a_w, 1)

            def transposes(dst, src, t0):
                for t in range(NT):
                    last = nc.tensor.transpose(dst[:, t * 128:(t + 1) * 128], src(t0 + t), ident[:, :])
                return last

            def pre_outputs(n, first):
                if first:
                    pe.wait_ge(r_oc0, 1)
                else:
                    pe.wait_ge(r_oc, n)
                    pe.wait_ge(r_lo, n * NC)
                for k in range(NC):
                    transposes(p_pre[k], lambda t: o_cur[:, t, :], k * NT).then_inc(r_otr, 1)

            def pre_project(n):
                for k in range(NC):
                    pe.wait_ge(r_oT, n * NC + k + 1)
                    for t in range(NT):
                        c = (k * NT + t) * 128
                        last = nc.tensor.matmul(p_pre[k][:, t * 128:(t + 1) * 128], oT[:, c:c + 128], wo_sb[:, :],
                                                start=True, stop=True)
                    last.then_inc(r_y, 1)

            def pre_hidden(n):
                pe.wait_ge(r_dv, n * PRE + PRE)
                for k in range(NC):
                    transposes(p_pre[k], lambda t: y[:, t, :], k * NT).then_inc(r_xtr, 1)

            def post_transpose(n, first):
                for k in range(NC):
                    pe.wait_ge(w_zT, n * NC + k + 1)
                    if k == 0 and not first:
                        pe.wait_ge(w_dv, n * POST)
                    transposes(p_post[k], lambda t: zT[:, t * 128:(t + 1) * 128], k * NT).then_inc(w_tr, 1)

            def layer(n, l, k, first, low_parts):
                if l == 0:
                    if k == 0:
                        pe.wait_ge(r_lo, n * NC + NC)
                    hi, lo = [x1T_hi[:, k * FC:(k + 1) * FC]], [x1T_lo[:, k * FC:(k + 1) * FC]]
                else:
                    pe.wait_ge(f_lo, n * ACTS + split_of(l - 1, k, HC - 1) + 1)
                    hi, lo = ([t[k][(l + 1) % 2][:, j, :] for j in range(HC)] for t in (hid_hi, hid_lo))
                for idx, (tl, tk, w, o) in enumerate(TILES):
                    if (tl, tk) != (l, k):
                        continue
                    if idx >= NZ:
                        s, per, place = reader(idx - NZ)
                        pe.wait_ge(s, n * per + place + 1)
                    elif not first:
                        s, per, place = reader(max(i for i in range(ZT) if i % NZ == idx))
                        pe.wait_ge(s, n * per + place + 1 - per)
                    bank = p_z[idx % NZ]
                    cols = slice(o * 128, (o + 1) * 128)
                    for j in range(len(hi)):
                        nc.tensor.matmul(bank[:, :], whi[w][:, j, cols], hi[j], start=(j == 0), stop=False)
                        if low_parts:
                            nc.tensor.matmul(bank[:, :], wlo[w][:, j, cols], hi[j], start=False, stop=False)
                        last = nc.tensor.matmul(bank[:, :], whi[w][:, j, cols], lo[j], start=False,
                                                stop=(j == len(hi) - 1))
                    last.then_inc(f_z, 1)

            pe.wait_ge(a_small, 7 * 16)
            weight_bank(0)
            weight_bank(1)
            pre_outputs(0, True)
            pre_project(0)
            for i in range(2, len(wbanks)):
                weight_bank(i)
            pe.wait_ge(a_wlo, len(wbanks))
            pre_hidden(0)

            def turn(n, first, last, low_parts):
                def layer_of(l, k):
                    layer(n, l, k, first, low_parts)

                if not last:
                    pre_outputs(n + 1, False)
                layer_of(0, 0)
                if not first:
                    post_transpose(n - 1, isinstance(n, int) and n == 1)
                if not last:
                    pre_project(n + 1)
                layer_of(0, 1)
                for l in (1, 2):
                    for k in range(NC):
                        layer_of(l, k)
                if not last:
                    pre_hidden(n + 1)
                for k in range(NC):
                    layer_of(3, k)

            def batches(low_parts):
                turn(0, True, False, low_parts)
                turn(1, False, False, low_parts)
                with pe.Fori(2, B - 1) as n:
                    turn(n, False, False, low_parts)
                turn(B - 1, False, True, low_parts)

            pe.wait_ge(a_low, 5)
            nc.tensor.matmul(p_post[0][0:1, 0:128], low_any[:, :], ident[:, :], start=True, stop=True).then_inc(a_sum, 1)
            pe.wait_ge(a_low, 6)
            low = pe.value_load(low_flag[0:1, 0:1], min_val=0, max_val=1)
            with pe.If(low > 0):
                batches(True)
            with pe.If(low < 1):
                batches(False)
            post_transpose(B - 1, False)

        @block.scalar
        def _(act):
            def weight_bank(i):
                w, k, rows = wbanks[i]
                act.wait_ge(a_w, i + 1)
                nc.scalar.activation(whi[w][:, k, :], p_z[i % NZ][:, 0:rows * 128], ACT.Copy).then_inc(a_whi, 1)

            nc.scalar.activation(o_cur[:, :, :].rearrange("p n (g d) -> p n g d", g=BG), heads_of(0),
                                 ACT.Copy).then_inc(r_oc0, 1)

            def low_sum(w):
                act.wait_ge(a_wlo, max(i for i, (k, _, _) in enumerate(wbanks) if k == w) + 1)
                nc.scalar.activation(act_f[w - 2][:, :, :], wlo[w][:, :, :].bitcast(F32), ACT.Abs,
                                     accum_out=low_max[:, w:w + 1]).then_inc(a_lowa, 1)

            def pre_oT(n, first):
                if not first:
                    act.wait_ge(r_y, n * NC)
                for k in range(NC):
                    act.wait_ge(r_otr, n * NC + k + 1)
                    nc.scalar.activation(oT[:, k * FC:(k + 1) * FC], p_pre[k][:, :], ACT.Copy).then_inc(r_oT, 1)

            def pre_root(n, which):
                act.wait_ge(r_dv, n * PRE + (5, 12)[which])
                nc.scalar.activation(sd3[:, :], ve3[:, :], ACT.Sqrt).then_inc(r_sd, 1)

            def pre_hi(n, first):
                if not first:
                    act.wait_ge(f_z, (n - 1) * ZT + 2 * HC * NC)
                for k in range(NC):
                    act.wait_ge(r_xtr, n * NC + k + 1)
                    nc.scalar.activation(x1T_hi[:, k * FC:(k + 1) * FC], p_pre[k][:, :], ACT.Copy).then_inc(r_hi, 1)

            def activations(n, l, k, first):
                fn, sc = ((ACT.Silu, s1_c), (ACT.Gelu, sh1_c), (ACT.Gelu, sh2_c))[l]
                if l == 0 and not first:
                    act.wait_ge(f_lo, n * ACTS + split_of(2, k, HC - 1) + 1 - ACTS)
                for idx, (tl, tk, w, o) in enumerate(TILES):
                    if (tl, tk) == (l, k) and not (l == 0 and w == 1):
                        act.wait_ge(f_z, n * ZT + idx + 1)
                        nc.scalar.activation(act_f[k][:, o, :], p_z[idx % NZ][:, :], fn,
                                             scale=sc[:, o:o + 1]).then_inc(f_act, 1)
                        if l > 0:
                            nc.scalar.activation(hid_hi[k][l % 2][:, o, :], p_z[idx % NZ][:, :], fn,
                                                 scale=sc[:, o:o + 1]).then_inc(f_ghi, 1)

            def outputs(n, first):
                if not first:
                    act.wait_ge(w_tr, n * NC)
                for k in range(NC):
                    idx = ZT - NC + k
                    act.wait_ge(f_z, n * ZT + idx + 1)
                    nc.scalar.activation(zT[:, k * FC:(k + 1) * FC], p_z[idx % NZ][:, :], ACT.Copy,
                                         scale=s3_c[:, 0:1]).then_inc(w_zT, 1)

            def post_root(n):
                act.wait_ge(w_dv, n * POST + 3)
                nc.scalar.activation(sd4[:, :], ve4[:, :], ACT.Sqrt).then_inc(w_sd, 1)

            act.wait_ge(a_small, 7 * 16)
            weight_bank(0)
            weight_bank(1)
            pre_oT(0, True)
            pre_root(0, 0)
            for i in range(2, 6):
                weight_bank(i)
            pre_root(0, 1)
            low_sum(2)
            for i in range(6, len(wbanks)):
                weight_bank(i)
            low_sum(3)
            pre_hi(0, True)

            def turn(n, first, last):
                activations(n, 0, 0, first)
                if not last:
                    pre_oT(n + 1, False)
                activations(n, 0, 1, first)
                if not last:
                    pre_root(n + 1, 0)
                if not first:
                    post_root(n - 1)
                activations(n, 1, 0, first)
                activations(n, 1, 1, first)
                if not last:
                    pre_root(n + 1, 1)
                activations(n, 2, 0, first)
                activations(n, 2, 1, first)
                if not last:
                    pre_hi(n + 1, False)
                outputs(n, first)

            turn(0, True, False)
            with act.Fori(1, B - 1) as n:
                turn(n, False, False)
            turn(B - 1, False, True)
            post_root(B - 1)

        @block.vector
        def _(dve):
            def weight_bank(i):
                w, k, rows = wbanks[i]
                dve.wait_ge(a_whi, i + 1)
                nc.vector.tensor_tensor(wlo[w][:, k, :], p_z[i % NZ][:, 0:rows * 128],
                                        whi[w][:, k, :].bitcast(F32), ALU.subtract).then_inc(a_wlo, 1)

            def statistics(st, mv, ve, src, chain, base, k):
                for t in range(NB):
                    last = nc.vector.bn_stats(st[:, t, :], src(t))
                last.then_inc(chain, 1)
                wait_alone(dve, chain, base + k, a_alone)
                for t in range(NB):
                    last = nc.vector.bn_aggr(mv[:, t, :], st[:, t, :])
                last.then_inc(chain, 1)
                dve.wait_ge(chain, base + k + 1)
                nc.vector.tensor_scalar(ve[:, :], mv[:, :, 1], EPS, None, ALU.add).then_inc(chain, 1)

            def pre_step(ins, n, k):
                ins.then_inc(r_dv, 1)
                dve.wait_ge(r_dv, n * PRE + k)

            def scale_shift(n, k):
                pre_step(nc.vector.reciprocal(rs3[:, :], sd3[:, :]), n, k)
                pre_step(nc.vector.scalar_tensor_tensor(out=nm3[:, :], in0=mv3[:, :, 0], scalar=-1.0, in1=rs3[:, :],
                                                        op0=ALU.mult, op1=ALU.mult), n, k + 1)

            def x1_rows(n):
                return x1_all[:, bass.ds(n * S, S)].rearrange("p (t e) -> p t e", e=E)

            def pre_y(n, first):
                if not first:
                    dve.wait_ge(r_xtr, n * NC)
                for k in range(NC):
                    dve.wait_ge(r_y, n * NC + k + 1)
                    nc.vector.tensor_tensor(y[:, k * NT:(k + 1) * NT, :], p_pre[k][:, :].rearrange("p (t e) -> p t e", e=E),
                                            bo_b[:, k * NT:(k + 1) * NT, :], ALU.add).then_inc(r_dv, 1)
                dve.wait_ge(r_dv, n * PRE + 2)
                statistics(st3, mv3, ve3, lambda t: y[:, t, :], r_dv, n * PRE, 3)

            def pre_x1(n):
                dve.wait_ge(r_sd, n * 2 + 1)
                scale_shift(n, 6)
                for t in range(NB):
                    last = nc.vector.tensor_scalar(y[:, t, :], y[:, t, :], rs3[:, t:t + 1], nm3[:, t:t + 1],
                                                   ALU.mult, ALU.add)
                pre_step(last, n, 8)
                dve.wait_ge(r_x, n * 16 + 16)
                pre_step(nc.vector.tensor_tensor(x1_rows(n), y[:, :, :], xres[:, :, :], ALU.add), n, 9)
                statistics(st3, mv3, ve3, lambda t: x1_all[:, bass.ds(n * S + t * E, E)], r_dv, n * PRE, 10)

            def pre_xh(n):
                dve.wait_ge(r_sd, n * 2 + 2)
                scale_shift(n, 13)
                for t in range(NB):
                    last = nc.vector.tensor_scalar(y[:, t, :], x1_all[:, bass.ds(n * S + t * E, E)], rs3[:, t:t + 1],
                                                   nm3[:, t:t + 1], ALU.mult, ALU.add)
                last.then_inc(r_dv, 1)

            def pre_lo(n):
                for k in range(NC):
                    c = slice(k * FC, (k + 1) * FC)
                    dve.wait_ge(r_hi, n * NC + k + 1)
                    nc.vector.tensor_tensor(x1T_lo[:, c], p_pre[k][:, :], x1T_hi[:, c].bitcast(F32),
                                            ALU.subtract).then_inc(r_lo, 1)

            def post_statistics(n):
                for k in range(NC):
                    dve.wait_ge(w_tr, n * NC + k + 1)
                statistics(st4, mv4, ve4, lambda t: p_post[t // NT][:, (t % NT) * 128:(t % NT + 1) * 128],
                           w_dv, n * POST, 1)

            def post_out(n, first):
                dve.wait_ge(w_sd, n + 1)
                nc.vector.reciprocal(rs4[:, :], sd4[:, :]).then_inc(w_dv, 1)
                dve.wait_ge(w_dv, n * POST + 4)
                if not first:
                    dve.wait_ge(w_out, n * 16)
                for t in range(NB):
                    last = nc.vector.tensor_scalar(res[:, t, :], p_post[t // NT][:, (t % NT) * 128:(t % NT + 1) * 128],
                                                   mv4[:, t, 0:1], rs4[:, t:t + 1], ALU.subtract, ALU.mult)
                last.then_inc(w_dv, 1)
                dve.wait_ge(w_dv, n * POST + 5)
                nc.vector.tensor_tensor(res[:, :, :], res[:, :, :], x1_rows(n), ALU.add).then_inc(w_dv, 1)

            def split(n, l, k, o):
                src, place = act_f[k][:, o, :], split_of(l, k, o)
                if l == 0:
                    nc.vector.tensor_copy(hid_hi[k][l % 2][:, o, :], src).then_inc(f_hi, 1)
                    dve.wait_ge(f_hi, n * (NC * HC) + place + 1)
                else:
                    dve.wait_ge(f_ghi, n * GHI + place - NC * HC + 1)
                nc.vector.tensor_tensor(hid_lo[k][l % 2][:, o, :], src, hid_hi[k][l % 2][:, o, :].bitcast(F32),
                                        ALU.subtract).then_inc(f_lo, 1)

            def gated(n, k):
                for o in range(HC):
                    idx = TILES.index((0, k, 1, o))
                    dve.wait_ge(f_z, n * ZT + idx + 1)
                    dve.wait_ge(f_act, n * ACTS + split_of(0, k, o) + 1)
                    nc.vector.scalar_tensor_tensor(out=act_f[k][:, o, :], in0=p_z[idx % NZ][:, :],
                                                   scalar=s2_c[:, o:o + 1], in1=act_f[k][:, o, :],
                                                   op0=ALU.mult, op1=ALU.mult).then_inc(f_mul, 1)
                    dve.wait_ge(f_mul, n * (NC * HC) + k * HC + o + 1)
                    split(n, 0, k, o)

            def splits(n, l, k):
                for o in range(HC):
                    dve.wait_ge(f_act, n * ACTS + split_of(l, k, o) + 1)
                    split(n, l, k, o)

            dve.wait_ge(a_small, 7 * 16)
            def low_parts(w):
                dve.wait_ge(a_wlo, max(i for i, (k, _, _) in enumerate(wbanks) if k == w) + 1)
                nc.vector.tensor_reduce(out=low_max[:, w:w + 1], in_=wlo[w][:, :, :].bitcast(F32), op=ALU.max,
                                        axis=AX.XY, apply_absolute_value=True).then_inc(a_low, 1)

            weight_bank(0)
            weight_bank(1)
            low_parts(0)
            low_parts(1)
            pre_y(0, True)
            pre_x1(0)
            for i in range(2, 6):
                weight_bank(i)
            pre_xh(0)
            for i in range(6, len(wbanks)):
                weight_bank(i)
            low_parts(4)
            pre_lo(0)
            dve.wait_ge(a_low, 3)
            dve.wait_ge(a_lowa, 2)
            nc.vector.tensor_scalar(low_max[:, :], low_max[:, :], 0.0, None, ALU.is_gt).then_inc(a_low, 1)
            dve.wait_ge(a_low, 4)
            nc.vector.tensor_reduce(out=low_any[:, :], in_=low_max[:, :], op=ALU.max, axis=AX.X).then_inc(a_low, 1)
            dve.wait_ge(a_sum, 1)
            nc.vector.tensor_reduce(out=low_flag[:, :], in_=p_post[0][0:1, 0:128], op=ALU.max, axis=AX.X).then_inc(a_low, 1)

            def turn(n, first, last):
                gated(n, 0)
                if not last:
                    pre_y(n + 1, False)
                gated(n, 1)
                if not first:
                    post_statistics(n - 1)
                splits(n, 1, 0)
                if not last:
                    pre_x1(n + 1)
                if not first:
                    post_out(n - 1, isinstance(n, int) and n == 1)
                splits(n, 1, 1)
                splits(n, 2, 0)
                if not last:
                    pre_xh(n + 1)
                splits(n, 2, 1)
                if not last:
                    pre_lo(n + 1)

            turn(0, True, False)
            turn(1, False, False)
            with dve.Fori(2, B - 1) as n:
                turn(n, False, False)
            turn(B - 1, False, True)
            post_statistics(B - 1)
            post_out(B - 1, False)


_INS = ['L0_attn_x', 'L0_attn_Wq', 'L0_attn_bq', 'L0_attn_Wk', 'L0_attn_bk', 'L0_attn_Wv', 'L0_attn_bv', 'L0_attn_Wo',
        'L0_attn_bo', 'L0_attn_rel_key', 'L0_ffn_w1_w', 'L0_ffn_w1_s', 'L0_ffn_w2_w', 'L0_ffn_w2_s', 'L0_ffn_h1_w',
        'L0_ffn_h1_s', 'L0_ffn_h2_w', 'L0_ffn_h2_s', 'L0_ffn_w3_w', 'L0_ffn_w3_s']


def kernel(**inputs):
    import numpy as _np
    import concourse.bacc as _bacc
    from concourse import mybir as _mybir
    from concourse.bass_utils import run_bass_kernel_spmd as _run

    nc = _bacc.Bacc("TRN2", target_bir_lowering=False, num_devices=1)
    arrays, args = {}, []
    for name in _INS:
        a = _np.ascontiguousarray(inputs[name])
        arrays[f"in_{name}_dram"] = a
        args.append(nc.dram_tensor(f"in_{name}_dram", a.shape, _mybir.dt.from_np(a.dtype), kind="ExternalInput").ap())
    args.append(nc.dram_tensor("out_dram", (B, S, E), _mybir.dt.float32, kind="ExternalOutput").ap())
    attention_ffn(nc, *args)
    r = _run(nc, [arrays], core_ids=[0])
    return r.results[0]["out_dram"]
```
